# Optimizing a Trainium2 kernel written in Bass

```python
import numpy as np
import jax
import jax.numpy as jnp

def _softmax(x, axis=-1):
    return jax.nn.softmax(x, axis=axis)

def _gelu(x):
    return jax.nn.gelu(x, approximate=True)

def _silu(x):
    return jax.nn.silu(x)

def _sigmoid(x):
    return jax.nn.sigmoid(x)

def _layernorm(x, axis=-1, eps=1e-05):
    m = jnp.mean(x, axis=axis, keepdims=True)
    v = jnp.var(x, axis=axis, keepdims=True)
    return (x - m) / jnp.sqrt(v + eps)

def _scatter_add(tgt, idx, src, axis=0):
    return tgt.at[idx].add(src)

def _segment_sum(src, seg, n):
    return jax.ops.segment_sum(src, seg, n)
kernel_name = 'mk_gnn_resnorm_d4_gnn_r32_70d51d'

def setup_inputs(seed: int=0):
    np.random.seed(seed)
    _w = jnp.asarray

    def _rec_inputs():
        import jax
        import jax.numpy as jnp
        _gk = jax.random.key(seed)
        x = -0.000202 + 1 * jax.random.normal(jax.random.fold_in(_gk, 1), (3125, 128), jnp.float32)
        src = jax.random.randint(jax.random.fold_in(_gk, 2), (50000,), 0, 3125, jnp.int32)
        dst = jnp.minimum((3125 * jax.random.uniform(jax.random.fold_in(_gk, 3), (50000,)) ** 2.0).astype(jnp.int32), 99999)
        _o = jnp.argsort(dst, stable=True)
        src = src[_o]
        dst = dst[_o]
        edge_attr_10 = 0.000254407 + 0.99978 * jax.random.normal(jax.random.fold_in(_gk, 11), (50000, 10), jnp.float32)
        edge_attr_2 = 0.0007022 + 0.999661 * jax.random.normal(jax.random.fold_in(_gk, 12), (50000, 2), jnp.float32)
        edge_type_4 = jax.random.randint(jax.random.fold_in(_gk, 14), (50000,), 0, 4, jnp.int32)
        edge_type_9 = jax.random.randint(jax.random.fold_in(_gk, 15), (50000,), 0, 9, jnp.int32)
        return (x, src, dst, edge_attr_10, edge_attr_2, edge_type_4, edge_type_9)
    x, src, dst, edge_attr_10, edge_attr_2, edge_type_4, edge_type_9 = _rec_inputs()

    def _L0_gnn_setup():
        import jax, jax.numpy as jnp
        import numpy as np
        N_NODES = 50000
        N_EDGES = 18750
        DIM = 128
        N_EDGE_TYPES = 4
        N_STEPS = 4

        def _gru_cell(x, h, w_ih, w_hh, b_ih, b_hh):
            gi = x @ w_ih.T + b_ih
            gh = h @ w_hh.T + b_hh
            i_r, i_z, i_n = jnp.split(gi, 3, axis=-1)
            h_r, h_z, h_n = jnp.split(gh, 3, axis=-1)
            r = jax.nn.sigmoid(i_r + h_r)
            z = jax.nn.sigmoid(i_z + h_z)
            n = jnp.tanh(i_n + r * h_n)
            return (1.0 - z) * n + z * h

        def _step(embedding, src, dst, etype, W_msg, b_msg, w_ih, w_hh, b_ih, b_hh):
            n = embedding.shape[0]
            m = (embedding @ W_msg.T + b_msg).reshape(n, N_EDGE_TYPES, DIM)
            q = m[src, etype]
            r = jax.ops.segment_sum(q, dst, num_segments=n)
            return _gru_cell(r, embedding, w_ih, w_hh, b_ih, b_hh)
        key = jax.random.key(seed)
        ks = jax.random.split(key, 9)
        bound = 1.0 / np.sqrt(DIM)
        return {'embedding': jax.random.normal(ks[0], (N_NODES, DIM), dtype=jnp.float32), 'edge_uv': jax.random.randint(ks[1], (2, N_EDGES), 0, N_NODES, dtype=jnp.int64), 'edge_type': jax.random.randint(ks[2], (N_EDGES,), 0, N_EDGE_TYPES, dtype=jnp.int64), 'W_msg': jax.random.uniform(ks[3], (DIM * N_EDGE_TYPES, DIM), jnp.float32, -bound, bound), 'b_msg': jax.random.uniform(ks[4], (DIM * N_EDGE_TYPES,), jnp.float32, -bound, bound), 'w_ih': jax.random.uniform(ks[5], (3 * DIM, DIM), jnp.float32, -bound, bound), 'w_hh': jax.random.uniform(ks[6], (3 * DIM, DIM), jnp.float32, -bound, bound), 'b_ih': jax.random.uniform(ks[7], (3 * DIM,), jnp.float32, -bound, bound), 'b_hh': jax.random.uniform(ks[8], (3 * DIM,), jnp.float32, -bound, bound)}
    _L0_gnn_all = _L0_gnn_setup()
    _L0_gnn_in = {k: v for k, v in _L0_gnn_all.items() if k in ('W_msg', 'b_msg', 'w_ih', 'w_hh', 'b_ih', 'b_hh')}
    del _L0_gnn_all

    def _L1_gnn_setup():
        import jax, jax.numpy as jnp
        import numpy as np
        N, E, D = (3125, 31250, 128)

        def _batchnorm(h, gamma, beta, eps=1e-05):
            mu = jnp.mean(h, axis=0)
            var = jnp.var(h, axis=0)
            return (h - mu) * jax.lax.rsqrt(var + eps) * gamma + beta
        key = jax.random.key(seed)
        ks = jax.random.split(key, 9)
        return {'x': jax.random.normal(ks[0], (N, D), jnp.float32), 'edge_index': jax.random.randint(ks[1], (2, E), 0, N, dtype=jnp.int64), 'edge_w': jax.random.normal(ks[2], (E, 2), jnp.float32), 'pos_w1': jax.random.normal(ks[3], (2, D), jnp.float32) * 0.5, 'pos_w2': jax.random.normal(ks[4], (D, D), jnp.float32) * (1.0 / np.sqrt(D)), 'sage_w': jax.random.normal(ks[5], (2 * D, D), jnp.float32) * (1.0 / np.sqrt(2 * D)), 'sage_b': jnp.zeros((D,), jnp.float32), 'bn_gamma': jnp.ones((D,), jnp.float32), 'bn_beta': jnp.zeros((D,), jnp.float32)}
    _L1_gnn_all = _L1_gnn_setup()
    _L1_gnn_in = {k: v for k, v in _L1_gnn_all.items() if k in ('pos_w1', 'pos_w2', 'sage_w', 'sage_b', 'bn_gamma', 'bn_beta')}
    del _L1_gnn_all

    def _L2_gnn_setup():
        import jax, jax.numpy as jnp
        import numpy as np
        NUM_EDGE_TYPES = 8
        HIDDEN = 128
        N_NODES = 50000
        N_EDGES = 18750

        def _gru_cell(x, h, W_ih, W_hh, b_ih, b_hh):
            H = h.shape[-1]
            gi = x @ W_ih.T + b_ih
            gh = h @ W_hh.T + b_hh
            i_r, i_z, i_n = (gi[:, :H], gi[:, H:2 * H], gi[:, 2 * H:])
            h_r, h_z, h_n = (gh[:, :H], gh[:, H:2 * H], gh[:, 2 * H:])
            r = jax.nn.sigmoid(i_r + h_r)
            z = jax.nn.sigmoid(i_z + h_z)
            n = jnp.tanh(i_n + r * h_n)
            return (1.0 - z) * n + z * h
        key = jax.random.key(seed)
        ks = jax.random.split(key, 10)
        H = HIDDEN
        h = jax.random.normal(ks[0], (N_NODES, H), dtype=jnp.float32)
        edge_index = jax.random.randint(ks[1], (2, N_EDGES), 0, N_NODES, dtype=jnp.int32)
        edge_type = jax.random.randint(ks[2], (N_EDGES,), 0, NUM_EDGE_TYPES + 1, dtype=jnp.int32)
        s = 1.0 / np.sqrt(H)
        W_msg = jax.random.uniform(ks[3], (H, H), jnp.float32, -s, s)
        b_msg = jax.random.uniform(ks[4], (H,), jnp.float32, -s, s)
        edge_embed = jax.random.normal(ks[5], (NUM_EDGE_TYPES + 1, H), dtype=jnp.float32)
        W_ih = jax.random.uniform(ks[6], (3 * H, H), jnp.float32, -s, s)
        W_hh = jax.random.uniform(ks[7], (3 * H, H), jnp.float32, -s, s)
        b_ih = jax.random.uniform(ks[8], (3 * H,), jnp.float32, -s, s)
        b_hh = jax.random.uniform(ks[9], (3 * H,), jnp.float32, -s, s)
        return {'h': h, 'edge_index': edge_index, 'edge_type': edge_type, 'num_nodes': N_NODES, 'W_msg': W_msg, 'b_msg': b_msg, 'edge_embed': edge_embed, 'W_ih': W_ih, 'W_hh': W_hh, 'b_ih': b_ih, 'b_hh': b_hh}
    _L2_gnn_all = _L2_gnn_setup()
    _L2_gnn_in = {k: v for k, v in _L2_gnn_all.items() if k in ('W_msg', 'b_msg', 'edge_embed', 'W_ih', 'W_hh', 'b_ih', 'b_hh')}
    del _L2_gnn_all

    def _L3_gnn_setup():
        import jax, jax.numpy as jnp
        import numpy as np
        N = 50000
        E = 25000
        D = 128
        H = 8
        C = D // H
        ED = 10
        FF = 4 * D

        def _layer(x, edge_index, edge_attr, Wq, bq, Wk, bk, Wv, bv, We, Wskip, bskip, Wbeta, gn_w, gn_b, gn_ms, W1, b1, W2, b2):
            n = x.shape[0]
            src, dst = (edge_index[0], edge_index[1])
            q = (x @ Wq + bq).reshape(n, H, C)
            k = (x @ Wk + bk).reshape(n, H, C)
            v = (x @ Wv + bv).reshape(n, H, C)
            e = (edge_attr @ We).reshape(-1, H, C)
            k_j = k[src] + e
            alpha = jnp.einsum('ehc,ehc->eh', q[dst], k_j) / jnp.sqrt(jnp.float32(C))
            amax = jax.ops.segment_max(alpha, dst, num_segments=n)
            ex = jnp.exp(alpha - amax[dst])
            denom = jax.ops.segment_sum(ex, dst, num_segments=n)
            alpha = ex / (denom[dst] + 1e-16)
            msg = (v[src] + e) * alpha[:, :, None]
            out = jax.ops.segment_sum(msg.reshape(-1, H * C), dst, num_segments=n)
            x_r = x @ Wskip + bskip
            beta = jax.nn.sigmoid(jnp.concatenate([out, x_r, out - x_r], axis=-1) @ Wbeta)
            x_att = beta * x_r + (1.0 - beta) * out
            h = x + x_att
            mean = h.mean(axis=0)
            hc = h - gn_ms * mean
            var = (hc * hc).mean(axis=0)
            h = hc / jnp.sqrt(var + 1e-05) * gn_w + gn_b
            ffn = jax.nn.gelu(h @ W1 + b1, approximate=False) @ W2 + b2
            return h + ffn
        key = jax.random.key(seed)
        ks = jax.random.split(key, 20)
        s = 0.05
        p = lambda k, shape: jax.random.normal(k, shape, jnp.float32) * s
        return {'x': jax.random.normal(ks[0], (N, D), jnp.float32), 'edge_index': jax.random.randint(ks[1], (2, E), 0, N), 'edge_attr': jax.random.normal(ks[2], (E, ED), jnp.float32), 'Wq': p(ks[3], (D, D)), 'bq': jnp.zeros((D,), jnp.float32), 'Wk': p(ks[4], (D, D)), 'bk': jnp.zeros((D,), jnp.float32), 'Wv': p(ks[5], (D, D)), 'bv': jnp.zeros((D,), jnp.float32), 'We': p(ks[6], (ED, D)), 'Wskip': p(ks[7], (D, D)), 'bskip': jnp.zeros((D,), jnp.float32), 'Wbeta': p(ks[8], (3 * D, 1)), 'gn_w': jnp.ones((D,), jnp.float32), 'gn_b': jnp.zeros((D,), jnp.float32), 'gn_ms': jnp.ones((D,), jnp.float32), 'W1': p(ks[9], (D, FF)), 'b1': jnp.zeros((FF,), jnp.float32), 'W2': p(ks[10], (FF, D)), 'b2': jnp.zeros((D,), jnp.float32)}
    _L3_gnn_all = _L3_gnn_setup()
    _L3_gnn_in = {k: v for k, v in _L3_gnn_all.items() if k in ('Wq', 'bq', 'Wk', 'bk', 'Wv', 'bv', 'We', 'Wskip', 'bskip', 'Wbeta', 'gn_w', 'gn_b', 'gn_ms', 'W1', 'b1', 'W2', 'b2')}
    del _L3_gnn_all
    return {'x': x, 'src': src, 'dst': dst, 'edge_attr_10': edge_attr_10, 'edge_attr_2': edge_attr_2, 'edge_type_4': edge_type_4, 'edge_type_9': edge_type_9, 'L0_gnn_W_msg': _L0_gnn_in['W_msg'], 'L0_gnn_b_msg': _L0_gnn_in['b_msg'], 'L0_gnn_w_ih': _L0_gnn_in['w_ih'], 'L0_gnn_w_hh': _L0_gnn_in['w_hh'], 'L0_gnn_b_ih': _L0_gnn_in['b_ih'], 'L0_gnn_b_hh': _L0_gnn_in['b_hh'], 'L1_gnn_pos_w1': _L1_gnn_in['pos_w1'], 'L1_gnn_pos_w2': _L1_gnn_in['pos_w2'], 'L1_gnn_sage_w': _L1_gnn_in['sage_w'], 'L1_gnn_sage_b': _L1_gnn_in['sage_b'], 'L1_gnn_bn_gamma': _L1_gnn_in['bn_gamma'], 'L1_gnn_bn_beta': _L1_gnn_in['bn_beta'], 'L2_gnn_W_msg': _L2_gnn_in['W_msg'], 'L2_gnn_b_msg': _L2_gnn_in['b_msg'], 'L2_gnn_edge_embed': _L2_gnn_in['edge_embed'], 'L2_gnn_W_ih': _L2_gnn_in['W_ih'], 'L2_gnn_W_hh': _L2_gnn_in['W_hh'], 'L2_gnn_b_ih': _L2_gnn_in['b_ih'], 'L2_gnn_b_hh': _L2_gnn_in['b_hh'], 'L3_gnn_Wq': _L3_gnn_in['Wq'], 'L3_gnn_bq': _L3_gnn_in['bq'], 'L3_gnn_Wk': _L3_gnn_in['Wk'], 'L3_gnn_bk': _L3_gnn_in['bk'], 'L3_gnn_Wv': _L3_gnn_in['Wv'], 'L3_gnn_bv': _L3_gnn_in['bv'], 'L3_gnn_We': _L3_gnn_in['We'], 'L3_gnn_Wskip': _L3_gnn_in['Wskip'], 'L3_gnn_bskip': _L3_gnn_in['bskip'], 'L3_gnn_Wbeta': _L3_gnn_in['Wbeta'], 'L3_gnn_gn_w': _L3_gnn_in['gn_w'], 'L3_gnn_gn_b': _L3_gnn_in['gn_b'], 'L3_gnn_gn_ms': _L3_gnn_in['gn_ms'], 'L3_gnn_W1': _L3_gnn_in['W1'], 'L3_gnn_b1': _L3_gnn_in['b1'], 'L3_gnn_W2': _L3_gnn_in['W2'], 'L3_gnn_b2': _L3_gnn_in['b2']}

def reference(x, src, dst, edge_attr_10, edge_attr_2, edge_type_4, edge_type_9, L0_gnn_W_msg, L0_gnn_b_msg, L0_gnn_w_ih, L0_gnn_w_hh, L0_gnn_b_ih, L0_gnn_b_hh, L1_gnn_pos_w1, L1_gnn_pos_w2, L1_gnn_sage_w, L1_gnn_sage_b, L1_gnn_bn_gamma, L1_gnn_bn_beta, L2_gnn_W_msg, L2_gnn_b_msg, L2_gnn_edge_embed, L2_gnn_W_ih, L2_gnn_W_hh, L2_gnn_b_ih, L2_gnn_b_hh, L3_gnn_Wq, L3_gnn_bq, L3_gnn_Wk, L3_gnn_bk, L3_gnn_Wv, L3_gnn_bv, L3_gnn_We, L3_gnn_Wskip, L3_gnn_bskip, L3_gnn_Wbeta, L3_gnn_gn_w, L3_gnn_gn_b, L3_gnn_gn_ms, L3_gnn_W1, L3_gnn_b1, L3_gnn_W2, L3_gnn_b2):
    import jax
    import jax.numpy as jnp

    def _L0_gnn_ref(embedding, edge_uv, edge_type, W_msg, b_msg, w_ih, w_hh, b_ih, b_hh):
        import jax, jax.numpy as jnp
        import numpy as np
        N_NODES = 50000
        N_EDGES = 18750
        DIM = 128
        N_EDGE_TYPES = 4
        N_STEPS = 4

        def _gru_cell(x, h, w_ih, w_hh, b_ih, b_hh):
            gi = x @ w_ih.T + b_ih
            gh = h @ w_hh.T + b_hh
            i_r, i_z, i_n = jnp.split(gi, 3, axis=-1)
            h_r, h_z, h_n = jnp.split(gh, 3, axis=-1)
            r = jax.nn.sigmoid(i_r + h_r)
            z = jax.nn.sigmoid(i_z + h_z)
            n = jnp.tanh(i_n + r * h_n)
            return (1.0 - z) * n + z * h

        def _step(embedding, src, dst, etype, W_msg, b_msg, w_ih, w_hh, b_ih, b_hh):
            n = embedding.shape[0]
            m = (embedding @ W_msg.T + b_msg).reshape(n, N_EDGE_TYPES, DIM)
            q = m[src, etype]
            r = jax.ops.segment_sum(q, dst, num_segments=n)
            return _gru_cell(r, embedding, w_ih, w_hh, b_ih, b_hh)
        src, dst = (edge_uv[0], edge_uv[1])
        for _ in range(N_STEPS):
            embedding = _step(embedding, src, dst, edge_type, W_msg, b_msg, w_ih, w_hh, b_ih, b_hh)
        return embedding

    def _L1_gnn_ref(x, edge_index, edge_w, pos_w1, pos_w2, sage_w, sage_b, bn_gamma, bn_beta):
        import jax, jax.numpy as jnp
        import numpy as np
        N, E, D = (3125, 31250, 128)

        def _batchnorm(h, gamma, beta, eps=1e-05):
            mu = jnp.mean(h, axis=0)
            var = jnp.var(h, axis=0)
            return (h - mu) * jax.lax.rsqrt(var + eps) * gamma + beta
        n_nodes = x.shape[0]
        src, dst = (edge_index[0], edge_index[1])
        pe = jax.nn.relu(edge_w @ pos_w1) @ pos_w2
        x_j = x[src]
        msg = pe * x_j + x_j
        s = jax.ops.segment_sum(msg, dst, num_segments=n_nodes)
        cnt = jax.ops.segment_sum(jnp.ones((msg.shape[0],), msg.dtype), dst, num_segments=n_nodes)
        agg = s / jnp.maximum(cnt, 1.0)[:, None]
        out = jnp.concatenate([x, agg], axis=-1) @ sage_w + sage_b
        out = jax.nn.relu(_batchnorm(out, bn_gamma, bn_beta))
        return out + x

    def _L2_gnn_ref(h, edge_index, edge_type, num_nodes, W_msg, b_msg, edge_embed, W_ih, W_hh, b_ih, b_hh):
        import jax, jax.numpy as jnp
        import numpy as np
        NUM_EDGE_TYPES = 8
        HIDDEN = 128
        N_NODES = 50000
        N_EDGES = 18750

        def _gru_cell(x, h, W_ih, W_hh, b_ih, b_hh):
            H = h.shape[-1]
            gi = x @ W_ih.T + b_ih
            gh = h @ W_hh.T + b_hh
            i_r, i_z, i_n = (gi[:, :H], gi[:, H:2 * H], gi[:, 2 * H:])
            h_r, h_z, h_n = (gh[:, :H], gh[:, H:2 * H], gh[:, 2 * H:])
            r = jax.nn.sigmoid(i_r + h_r)
            z = jax.nn.sigmoid(i_z + h_z)
            n = jnp.tanh(i_n + r * h_n)
            return (1.0 - z) * n + z * h
        src = edge_index[0]
        dst = edge_index[1]
        src_h = h[src] @ W_msg.T + b_msg
        emb = edge_embed[jnp.clip(edge_type, 0, NUM_EDGE_TYPES)]
        msg = src_h + emb
        messages = jax.ops.segment_sum(msg, dst, num_segments=num_nodes)
        h_new = _gru_cell(messages, h[:num_nodes], W_ih, W_hh, b_ih, b_hh)
        result = jnp.zeros_like(h).at[:num_nodes].set(h_new)
        return result

    def _L3_gnn_ref(x, edge_index, edge_attr, Wq, bq, Wk, bk, Wv, bv, We, Wskip, bskip, Wbeta, gn_w, gn_b, gn_ms, W1, b1, W2, b2):
        import jax, jax.numpy as jnp
        import numpy as np
        N = 50000
        E = 25000
        D = 128
        H = 8
        C = D // H
        ED = 10
        FF = 4 * D

        def _layer(x, edge_index, edge_attr, Wq, bq, Wk, bk, Wv, bv, We, Wskip, bskip, Wbeta, gn_w, gn_b, gn_ms, W1, b1, W2, b2):
            n = x.shape[0]
            src, dst = (edge_index[0], edge_index[1])
            q = (x @ Wq + bq).reshape(n, H, C)
            k = (x @ Wk + bk).reshape(n, H, C)
            v = (x @ Wv + bv).reshape(n, H, C)
            e = (edge_attr @ We).reshape(-1, H, C)
            k_j = k[src] + e
            alpha = jnp.einsum('ehc,ehc->eh', q[dst], k_j) / jnp.sqrt(jnp.float32(C))
            amax = jax.ops.segment_max(alpha, dst, num_segments=n)
            ex = jnp.exp(alpha - amax[dst])
            denom = jax.ops.segment_sum(ex, dst, num_segments=n)
            alpha = ex / (denom[dst] + 1e-16)
            msg = (v[src] + e) * alpha[:, :, None]
            out = jax.ops.segment_sum(msg.reshape(-1, H * C), dst, num_segments=n)
            x_r = x @ Wskip + bskip
            beta = jax.nn.sigmoid(jnp.concatenate([out, x_r, out - x_r], axis=-1) @ Wbeta)
            x_att = beta * x_r + (1.0 - beta) * out
            h = x + x_att
            mean = h.mean(axis=0)
            hc = h - gn_ms * mean
            var = (hc * hc).mean(axis=0)
            h = hc / jnp.sqrt(var + 1e-05) * gn_w + gn_b
            ffn = jax.nn.gelu(h @ W1 + b1, approximate=False) @ W2 + b2
            return h + ffn
        return _layer(x, edge_index, edge_attr, Wq, bq, Wk, bk, Wv, bv, We, Wskip, bskip, Wbeta, gn_w, gn_b, gn_ms, W1, b1, W2, b2)
    edge_index = jnp.stack([src, dst])
    x = _layernorm(x + _L0_gnn_ref(x, edge_index, edge_type_4, L0_gnn_W_msg, L0_gnn_b_msg, L0_gnn_w_ih, L0_gnn_w_hh, L0_gnn_b_ih, L0_gnn_b_hh), axis=-1)
    x = _layernorm(x + _L1_gnn_ref(x, edge_index, edge_attr_2, L1_gnn_pos_w1, L1_gnn_pos_w2, L1_gnn_sage_w, L1_gnn_sage_b, L1_gnn_bn_gamma, L1_gnn_bn_beta), axis=-1)
    x = _layernorm(x + _L2_gnn_ref(x, edge_index, edge_type_9, 3125, L2_gnn_W_msg, L2_gnn_b_msg, L2_gnn_edge_embed, L2_gnn_W_ih, L2_gnn_W_hh, L2_gnn_b_ih, L2_gnn_b_hh), axis=-1)
    x = _layernorm(x + _L3_gnn_ref(x, edge_index, edge_attr_10, L3_gnn_Wq, L3_gnn_bq, L3_gnn_Wk, L3_gnn_bk, L3_gnn_Wv, L3_gnn_bv, L3_gnn_We, L3_gnn_Wskip, L3_gnn_bskip, L3_gnn_Wbeta, L3_gnn_gn_w, L3_gnn_gn_b, L3_gnn_gn_ms, L3_gnn_W1, L3_gnn_b1, L3_gnn_W2, L3_gnn_b2), axis=-1)
    return x

_drawn_inputs = setup_inputs


def setup_inputs(seed=0):
    import zlib

    import numpy as np

    out = dict(_drawn_inputs(seed))
    spreads = {'L1_gnn_sage_b': (0.0, 0.8),
     'L1_gnn_bn_gamma': (1.0, 0.2),
     'L1_gnn_bn_beta': (0.0, 0.1),
     'L3_gnn_bq': (0.0, 0.8),
     'L3_gnn_bk': (0.0, 0.8),
     'L3_gnn_bv': (0.0, 0.8),
     'L3_gnn_bskip': (0.0, 0.8),
     'L3_gnn_gn_w': (1.0, 0.2),
     'L3_gnn_gn_b': (0.0, 0.1),
     'L3_gnn_gn_ms': (1.0, 0.2),
     'L3_gnn_b1': (0.0, 0.1),
     'L3_gnn_b2': (0.0, 0.1)}
    factors = {'edge_attr_10': 3.894,
     'L2_gnn_b_ih': 6.494,
     'L2_gnn_b_hh': 8.0,
     'L3_gnn_Wq': 3.795,
     'L3_gnn_Wk': 3.909,
     'L3_gnn_We': 3.913}
    for name, (base, spread) in spreads.items():
        noise = np.random.default_rng([zlib.crc32(name.encode()), seed]).standard_normal(out[name].shape)
        drawn = base * np.exp(spread * noise) if base else spread * noise
        out[name] = jnp.asarray(drawn.astype(out[name].dtype))
    for name, factor in factors.items():
        out[name] = (out[name] * factor).astype(out[name].dtype)
    return out
```

```python
from contextlib import ExitStack

import numpy as np
import concourse.bass as bass
from concourse import mybir

F32 = mybir.dt.float32
BF16 = mybir.dt.bfloat16
I32 = mybir.dt.int32
ALU = mybir.AluOpType
ACT = mybir.ActivationFunctionType
AX = mybir.AxisListType
ds = bass.ds

P = 128
N = 3125
E = 50000
D = 128
ET = 4
HEADS, HC = 8, 16
FF = 512
WIN = (N + P - 1) // P
NP = WIN * P
TILES = (E + P - 1) // P
EXTRA = WIN - 1
WV = 8
WAVES = -(-(TILES + EXTRA) // WV)
SLOTS = WAVES * WV
RING = 4
TURNS = WAVES // RING
AHEAD = RING - 1
STAGED = WAVES + AHEAD
FIELDS = 16
F_ATTR2, F_DST, F_SRC, F_T4, F_T9 = 10, 12, 13, 14, 15
CH = [(c * 512, min(512, NP - c * 512)) for c in range(-(-NP // 512))]
NCH = len(CH)
EV_D = (NCH + 1) // 2
EV_A = NCH // 2
FAR = 1.0e6
BIG = 1.0e38
STEPS = 4
SORT_G = 23
SORT_N = TILES // SORT_G
SORT_TILES = TILES + TILES % 2
assert SORT_N * SORT_G == TILES
EPS = 1e-5
OUTS = [0, 1, 2, 2, 3]
MT_SLOTS = [len(range(b, WIN, RING)) for b in range(RING)]
assert WAVES % RING == 0



def LN_DMA(ln, b):
    return 16 * OUTS[ln] * len(range(b, NCH, 2))


def load_cols(pe, row, i, u, hi=NP - P):
    return pe.bass.values_load_multi_w_load_instructions(
        row[0:1, ds((i * RING + u) * WV, WV)], engines=[mybir.EngineType.PE], min_val=0, max_val=hi,
        skip_runtime_bounds_check_because="window starts are multiples of 128 under 3200 by construction")[1]


def load_tiles(dve, tix, i):
    return dve.bass.values_load_multi_w_load_instructions(
        tix[0:1, ds(i * WV, WV)], engines=[mybir.EngineType.DVE], min_val=0, max_val=TILES - 1,
        skip_runtime_bounds_check_because="a number of edges before the last, over 128")[1]


PASS_L1, PASS_L2, PASS_L3 = STEPS, STEPS + 1, STEPS + 2


class Any1(dict):
    def __missing__(self, k):
        return 1


def build(nc, a, out, seen, known):
    ctx = ExitStack()
    with ctx:
        def sb(name, shape, dt=F32):
            return ctx.enter_context(nc.sbuf_tensor(name, shape, dt))

        def sem(name):
            return ctx.enter_context(nc.semaphore(name))

        def dram(name, shape):
            return nc.dram_tensor(name, shape, F32, kind="Internal").ap()

        m_tab = dram("m_tab", (NP * ET, D))
        x_tab = [dram(f"x_tab{i}", (NP, D)) for i in (1, 2)]
        kv_tab = dram("kv_tab", (NP, 2 * D))
        sorted_dr = dram("sorted_dr", (TILES * P, FIELDS))
        ve_dr = dram("ve_dr", (WAVES * P, WV * D))

        rec = sb("rec", [P, SLOTS, FIELDS])
        rec_flat = rec[:, :, :].rearrange("p s f -> p (s f)")
        recT = sb("recT", [P, (WAVES + 1) * P])
        idx4 = sb("idx4", [P, STAGED * WV], I32)
        idx1 = sb("idx1", [P, STAGED * WV], I32)
        dl = sb("dl", [P, SLOTS + WV])
        dlb = sb("dlb", [P, SLOTS], BF16)
        t9b = sb("t9b", [P, SLOTS], BF16)
        cols = sb("cols", [1, SLOTS], I32)
        cols7 = sb("cols7", [1, SLOTS], I32)
        tix = sb("tix", [1, 2 * EXTRA], I32)
        basef = sb("basef", [1, 2, SLOTS])
        grp = sb("grp", [P, SLOTS])
        ring = sb("ring", [P, RING, WV, 2 * D])
        ring_flat = ring[:, :, :, :].rearrange("p r w d -> p (r w d)")
        raw_i = ring_flat[:, 12 * TILES:16 * TILES].bitcast(I32).rearrange("p (k t) -> p k t", k=4)
        next_i = ring_flat[:, 16 * TILES:17 * TILES].bitcast(I32)
        wk = ring_flat[:, 0:6 * 1024].rearrange("p (k b c) -> p k b c", k=6, b=2)
        key = ring_flat[:, 0:SORT_TILES]
        rank, part, tile_no, one_s = (ring_flat[:, 512 + 512 * j:512 + 512 * j + SORT_TILES] for j in range(4))
        rank_i = ring_flat[:, 2560:2560 + TILES].bitcast(I32)
        turn_in = ring_flat[:, 3072:3072 + 2 * P].rearrange("p (v e) -> p v e", e=P)
        tri, tie = ring_flat[:, 3328:3328 + P], ring_flat[:, 3328 + P:3328 + P + 2]
        sc_rec = ring_flat[:, 3584:3584 + SORT_G * FIELDS].rearrange("p (g f) -> p g f", f=FIELDS)
        sc_idx = ring_flat[:, 4096:4096 + SORT_G].bitcast(I32)
        flag = sb("flag", [1, 1], I32)
        ixr = sb("ixr", [P, RING, WV], I32)
        oh = sb("oh", [P, 2, WV, P])
        rts = sb("rts", [P, 2, P])
        nodes = sb("nodes", [P, 4, NP])
        xT, hT, gT, yT = (nodes[:, i, :] for i in range(4))
        pw = sb("pw", [P, 4, 512])
        C9 = rec_flat[:, 0:NP]
        alE = rec_flat[:, 0:SLOTS * HEADS].rearrange("p (s h) -> p s h", h=HEADS)
        oht = rec_flat[:, 3328:3328 + 2048].rearrange("p (b c) -> p b c", b=2)
        fF, fB = (rec_flat[:, 5376 + 512 * j:5888 + 512 * j] for j in range(2))
        exg = recT[:, 0:4 * 448].rearrange("p (b s c) -> p b s c", b=4, s=WV)
        gmask = recT[:, 1792:1792 + SLOTS * NCH].rearrange("p (s g) -> p s g", g=NCH)
        den, rden = (recT[0:HEADS * NCH, 4736 + 512 * j:5248 + 512 * j] for j in range(2))
        wt = sb("wt", [P, 36, P])
        wpad = sb("wpad", [P, 2, WV, P])
        brow = sb("brow", [P, 512 + 3 * P])
        bc = sb("bc", [P, 48])
        cst = sb("cst", [P, 4 * P])
        ident, iota, ones, onesD = (cst[:, i * P:(i + 1) * P] for i in range(4))
        iotab = sb("iotab", [P, P], BF16)
        sel = sb("sel", [8 * NCH, NCH, P])
        small = sb("small", [P, 640])
        sd, rs = small[:, 576:576 + WIN], small[:, 608:608 + WIN]
        gate = sb("gate", [1, 2])
        zrow = sb("zrow", [1, 512], BF16)
        ps = ctx.enter_context(nc.psum_tensor("ps", [P, 8, 512], F32))
        psf = ps[:, :, :].rearrange("p b c -> p (b c)")

        s_edge = sem("s_edge")
        srt_d = sem("srt_d")
        srt_in = sem("srt_in")
        srt_row = sem("srt_row")
        srt_cmp = sem("srt_cmp")
        srt_red = sem("srt_red")
        srt_acc = sem("srt_acc")
        srt_st = sem("srt_st")
        srt_gate = sem("srt_gate")
        srt_sc = sem("srt_sc")
        srt_ld = sem("srt_ld")
        s_w = sem("s_w")
        s_dv = sem("s_dv")
        s_pe = sem("s_pe")
        s_ac = sem("s_ac")
        s_gate = sem("s_gate")
        ix_ready = sem("ix_ready")
        oh_ready = sem("oh_ready")
        credit = sem("credit")
        gat = [sem(f"gat{i}") for i in range(RING)]
        cnt_oh = sem("cnt_oh")
        cnt_mm = sem("cnt_mm")
        mt_mm = sem("mt_mm")
        mt_ev = sem("mt_ev")
        mt_dma = [sem(f"mt_dma{i}") for i in range(RING)]
        ev_d = sem("ev_d")
        ev_a = sem("ev_a")
        gru_mm = sem("gru_mm")
        gru_r = sem("gru_r")
        gru_z = sem("gru_z")
        gru_t = sem("gru_t")
        gru_p = sem("gru_p")
        gru_n = sem("gru_n")
        gru_d = sem("gru_d")
        gru_e = sem("gru_e")
        gru_h = sem("gru_h")
        l1_hid = sem("l1_hid")
        l1_relu = sem("l1_relu")
        l1_pe = sem("l1_pe")
        l1_msg = sem("l1_msg")
        a_tp = sem("a_tp")
        a_e = sem("a_e")
        a_q = sem("a_q")
        a_oht = sem("a_oht")
        a_kv = sem("a_kv")
        a_v = sem("a_v")
        a_prod = sem("a_prod")
        a_red = sem("a_red")
        a_out = sem("a_out")
        a_st = [sem(f"a_st{i}") for i in range(2)]
        b_ld = [sem(f"b_ld{i}") for i in range(RING)]
        b_ready = sem("b_ready")
        b_used = sem("b_used")
        ln_y = sem("ln_y")
        ln_m = sem("ln_m")
        ln_c = sem("ln_c")
        ln_q = sem("ln_q")
        ln_v = sem("ln_v")
        ln_s = sem("ln_s")
        ln_r = sem("ln_r")
        ln_x = sem("ln_x")
        ln_b = sem("ln_b")
        ln_t = sem("ln_t")
        ln_o = sem("ln_o")
        ln_dma = [sem(f"ln_dma{i}") for i in range(2)]
        x_step = sem("x_step")
        f_mm = sem("f_mm")
        f_act = sem("f_act")
        f_dve = sem("f_dve")

        W = {}
        loads = []

        def weight(name, src, k=1):
            i = sum(v[1] for v in W.values())
            W[name] = (i, k)
            loads.append((wt[:src.shape[0], i:i + k, :].rearrange("p k d -> p (k d)"), src))

        for n, k in (("L0_WmsgT", 4), ("L0_wihT", 3), ("L0_whhT", 3), ("L1_pos_w2", 1), ("L1_sage", 2),
                     ("L2_WmsgT", 1), ("L2_wihT", 3), ("L2_whhT", 3), ("L2_emb", 1), ("L2_bmsg9", 1),
                     ("L3_qkv", 3), ("L3_Wskip", 1), ("L3_W1", 4), ("L3_W2", 4)):
            weight(n, a[n], k)

        def w(name, j=0, k=1, rows=P):
            i = W[name][0] + j
            return wt[:rows, i:i + k, :].rearrange("p k d -> p (k d)")

        NBC = a["bcols"].shape[1]
        bcol = {n: i for i, n in enumerate(BCOLS)}

        def b_(name):
            return bc[:, bcol[name]:bcol[name] + 1]

        loads += [(bc[:, 0:NBC], a["bcols"]), (cst[:, :], a["consts"]),
                  (brow[:, :], a["brows"].rearrange("(a n) -> a n", a=1).to_broadcast([P, brow.shape[1]])),
                  (wpad[:, :, :, :].rearrange("p a s d -> p (a s d)"), a["wpad"]),
                  (sel[:, :, :].rearrange("p g d -> p (g d)"), a["sel"]),
                  (xT, a["xT"]), (hT, a["xT"])]
        NLOADS = 16 * len(loads)
        wbeta = sb("wbeta", [P, 3, P])

        t9oh, ohb = (pw[:, 2 * j:2 * j + 2, :].rearrange("p a b -> p (a b)").bitcast(BF16)
                     .rearrange("p (b s c) -> p b s c", b=2, c=P) for j in range(2))
        tail = nodes[:, 1:4, :].rearrange("p a b -> p (a b)")
        L8 = ([tail[0:HEADS, j * 512:(j + 1) * 512] for j in range(6)]
              + [tail[0:HEADS, NP + 4096 + j * 512:NP + 4608 + j * 512] for j in range(4)]
              + [pw[0:HEADS, j, :] for j in range(2)])
        fd, ld, hd, tl, conn, full, A, B, Dd, De, cf, cb = L8

        block = ctx.enter_context(nc.Block())

        def wave_no(k, i, u):
            return k * WAVES + i * RING + u

        def oh_no(k, i, u):
            return wave_no(k, i, u) + (2 if k > PASS_L1 else 1)

        DV, PE, AC = ({n: i + 1 for i, n in enumerate(known[e])} if known else Any1() for e in ("DV", "PE", "AC"))

        @block.sync
        def _(sp):
            for i, n in enumerate(("dst_t", "src_t", "t4_t", "t9_t")):
                sp.dma_start(raw_i[:, i, :], a[n]).then_inc(s_edge, 16)
            sp.dma_start(ring_flat[:, 0:TILES * 10], a["attr10_t"]).then_inc(s_edge, 16)
            sp.dma_start(ring_flat[:, TILES * 10:TILES * 12], a["attr2_t"]).then_inc(s_edge, 16)
            sp.dma_start(next_i, a["dstn_t"]).then_inc(s_edge, 16)
            for dst, src in loads:
                sp.dma_start(dst, src).then_inc(s_w, 16)

            def table(t, rows, width):
                for n in range(WIN):
                    b = n % RING
                    sp.wait_ge(mt_ev, t * WIN + (n + 1))
                    sp.dma_start(rows[n], wk[:, b // 2, b % 2, 512 - width:512]).then_inc(mt_dma[b], 16)

            m_rows = m_tab.rearrange("(n p t) d -> n p (t d)", p=P, t=ET)
            kv_rows = kv_tab.rearrange("(n p) d -> n p d", p=P)
            table(0, m_rows, 512)
            with sp.Fori(0, STEPS - 1) as s:
                table(s + 1, m_rows, 512)

            def rows_out(ln):
                for c, (c0, cw) in enumerate(CH):
                    sp.wait_ge(ln_o, NCH * OUTS[ln] + c + 1)
                    buf = wk[:, 3, c % 2, 0:cw].rearrange("p (w d) -> p w d", d=D)
                    if ln < 3:
                        dst = x_tab[ln].rearrange("(w p) d -> p w d", p=P)[:, c0 // P:(c0 + cw) // P, :]
                    elif c0 + cw <= N:
                        dst = out.rearrange("(a w) d -> a w d", a=1)[0, c0:c0 + cw, :].rearrange("(w p) d -> p w d", p=P)
                    else:
                        dst = out[c0:N, :].rearrange("(w p) d -> p w d", w=1)
                        buf = buf[0:N - c0, :, :]
                    sp.dma_start(dst, buf).then_inc(ln_dma[c % 2], 16)

            for ln in (0, 1):
                rows_out(ln)
            table(STEPS, kv_rows, 2 * D)
            with sp.Fori(0, TURNS) as i:
                for u in range(RING):
                    sp.wait_ge(a_v, (i * RING + (u + 1)) * 2 + 1)
                    sp.dma_start(ve_dr[ds((i * RING + u) * P, P), :],
                                 pw[:, 2 * (u % 2):2 * (u % 2) + 2, :].rearrange("p a b -> p (a b)")
                                 ).then_inc(a_st[u % 2], 16)
            for b in range(2):
                sp.wait_ge(a_st[b], 16 * (WAVES // 2 + 1))
            sp.wait_ge(s_dv, DV["ex_done"])
            with sp.Fori(0, TURNS) as i:
                for u in range(RING):
                    sp.wait_ge(b_used, i * RING + (u + 1))
                    sp.dma_start(ring[:, u, 0:WV // 2, :].rearrange("p a b -> p (a b)"),
                                 ve_dr[ds((i * RING + u) * P, P), :]).then_inc(b_ld[u], 16)
            rows_out(3)
            for c in range(2):
                sp.wait_ge(ln_dma[c], LN_DMA(4, c))

        @block.gpsimd
        def _(pool):
            pool.wait_ge(s_w, NLOADS)
            pool.wait_ge(s_dv, DV["flag"])
            unsorted = pool.value_load(flag[0:1, 0:1], min_val=0, max_val=1)
            with pool.If(unsorted > 0):
                with pool.Fori(0, SORT_N) as c:
                    pool.wait_ge(srt_st, c * 2 + 2)
                    nc.gpsimd.tensor_tensor(gate[:, 0:1], cst[0:1, 0:1], cst[0:1, 0:1], ALU.add).then_inc(srt_gate, 1)
                    for g in range(SORT_G):
                        pool.indirect_dma_start(
                            sorted_dr, bass.IndirectOffsetOnAxis(ap=sc_idx[:, g:g + 1], axis=0),
                            sc_rec[:, g, :], None).then_inc(srt_sc, 16)
                    pool.wait_ge(srt_sc, (c + 1) * (16 * SORT_G))
                    pool.wait_ge(srt_gate, c * 2 + 1)
                    nc.gpsimd.tensor_tensor(gate[:, 1:2], cst[0:1, 0:1], cst[0:1, 0:1], ALU.add).then_inc(srt_gate, 1)
                pool.wait_ge(srt_gate, 2 * SORT_N)
                back = sorted_dr.rearrange("(t p) f -> p t f", p=P)
                for c in range(SORT_N):
                    cs = slice(c * SORT_G, (c + 1) * SORT_G)
                    pool.dma_start(rec[:, cs, :], back[:, cs, :]).then_inc(srt_ld, 16)

            def passage(gates, *waits):
                for s_, v_ in waits:
                    pool.wait_ge(s_, v_)
                pool.wait_ge(s_gate, gates + 1)
                nc.gpsimd.tensor_tensor(gate[:, 0:1], cst[0:1, 0:1], cst[0:1, 0:1], ALU.add).then_inc(s_gate, 1)

            def gathers(k, table, width):
                with pool.Fori(0, TURNS) as i:
                    for u in range(RING):
                        passage(k * (WAVES + 1) + i * RING + (u + 1),
                                (ix_ready, k * STAGED + i * RING + (u + 1)))
                        for j in range(WV):
                            pool.indirect_dma_start(
                                ring[:, u, j, 0:width], None, table,
                                bass.IndirectOffsetOnAxis(ap=ixr[:, u, j:j + 1], axis=0)).then_inc(gat[u], 16)

            with pool.Fori(0, STEPS) as s:
                passage(s * (WAVES + 1), *[(mt_dma[b], (s + 1) * (16 * MT_SLOTS[b])) for b in range(RING)])
                gathers(s, m_tab, D)
            for k, ln in ((PASS_L1, 0), (PASS_L2, 1)):
                passage(k * (WAVES + 1), *[(ln_dma[c], LN_DMA(ln + 1, c)) for c in range(2)])
                gathers(k, x_tab[ln], D)
            passage(PASS_L3 * (WAVES + 1),
                    *[(mt_dma[b], (STEPS + 1) * 16 * MT_SLOTS[b]) for b in range(RING)])
            gathers(PASS_L3, kv_tab, 2 * D)

        @block.scalar
        def _(act):
            n_ac = [0]

            def step(name, ins):
                n_ac[0] += 1
                seen["AC"].append(name)
                ins.then_inc(s_ac, 1)

            act.wait_ge(s_w, NLOADS)
            for q in range(WAVES // 4):
                act.wait_ge(s_pe, PE[f"recT{q}"])
                step(f"recT{q}", nc.scalar.activation(recT[:, q * 512:(q + 1) * 512], ps[:, q % 4, :], ACT.Copy))
            act.wait_ge(cnt_mm, WAVES + 2)
            for c in range(1, NCH, 2):
                c0, cw = CH[c]
                step(f"c9_{c}", nc.scalar.activation(C9[:, c0:c0 + cw], ps[:, c, 0:cw], ACT.Copy))

            def evac(k):
                act.wait_ge(credit, (k + 1) * WAVES + RING)
                for c in range(1, NCH, 2):
                    c0, cw = CH[c]
                    nc.scalar.activation(gT[:, c0:c0 + cw], ps[:, c, 0:cw], ACT.Copy).then_inc(ev_a, 1)

            def gru(r, L):
                for c in range(NCH + 1):
                    if c < NCH:
                        cw, b, t = CH[c][1], c % 2, r * NCH + (c + 1)
                        act.wait_ge(gru_mm, t)
                        if c >= 2:
                            act.wait_ge(gru_h, r * NCH + (c - 1))
                        nc.scalar.activation(wk[:, 0, b, 0:cw], ps[:, 4 * b, 0:cw], ACT.Sigmoid,
                                             bias=b_(L + "_br")).then_inc(gru_r, 1)
                        nc.scalar.activation(wk[:, 1, b, 0:cw], ps[:, 4 * b + 1, 0:cw], ACT.Sigmoid,
                                             bias=b_(L + "_bz")).then_inc(gru_z, 1)
                    if c >= 1:
                        cw, b = CH[c - 1][1], (c - 1) % 2
                        act.wait_ge(gru_p, r * NCH + c)
                        nc.scalar.activation(wk[:, 3, b, 0:cw], wk[:, 2, b, 0:cw], ACT.Tanh,
                                             bias=b_(L + "_bin")).then_inc(gru_n, 1)

            def norm(ln):
                n0 = NCH * ln
                for c in range(NCH + 3):
                    if c < NCH:
                        cw, b = CH[c][1], c % 2
                        act.wait_ge(ln_c, n0 + c + 1)
                        if c >= 2:
                            act.wait_ge(ln_v, n0 + c - 1)
                        nc.scalar.activation(wk[:, 1, b, 0:cw], wk[:, 0, b, 0:cw], ACT.Square).then_inc(ln_q, 1)
                    if 1 <= c <= NCH:
                        w0, nw = CH[c - 1][0] // P, CH[c - 1][1] // P
                        act.wait_ge(ln_v, n0 + c)
                        nc.scalar.activation(sd[:, w0:w0 + nw], ps[:, 2 + (c - 1) % 2, 0:nw], ACT.Sqrt,
                                             bias=b_("eps")).then_inc(ln_s, 1)
                    if c >= 3 and ln != 2:
                        cw, b = CH[c - 3][1], (c - 3) % 2
                        act.wait_ge(ln_t, NCH * OUTS[ln] + c - 2)
                        if c >= 5:
                            act.wait_ge(ln_dma[b], LN_DMA(ln, b) + 16 * ((c - 3) // 2))
                        nc.scalar.activation(wk[:, 3, b, 0:cw], ps[:, 4 + b, 0:cw], ACT.Copy).then_inc(ln_o, 1)

            with act.Fori(0, STEPS) as s:
                evac(s)
                gru(s, "L0")
            norm(0)

            with act.Fori(0, TURNS) as i:
                for u in range(RING):
                    for hf in range(2):
                        q = (i * RING + u) * 2 + hf
                        act.wait_ge(l1_hid, q + 1)
                        nc.scalar.activation(pw[:, hf, :], ps[:, 7, :], ACT.Relu).then_inc(l1_relu, 1)
            evac(PASS_L1)
            for c, (c0, cw) in enumerate(CH):
                act.wait_ge(s_pe, PE[f"sage{c}"])
                step(f"sage{c}", nc.scalar.activation(yT[:, c0:c0 + cw], ps[:, 4 + c % 2, 0:cw], ACT.Identity,
                                                      bias=b_("L1_sage_b")))
            act.wait_ge(s_dv, DV["bn_agg"])
            step("bn_sqrt", nc.scalar.activation(small[:, 2:3], small[:, 1:2], ACT.Sqrt, bias=b_("eps")))

            def bn_relu(c):
                c0, cw = CH[c]
                if c == 0:
                    act.wait_ge(s_dv, DV["bn_shift"])
                nc.scalar.activation(yT[:, c0:c0 + cw], yT[:, c0:c0 + cw], ACT.Relu, bias=small[:, 5:6],
                                     scale=small[:, 4:5]).then_inc(x_step, 1)

            for c in range(NCH):
                bn_relu(c)
            norm(1)

            evac(PASS_L2)
            for c, (c0, cw) in enumerate(CH):
                act.wait_ge(s_pe, PE[f"msg{c}"])
                step(f"msg{c}", nc.scalar.activation(yT[:, c0:c0 + cw], ps[:, c % 2, 0:cw], ACT.Copy))
            gru(STEPS, "L2")
            norm(2)

            with act.Fori(0, TURNS) as i:
                for u in range(RING):
                    for hf in range(2):
                        g2 = (i * RING + u) * 2 + hf
                        act.wait_ge(a_tp, g2 + 1)
                        nc.scalar.activation(oht[:, u % 2, hf * 512:(hf + 1) * 512], ps[:, 4 + hf, :],
                                             ACT.Copy).then_inc(a_oht, 1)
            alT = ring_flat[:, 0:4096]
            for h in range(HEADS):
                act.wait_ge(s_dv, DV[f"sub{h}"])
                step(f"exp{h}", nc.scalar.activation(alT[:, h * 512:(h + 1) * 512], alT[:, h * 512:(h + 1) * 512],
                                                     ACT.Exp))
            act.wait_ge(b_used, WAVES + RING)
            for c in range(1, NCH, 2):
                c0, cw = CH[c]
                step(f"o{c}", nc.scalar.activation(gT[:, c0:c0 + cw], ps[:, c, 0:cw], ACT.Copy))
            for c, (c0, cw) in enumerate(CH):
                b = c % 2
                act.wait_ge(f_mm, 2 * c + 1)
                if c >= 2:
                    act.wait_ge(f_dve, 3 * (c - 2) + 3)
                nc.scalar.activation(wk[:, 0, b, 0:cw], ps[:, b, 0:cw], ACT.Identity,
                                     bias=b_("L3_bskip")).then_inc(f_act, 1)
                act.wait_ge(f_mm, 2 * c + 2)
                nc.scalar.activation(wk[:, 3, b, 0:cw], ps[:, 4 + b, 0:cw], ACT.Sigmoid).then_inc(f_act, 1)
            act.wait_ge(s_dv, DV["gn_var"])
            step("gn_sqrt", nc.scalar.activation(small[:, 2:3], small[:, 1:2], ACT.Sqrt, bias=b_("eps")))
            act.wait_ge(s_dv, DV["gn_shift"])
            for c, (c0, cw) in enumerate(CH):
                step(f"gn{c}", nc.scalar.activation(hT[:, c0:c0 + cw], hT[:, c0:c0 + cw], ACT.Identity,
                                                    bias=small[:, 5:6], scale=small[:, 4:5]))
            for c, (c0, cw) in enumerate(CH):
                for j in range(4):
                    act.wait_ge(s_pe, PE[f"ff{c}_{j}"])
                    if c >= 1 and j == 0:
                        act.wait_ge(s_pe, PE[f"ffo{c - 1}"])
                    step(f"gelu{c}_{j}", nc.scalar.activation(wk[:, j // 2, j % 2, 0:cw], ps[:, j, 0:cw], ACT.Gelu,
                                                              bias=b_(f"L3_b1_{j}")))
            norm(3)

        @block.vector
        def _(dve):
            V = nc.vector
            n_dv = [0]

            def step(name, ins):
                n_dv[0] += 1
                seen["DV"].append(name)
                ins.then_inc(s_dv, 1)

            def after(name):
                dve.wait_ge(s_dv, DV[name])

            start = ((credit, RING), (cnt_mm, 2), (b_used, RING), (s_gate, 1), (l1_msg, 1), (a_v, 1), (a_q, 1),
                     (a_prod, 1), (a_out, 1), (a_st[0], 16), (a_st[1], 16))
            for j, (s_, v_) in enumerate(start):
                V.memset(idx4[:, j * 40:(j + 1) * 40], 0).then_inc(s_, v_)
            step("z_idx1", V.memset(idx1[:, :], 0))
            step("z_dl", V.memset(dl[:, :], -1.0))
            step("z_row", V.memset(zrow[:, :], 0.0))
            step("z_cols", V.memset(cols[:, :], 0))
            step("z_recT", V.memset(recT[:, WAVES * P:(WAVES + 1) * P], 0.0))
            step("z_base", V.memset(basef[:, :, :], FAR))
            dve.wait_ge(s_edge, 112)
            R = rec[:, 0:TILES, :]
            step("r_a10", V.tensor_copy(R[:, :, 0:10], ring_flat[:, 0:TILES * 10].rearrange("p (t f) -> p t f", f=10)))
            step("r_a2", V.tensor_copy(R[:, :, F_ATTR2:F_DST],
                                       ring_flat[:, TILES * 10:TILES * 12].rearrange("p (t f) -> p t f", f=2)))
            for n, (i, f) in enumerate(((0, F_DST), (1, F_SRC), (2, F_T4))):
                step(f"r_i{n}", V.tensor_copy(R[:, :, f], raw_i[:, i, :]))
            step("r_t9", V.tensor_scalar(R[:, :, F_T9], raw_i[:, 3, :], 0, 8, ALU.max, ALU.min))
            after("r_t9")
            far = nodes[:, 2, 0:TILES]
            step("f_gt", V.tensor_tensor(far, raw_i[:, 0, :], next_i, ALU.is_gt))
            after("f_gt")
            step("f_sum", V.tensor_reduce(small[:, 639:640], far, AX.X, ALU.add))
            dve.wait_ge(s_pe, PE["flag"])
            step("flag", V.tensor_scalar(flag[:, :], ps[0:1, 7, 0:1], 1.0, None, ALU.min))
            after("flag")
            dve.wait_ge(s_w, NLOADS)
            unsorted = dve.value_load(flag[0:1, 0:1], min_val=0, max_val=1)
            with dve.If(unsorted > 0):
                n_srt = [0]

                def then(ins):
                    n_srt[0] += 1
                    ins.then_inc(srt_d, 1)
                    dve.wait_ge(srt_d, n_srt[0])

                then(V.memset(one_s, 1.0))
                then(V.memset(rank, 0.0))
                then(V.tensor_tensor_scan(tile_no, one_s, rank, 0.0, ALU.add, ALU.add))
                then(V.memset(key, 4.0e6))
                then(V.scalar_tensor_tensor(key[:, 0:TILES], R[:, :, F_DST], 512.0, tile_no[:, 0:TILES],
                                            ALU.mult, ALU.add))
                then(V.tensor_tensor(tri, ident, iota, ALU.mult))
                then(V.tensor_reduce(tie[:, 0:1], tri, AX.X, ALU.add))
                then(V.tensor_tensor(tri, iota, tie[:, 0:1].to_broadcast([P, P]), ALU.is_lt))
                cmp_ = nodes[:, 2:4, :].rearrange("p a b -> p (a b)")[:, 0:SORT_G * 2 * P].rearrange(
                    "p (t e) -> p t e", t=SORT_G)
                c2 = nodes[:, 2, 0:2 * P].rearrange("p (v e) -> p v e", e=P)
                rows = ps[:, 6, 0:2 * P]
                NG = SORT_N + 1
                with dve.Fori(0, SORT_TILES // 2) as c:
                    V.tensor_scalar(turn_in, key[:, ds(c * 2, 2)].unsqueeze(2).to_broadcast([P, 2, P]), 0.0, None,
                                    ALU.add).then_inc(srt_in, 1)
                    dve.wait_ge(srt_row, c + 1)
                    for g in range(SORT_N):
                        gs = slice(g * SORT_G, (g + 1) * SORT_G)
                        V.tensor_tensor(cmp_, rows.unsqueeze(1).to_broadcast([P, SORT_G, 2 * P]),
                                        key[:, gs].unsqueeze(2).to_broadcast([P, SORT_G, 2 * P]),
                                        ALU.is_lt).then_inc(srt_cmp, 1)
                        dve.wait_ge(srt_cmp, c * (NG + 1) + (g + 1))
                        V.tensor_reduce(part[:, gs], cmp_, AX.X, ALU.add).then_inc(srt_red, 1)
                        dve.wait_ge(srt_red, c * NG + (g + 1))
                    V.tensor_tensor(rank[:, 0:TILES], rank[:, 0:TILES], part[:, 0:TILES], ALU.add).then_inc(srt_acc, 1)
                    V.tensor_tensor(c2, rows.rearrange("p (v e) -> p v e", e=P),
                                    key[:, ds(c * 2, 2)].unsqueeze(2).to_broadcast([P, 2, P]),
                                    ALU.is_equal).then_inc(srt_cmp, 1)
                    dve.wait_ge(srt_cmp, c * (NG + 1) + NG)
                    V.tensor_tensor(c2, c2, tri.unsqueeze(1).to_broadcast([P, 2, P]), ALU.mult).then_inc(srt_cmp, 1)
                    dve.wait_ge(srt_cmp, c * (NG + 1) + (NG + 1))
                    V.tensor_reduce(tie, c2, AX.X, ALU.add).then_inc(srt_red, 1)
                    dve.wait_ge(srt_red, c * NG + NG)
                    dve.wait_ge(srt_acc, c * 2 + 1)
                    V.tensor_tensor(rank[:, ds(c * 2, 2)], rank[:, ds(c * 2, 2)], tie, ALU.add).then_inc(srt_acc, 1)
                    dve.wait_ge(srt_acc, c * 2 + 2)
                then(V.tensor_copy(rank_i, rank[:, 0:TILES]))
                with dve.Fori(0, SORT_N) as c:
                    V.tensor_scalar(sc_rec, rec[:, ds(c * SORT_G, SORT_G), :], 0.0, None, ALU.add).then_inc(srt_st, 1)
                    V.tensor_scalar(sc_idx, rank_i[:, ds(c * SORT_G, SORT_G)], 0.0, None, ALU.add).then_inc(srt_st, 1)
                    dve.wait_ge(srt_sc, (c + 1) * (16 * SORT_G))
                dve.wait_ge(srt_ld, 16 * SORT_N)
            step("w_dst", V.tensor_copy(raw_i[0:1, 0, :], rec[0:1, 0:TILES, F_DST]))
            after("w_dst")
            step("w_col", V.tensor_scalar(cols[0:1, 0:TILES], raw_i[0:1, 0, :], 7, 7, ALU.arith_shift_right,
                                          ALU.logical_shift_left))
            HALF = EXTRA // 2
            cmp = nodes[:, 2:4, :].rearrange("p a b -> p (a b)")[:, 0:HALF * TILES].rearrange("p (i t) -> p i t", t=TILES)
            for k in range(2):
                th = small[:, 32 + k * HALF:32 + (k + 1) * HALF]
                step(f"w_th{k}", V.tensor_scalar(th, iota[:, 1 + k * HALF:1 + (k + 1) * HALF], float(P), None, ALU.mult))
                after(f"w_th{k}")
                step(f"w_cmp{k}", V.tensor_tensor(cmp, R[:, :, F_DST].unsqueeze(1).to_broadcast([P, HALF, TILES]),
                                                  th.unsqueeze(2).to_broadcast([P, HALF, TILES]), ALU.is_lt))
                after(f"w_cmp{k}")
                step(f"w_cnt{k}", V.tensor_reduce(small[:, k * HALF:(k + 1) * HALF], cmp, AX.X, ALU.add))
            dve.wait_ge(s_pe, PE["off"])
            offs = small[0:1, 64:64 + EXTRA]
            step("w_off", V.tensor_copy(offs, ps[0:1, 7, 0:EXTRA]))
            after("w_off")
            step("w_offi", V.tensor_copy(tix[0:1, EXTRA:2 * EXTRA], offs))
            after("w_offi")
            step("w_tix", V.tensor_scalar(tix[0:1, 0:EXTRA], tix[0:1, EXTRA:2 * EXTRA], 7, None, ALU.arith_shift_right))
            step("w_rem", V.tensor_scalar(raw_i[0:1, 1, 0:EXTRA], tix[0:1, EXTRA:2 * EXTRA], P - 1, None, ALU.bitwise_and))
            after("w_rem")
            step("w_inv", V.tensor_scalar(offs, raw_i[0:1, 1, 0:EXTRA], 0.0, FAR, ALU.is_equal, ALU.mult))
            step("w_colx", V.tensor_copy(cols[0:1, TILES:TILES + EXTRA], small[0:1, 32:32 + EXTRA]))
            after("w_colx")
            step("w_b0", V.tensor_copy(basef[0:1, 0, 0:TILES], cols[0:1, 0:TILES]))
            step("w_bx", V.tensor_tensor(basef[0:1, 0, TILES:TILES + EXTRA], offs, small[0:1, 32:32 + EXTRA], ALU.add))
            step("w_c7", V.tensor_scalar(cols7[:, :], cols[:, :], 511, None, ALU.bitwise_and))
            step("w_grp", V.tensor_scalar(raw_i[0:1, 1, :], cols[0:1, 0:TILES], 9, None, ALU.arith_shift_right))
            step("w_grx", V.tensor_scalar(raw_i[0:1, 2, 0:SLOTS - TILES], cols[0:1, TILES:SLOTS], 9, None,
                                          ALU.arith_shift_right))
            after("w_grx")
            step("w_gf", V.tensor_copy(basef[0:1, 1, 0:TILES], raw_i[0:1, 1, :]))
            step("w_gx", V.tensor_copy(basef[0:1, 1, TILES:SLOTS], raw_i[0:1, 2, 0:SLOTS - TILES]))
            after("w_gx")
            with dve.Fori(0, EXTRA // WV) as i:
                t = load_tiles(dve, tix, i)
                for j in range(WV):
                    V.tensor_scalar(rec[:, ds(i * WV + (TILES + j), 1), :], rec[:, ds(t[j], 1), :], 0.0, None, ALU.add)
            step("x_last", V.tensor_copy(rec[:, TILES + EXTRA:SLOTS, :], rec[:, 0:SLOTS - TILES - EXTRA, :]))
            after("x_last")
            step("i_4", V.scalar_tensor_tensor(idx4[:, 0:SLOTS], rec[:, :, F_SRC], float(ET), rec[:, :, F_T4],
                                               ALU.mult, ALU.add))
            step("i_1", V.tensor_copy(idx1[:, 0:SLOTS], rec[:, :, F_SRC]))
            step("i_t9", V.tensor_copy(t9b[:, :], rec[:, :, F_T9]))
            dve.wait_ge(s_pe, PE["base"])
            step("i_dl", V.tensor_tensor(dl[:, 0:SLOTS], rec[:, :, F_DST], ps[:, 5, 0:SLOTS], ALU.subtract))
            step("i_gm", V.tensor_copy(grp[:, :], ps[:, 6, 0:SLOTS]))
            after("i_gm")
            step("i_dlb", V.tensor_copy(dlb[:, :], dl[:, 0:SLOTS]))
            step("i_iob", V.tensor_copy(iotab[:, :], iota))
            for L, j in (("L0", 0), ("L2", 2)):
                for g, n in enumerate(("r", "z")):
                    step(f"{L}_b{n}", V.tensor_tensor(b_(f"{L}_b{n}"), b_(f"{L}_bih_{n}"), b_(f"{L}_bhh_{n}"), ALU.add))

            def stage(k, i, u, idx):
                g3 = wave_no(k, i, u) + AHEAD
                dve.wait_ge(credit, g3 + 1)
                V.tensor_scalar(ixr[:, (u + AHEAD) % RING, :], idx[:, ds((i * RING + (u + AHEAD)) * WV, WV)], 0.0, None,
                                ALU.add).then_inc(ix_ready, 1)

            def stage_first(k, idx):
                for u in range(AHEAD):
                    dve.wait_ge(credit, k * WAVES + u + 1)
                    V.tensor_scalar(ixr[:, u, :], idx[:, u * WV:(u + 1) * WV], 0.0, None, ALU.add).then_inc(ix_ready, 1)

            def one_hot(k, i, u, ahead=0):
                v = (u + ahead) % 2
                V.tensor_tensor(oh[:, v, :, :], iota.unsqueeze(1).to_broadcast([P, WV, P]),
                                dl[:, ds((i * RING + (u + ahead)) * WV, WV)].unsqueeze(2).to_broadcast([P, WV, P]),
                                ALU.is_equal).then_inc(oh_ready, 1)

            def sums(k, idx):
                with dve.Fori(0, TURNS) as i:
                    for u in range(RING):
                        dve.wait_ge(credit, wave_no(k, i, u) + 3)
                        one_hot(k, i, u)
                        stage(k, i, u, idx)

            def evac(k):
                dve.wait_ge(credit, (k + 1) * WAVES + RING)
                for c in range(0, NCH, 2):
                    c0, cw = CH[c]
                    V.tensor_copy(gT[:, c0:c0 + cw], ps[:, c, 0:cw]).then_inc(ev_d, 1)

            def table(t, width, bias, q_rows=None):
                for n in range(WIN):
                    b = n % RING
                    dve.wait_ge(mt_mm, t * WIN + (n + 1))
                    if n >= RING:
                        dve.wait_ge(mt_dma[b], t * (16 * MT_SLOTS[b]) + 16 * (n // RING))
                    if q_rows is not None:
                        V.tensor_tensor(q_rows[:, n, :], ps[:, b, 0:D], bias[:, 0:D], ALU.add)
                        bs = bias[:, D:D + width]
                        src = ps[:, b, D:D + width]
                    else:
                        bs, src = bias, ps[:, b, 0:width]
                    V.tensor_tensor(wk[:, b // 2, b % 2, 512 - width:512], src, bs, ALU.add).then_inc(mt_ev, 1)

            def gru(r, L, h_in, h_out):
                for c in range(NCH + 1):
                    if c < NCH:
                        cw, b, t = CH[c][1], c % 2, r * NCH + (c + 1)
                        dve.wait_ge(gru_r, t)
                        V.scalar_tensor_tensor(wk[:, 2, b, 0:cw], ps[:, 4 * b + 3, 0:cw], b_(L + "_bhn"),
                                               wk[:, 0, b, 0:cw], ALU.add, ALU.mult).then_inc(gru_t, 1)
                        dve.wait_ge(gru_t, t)
                        V.tensor_tensor(wk[:, 2, b, 0:cw], wk[:, 2, b, 0:cw], ps[:, 4 * b + 2, 0:cw],
                                        ALU.add).then_inc(gru_p, 1)
                    if c >= 1:
                        c0, cw = CH[c - 1]
                        b, t = (c - 1) % 2, r * NCH + c
                        hi, ho, n = h_in[:, c0:c0 + cw], h_out[:, c0:c0 + cw], wk[:, 3, b, 0:cw]
                        dve.wait_ge(gru_n, t)
                        V.tensor_tensor(wk[:, 4, b, 0:cw], hi, n, ALU.subtract).then_inc(gru_d, 1)
                        dve.wait_ge(gru_d, t)
                        V.tensor_tensor(wk[:, 4, b, 0:cw], wk[:, 4, b, 0:cw], wk[:, 1, b, 0:cw],
                                        ALU.mult).then_inc(gru_e, 1)
                        dve.wait_ge(gru_e, t)
                        V.tensor_tensor(ho, n, wk[:, 4, b, 0:cw], ALU.add).then_inc(gru_h, 1)

            def norm(ln, make_y):
                n0 = NCH * ln
                for c in range(NCH + 2):
                    if c < NCH:
                        make_y(c)
                    if c >= 2:
                        (c0, cw), b = CH[c - 2], c % 2
                        dve.wait_ge(ln_b, n0 + c - 1)
                        V.tensor_tensor(xT[:, c0:c0 + cw], wk[:, 0, b, 0:cw], ps[:, 6 + b, 0:cw],
                                        ALU.mult).then_inc(ln_x, 1)
                    if c < NCH:
                        (c0, cw), b = CH[c], c % 2
                        dve.wait_ge(ln_m, n0 + c + 1)
                        if c >= 2:
                            dve.wait_ge(ln_q, n0 + c - 1)
                            dve.wait_ge(ln_x, n0 + c - 1)
                        V.tensor_tensor(wk[:, 0, b, 0:cw], yT[:, c0:c0 + cw], ps[:, b, 0:cw],
                                        ALU.subtract).then_inc(ln_c, 1)
                    if 1 <= c <= NCH:
                        w0, nw = CH[c - 1][0] // P, CH[c - 1][1] // P
                        dve.wait_ge(ln_s, n0 + c)
                        V.reciprocal(rs[:, w0:w0 + nw], sd[:, w0:w0 + nw]).then_inc(ln_r, 1)

            dT = pw[:, 0, :]
            LAST = TILES % P
            step("t_zd", V.memset(dT, -1.0))
            after("t_zd")
            dve.wait_ge(s_pe, PE["dT"])
            step("t_d0", V.tensor_copy(dT[:, 0:384], ps[:, 4, 0:384]))
            step("t_d1", V.tensor_copy(dT[0:LAST, 384:512], ps[0:LAST, 4, 384:512]))
            after("t_d1")
            dv, ff, fb = (x.rearrange("p (b e) -> p b e", e=P) for x in (dT, fF, fB))
            dve.wait_ge(s_pe, PE[f"recT{WAVES // 4 - 1}"])
            step("t_f0", V.memset(rec_flat[:, 5376:6400], -BIG))
            after("t_f0")
            step("t_f1", V.tensor_tensor(ff[:, :, 1:P], dv[:, :, 1:P], dv[:, :, 0:P - 1], ALU.not_equal))
            step("t_f2", V.tensor_tensor(fb[:, :, 0:P - 1], dv[:, :, 1:P], dv[:, :, 0:P - 1], ALU.not_equal))
            after("t_f2")
            step("t_f3", V.tensor_scalar(ff[:, :, 1:P], ff[:, :, 1:P], -BIG, None, ALU.mult))
            step("t_f4", V.tensor_scalar(fb[:, :, 0:P - 1], fb[:, :, 0:P - 1], -BIG, None, ALU.mult))
            edge = small[:, 384:384 + 64].rearrange("p (w b h) -> p w b h", w=2, b=4)
            step("t_e0", V.tensor_copy(edge[:, 0, :, :], dv[:, :, 0:1].to_broadcast([P, 4, HEADS])))
            step("t_e1", V.tensor_copy(edge[:, 1, :, :], dv[:, :, P - 1:P].to_broadcast([P, 4, HEADS])))
            dve.wait_ge(s_ac, AC[f"recT{WAVES // 4 - 1}"])
            table(0, 512, brow[:, 0:512])
            stage_first(0, idx4)
            step("z_t9", V.memset(pw[:, 0:2, :], 0.0))
            after("z_t9")
            with dve.Fori(0, WAVES // 2) as i:
                for u in range(2):
                    dve.wait_ge(cnt_mm, i * 2 + (u + 1))
                    sl = ds((i * 2 + u) * WV, WV)
                    V.tensor_tensor(t9oh[:, u, :, 0:16], iotab[:, 0:16].unsqueeze(1).to_broadcast([P, WV, 16]),
                                    t9b[:, sl].unsqueeze(2).to_broadcast([P, WV, 16]), ALU.is_equal)
                    V.tensor_tensor(ohb[:, u, :, :], iotab[:, :].unsqueeze(1).to_broadcast([P, WV, P]),
                                    dlb[:, sl].unsqueeze(2).to_broadcast([P, WV, P]), ALU.is_equal).then_inc(cnt_oh, 1)
            dve.wait_ge(cnt_mm, WAVES + 2)
            for c in range(0, NCH, 2):
                c0, cw = CH[c]
                step(f"c9_{c}", V.tensor_copy(C9[:, c0:c0 + cw], ps[:, c, 0:cw]))
            after(f"c9_{NCH - 1}")
            with dve.Fori(0, STEPS - 1) as s:
                sums(s, idx4)
                evac(s)
                gru(s, "L0", hT, hT)
                table(s + 1, 512, brow[:, 0:512])
                stage_first(s + 1, idx4)
            sums(STEPS - 1, idx4)
            evac(STEPS - 1)
            gru(STEPS - 1, "L0", hT, hT)

            def y_sum(c):
                c0, cw = CH[c]
                V.tensor_tensor(yT[:, c0:c0 + cw], xT[:, c0:c0 + cw], hT[:, c0:c0 + cw], ALU.add).then_inc(ln_y, 1)

            dve.wait_ge(gru_h, STEPS * NCH)
            norm(0, y_sum)

            stage_first(PASS_L1, idx1)
            V.tensor_scalar(rts[:, 0, :], recT[:, 0:P], 0.0, None, ALU.add)
            V.tensor_tensor(oh[:, 0, :, :], iota.unsqueeze(1).to_broadcast([P, WV, P]),
                            dl[:, 0:WV].unsqueeze(2).to_broadcast([P, WV, P]), ALU.is_equal).then_inc(oh_ready, 1)
            with dve.Fori(0, TURNS) as i:
                for u in range(RING):
                    for hf in range(2):
                        if hf:
                            dve.wait_ge(credit, wave_no(PASS_L1, i, u) + RING)
                            V.tensor_scalar(rts[:, (u + 1) % 2, :], recT[:, ds((i * RING + (u + 1)) * P, P)], 0.0,
                                            None, ALU.add)
                            one_hot(PASS_L1, i, u, ahead=1)
                            stage(PASS_L1, i, u, idx1)
                        dve.wait_ge(gat[u], (PASS_L1 * TURNS + i + 1) * (16 * WV))
                        dve.wait_ge(l1_pe, (i * RING + u) * 2 + (hf + 1))
                        xj = ring[:, u, 4 * hf:4 * hf + 4, 0:D]
                        V.scalar_tensor_tensor(xj, ps[:, 7, :].rearrange("p (s d) -> p s d", d=D), 1.0, xj,
                                               ALU.add, ALU.mult).then_inc(l1_msg, 1)
            evac(PASS_L1)
            for c, (c0, cw) in enumerate(CH):
                dve.wait_ge(s_pe, PE[f"cnt{c}"])
                step(f"mx{c}", V.tensor_scalar(wk[:, 0, c % 2, 0:cw], ps[:, c % 2, 0:cw], 1.0, None, ALU.max))
                after(f"mx{c}")
                step(f"rc{c}", V.reciprocal(wk[:, 1, c % 2, 0:cw], wk[:, 0, c % 2, 0:cw]))
                after(f"rc{c}")
                if c == 1:
                    dve.wait_ge(ev_a, (PASS_L1 + 1) * EV_A)
                step(f"ag{c}", V.tensor_tensor(gT[:, c0:c0 + cw], gT[:, c0:c0 + cw], wk[:, 1, c % 2, 0:cw], ALU.mult))

            def stats(T, ready, name):
                for c, (c0, cw) in enumerate(CH):
                    ready(c)
                    step(f"{name}s{c}", V.bn_stats(small[:, 128 + 6 * c:134 + 6 * c], T[:, c0:min(c0 + cw, N)]))
                after(f"{name}s{NCH - 1}")
                step(f"{name}_agg", V.bn_aggr(small[:, 0:2], small[:, 128:128 + 6 * NCH]))
                after(f"{name}_agg")

            stats(yT, lambda c: dve.wait_ge(s_ac, AC[f"sage{c}"]), "bn")
            dve.wait_ge(s_ac, AC["bn_sqrt"])
            step("bn_rs", V.reciprocal(small[:, 3:4], small[:, 2:3]))
            after("bn_rs")
            step("bn_scale", V.tensor_tensor(small[:, 4:5], small[:, 3:4], b_("L1_gamma"), ALU.mult))
            after("bn_scale")
            step("bn_ms", V.tensor_tensor(small[:, 7:8], small[:, 4:5], small[:, 0:1], ALU.mult))
            after("bn_ms")
            step("bn_shift", V.tensor_tensor(small[:, 5:6], b_("L1_beta"), small[:, 7:8], ALU.subtract))

            def y_l1(c):
                c0, cw = CH[c]
                dve.wait_ge(x_step, c + 1)
                V.scalar_tensor_tensor(yT[:, c0:c0 + cw], xT[:, c0:c0 + cw], 2.0, yT[:, c0:c0 + cw],
                                       ALU.mult, ALU.add).then_inc(ln_y, 1)

            norm(1, y_l1)

            stage_first(PASS_L2, idx1)
            dve.wait_ge(oh_ready, (PASS_L1 + 1) * WAVES + 1)
            sums(PASS_L2, idx1)
            evac(PASS_L2)
            gru(STEPS, "L2", xT, hT)
            dve.wait_ge(gru_h, (STEPS + 1) * NCH)
            norm(2, y_sum)

            q_rows = hT.rearrange("p (n d) -> p n d", d=D)
            dve.wait_ge(ln_x, 3 * NCH)
            table(STEPS, 2 * D, brow[:, 512:512 + 3 * D], q_rows)
            for j in range(3):
                step(f"wb{j}", V.tensor_copy(wbeta[:, j, :], bc[:, bcol["L3_wbeta0"] + j:bcol["L3_wbeta0"] + j + 1]
                                             .to_broadcast([P, P])))
            stage_first(PASS_L3, idx1)
            V.tensor_scalar(rts[:, 0, :], recT[:, 0:P], 0.0, None, ALU.add)
            V.tensor_tensor(oh[:, 0, :, :], iota.unsqueeze(1).to_broadcast([P, WV, P]),
                            dl[:, 0:WV].unsqueeze(2).to_broadcast([P, WV, P]), ALU.is_equal).then_inc(oh_ready, 1)
            ve = pw[:, :, :].rearrange("p (b c) d -> p b (c d)", b=2)
            red = small[:, 256:256 + 128].rearrange("p (b s) -> p b s", b=2)
            with dve.Fori(0, TURNS) as i:
                for u in range(RING):
                    g2 = (i * RING + u) * 2
                    v = u % 2
                    dve.wait_ge(a_q, g2 + 1)
                    w1 = (u + 1) % 2
                    V.tensor_scalar(rts[:, w1, :], recT[:, ds((i * RING + (u + 1)) * P, P)], 0.0, None, ALU.add)
                    one_hot(PASS_L3, i, u, ahead=1)
                    stage(PASS_L3, i, u, idx1)
                    dve.wait_ge(gat[u], (PASS_L3 * TURNS + i + 1) * (16 * WV))
                    dve.wait_ge(a_st[v], (i * 2 + (u // 2 + 1)) * 16)
                    for hf in range(2):
                        hs = slice(512 * hf, 512 * hf + 512)
                        dve.wait_ge(a_e, g2 + (hf + 1))
                        pe_ = ps[:, hf, :].rearrange("p (s d) -> p s d", d=D)
                        kj = ring[:, u, 4 * hf:4 * hf + 4, 0:D]
                        V.tensor_tensor(kj, kj, pe_, ALU.add).then_inc(a_kv, 1)
                        V.tensor_tensor(ve[:, v, hs].rearrange("p (s d) -> p s d", d=D),
                                        ring[:, u, 4 * hf:4 * hf + 4, D:2 * D], pe_, ALU.add).then_inc(a_v, 1)
                    for hf in range(2):
                        dve.wait_ge(a_kv, g2 + (hf + 1))
                        dve.wait_ge(a_q, g2 + (hf + 2))
                        kj = ring[:, u, 4 * hf:4 * hf + 4, 0:D]
                        V.tensor_tensor(kj, kj, ps[:, 2 + hf, :].rearrange("p (s d) -> p s d", d=D),
                                        ALU.mult).then_inc(a_prod, 1)
                    dve.wait_ge(a_prod, g2 + 3)
                    V.tensor_reduce(red[:, v, :].rearrange("p (s h) -> p s h", h=HEADS),
                                    ring[:, u, :, 0:D].rearrange("p s (h c) -> p s h c", c=HC), AX.X,
                                    ALU.add).then_inc(a_red, 1)
                    dve.wait_ge(a_red, i * RING + (u + 1))
                    dve.wait_ge(a_v, g2 + 3)
                    V.tensor_scalar(alE[:, ds((i * RING + u) * WV, WV), :],
                                    red[:, v, :].rearrange("p (s h) -> p s h", h=HEADS), 1.0 / HC ** 0.5, None,
                                    ALU.mult).then_inc(credit, 1)
            dve.wait_ge(credit, (PASS_L3 + 1) * WAVES + RING)
            step("gm", V.tensor_tensor(gmask, iota[:, 0:NCH].unsqueeze(1).to_broadcast([P, SLOTS, NCH]),
                                       grp[:, :].unsqueeze(2).to_broadcast([P, SLOTS, NCH]), ALU.is_equal))
            with dve.Fori(0, EXTRA // WV) as i:
                t = load_tiles(dve, tix, i)
                for j in range(WV):
                    dve.wait_ge(a_out, i * WV + (j + 1))
                    V.tensor_tensor(alE[:, ds(t[j], 1), :], alE[:, ds(t[j], 1), :],
                                    alE[:, ds(i * WV + (TILES + j), 1), :], ALU.add).then_inc(a_out, 1)
            dve.wait_ge(a_out, EXTRA + 1)
            alT = ring_flat[:, 0:4096].rearrange("p (h c) -> p h c", h=HEADS)
            fwd = ring_flat[:, 4096:8192].rearrange("p (h c) -> p h c", h=HEADS)
            bwd = nodes[:, 2:4, :].rearrange("p a b -> p (a b)")[:, 0:4096].rearrange("p (h c) -> p h c", h=HEADS)
            step("t_z", V.memset(alT, 0.0))
            after("t_z")
            for h in range(HEADS):
                dve.wait_ge(s_pe, PE[f"alT{h}"])
                step(f"t_a{h}", V.tensor_copy(alT[:, h, 0:384], ps[:, h, 0:384]))
                step(f"t_b{h}", V.tensor_copy(alT[0:LAST, h, 384:512], ps[0:LAST, h, 384:512]))
                after(f"t_b{h}")
                step(f"t_s{h}", V.tensor_tensor_scan(fwd[:, h, :], fF, alT[:, h, :], -BIG, ALU.add, ALU.max))
                step(f"t_r{h}", V.tensor_tensor_scan(bwd[:, h, ::-1], fB[:, ::-1], alT[:, h, ::-1], -BIG, ALU.add,
                                                     ALU.max))
            after(f"t_r{HEADS - 1}")
            ht = small[:, 448:448 + 64].rearrange("p (w b h) -> p w b h", w=2, b=4)
            step("t_h0", V.tensor_copy(ht[:, 0, :, :], bwd.rearrange("p h (b e) -> p b h e", e=P)[:, :, :, 0]))
            step("t_h1", V.tensor_copy(ht[:, 1, :, :], fwd.rearrange("p h (b e) -> p b h e", e=P)[:, :, :, P - 1]))
            dve.wait_ge(s_pe, PE["line"])
            for j in range(4):
                step(f"t_l{j}", V.tensor_copy(L8[j], ps[0:HEADS, 1 + j, :]))
            after("t_l3")
            n1 = slice(1, 512)
            n0 = slice(0, 511)
            for b in range(2):
                dve.wait_ge(a_st[b], 16 * (WAVES // 2 + 1))
            for j in range(4, 12):
                step(f"c_i{j}", V.memset(L8[j], -BIG))
            after("c_i11")
            step("c_1", V.tensor_tensor(conn[:, n1], fd[:, n1], ld[:, n0], ALU.is_equal))
            step("c_2", V.tensor_tensor(full, fd, ld, ALU.is_equal))
            after("c_2")
            step("c_3", V.tensor_tensor(A[:, n1], conn[:, n1], full[:, n0], ALU.mult))
            step("c_4", V.tensor_tensor(B[:, n1], conn[:, n1], full[:, n1], ALU.mult))
            after("c_4")
            for j, x in enumerate((A, B, conn)):
                step(f"c_5{j}", V.tensor_scalar(x[:, n1], x[:, n1], -1.0, BIG, ALU.add, ALU.mult))
            after("c_52")
            step("c_6", V.tensor_tensor(Dd[:, n1], tl[:, n0], conn[:, n1], ALU.add))
            step("c_7", V.tensor_tensor(De[:, n1], hd[:, n1], conn[:, n1], ALU.add))
            after("c_7")
            step("c_8", V.tensor_tensor_scan(cf[:, n1], A[:, n1], Dd[:, n1], -BIG, ALU.add, ALU.max))
            step("c_9", V.tensor_tensor_scan(cb[:, 510::-1], B[:, 511:0:-1], De[:, 511:0:-1], -BIG, ALU.add, ALU.max))
            dve.wait_ge(s_pe, PE["carry"])
            keep = small[:, 512:512 + 64].rearrange("p (w h b) -> p w h b", w=2, b=4)
            al4 = alT.rearrange("p h (b e) -> p h b e", e=P)
            crr = ps[:, 5, 0:64].rearrange("p (w b h) -> p w h b", w=2, b=4)
            for j, e in enumerate((0, P - 1)):
                step(f"k_{j}", V.tensor_copy(keep[:, j, :, :], al4[:, :, :, e]))
            after("k_1")
            for j, e in enumerate((0, P - 1)):
                step(f"k_m{j}", V.tensor_tensor(al4[:, :, :, e], keep[:, j, :, :], crr[:, j, :, :], ALU.max))
            after("k_m1")
            for h in range(HEADS):
                step(f"u_s{h}", V.tensor_tensor_scan(fwd[:, h, :], fF, alT[:, h, :], -BIG, ALU.add, ALU.max))
                step(f"u_r{h}", V.tensor_tensor_scan(bwd[:, h, ::-1], fB[:, ::-1], alT[:, h, ::-1], -BIG, ALU.add,
                                                     ALU.max))
            after(f"u_r{HEADS - 1}")
            for j, e in enumerate((0, P - 1)):
                step(f"k_b{j}", V.tensor_copy(al4[:, :, :, e], keep[:, j, :, :]))
            for h in range(HEADS):
                step(f"mx_{h}", V.tensor_tensor(fwd[:, h, :], fwd[:, h, :], bwd[:, h, :], ALU.max))
            after(f"mx_{HEADS - 1}")
            for h in range(HEADS):
                step(f"sub{h}", V.tensor_tensor(alT[:, h, :], alT[:, h, :], fwd[:, h, :], ALU.subtract))
            for h in range(HEADS):
                dve.wait_ge(s_pe, PE[f"exE{h}"])
                step(f"ex{h}", V.tensor_copy(alE[:, 0:TILES, h], ps[:, h, 0:TILES]))
            after(f"ex{HEADS - 1}")
            with dve.Fori(0, EXTRA // WV) as i:
                t = load_tiles(dve, tix, i)
                for j in range(WV):
                    V.tensor_scalar(alE[:, ds(i * WV + (TILES + j), 1), :], alE[:, ds(t[j], 1), :], 0.0, None, ALU.add)
            step("ex_done", V.tensor_copy(alE[:, TILES + EXTRA:SLOTS, :], alE[:, 0:SLOTS - TILES - EXTRA, :]))
            after("ex_done")
            exg5 = exg.rearrange("p b s (g h) -> p b s g h", h=HEADS)
            with dve.Fori(0, TURNS) as i:
                for u in range(RING):
                    g = i * RING + u
                    sl = ds(g * WV, WV)
                    dve.wait_ge(b_used, g + (RING - 1))
                    one_hot(PASS_L3, i, u)
                    V.tensor_tensor(exg5[:, u, :, :, :], alE[:, sl, :].unsqueeze(2).to_broadcast([P, WV, NCH, HEADS]),
                                    gmask[:, sl, :].unsqueeze(3).to_broadcast([P, WV, NCH, HEADS]), ALU.mult)
                    dve.wait_ge(b_ld[u], (i + 1) * 16)
                    vv = ring[:, u, 0:WV // 2, :].rearrange("p a (s c) -> p (a s) c", c=HC)
                    V.tensor_tensor(vv, vv, alE[:, sl, :].rearrange("p s h -> p (s h)").unsqueeze(2)
                                    .to_broadcast([P, WV * HEADS, HC]), ALU.mult).then_inc(b_ready, 1)

            dve.wait_ge(b_used, WAVES + RING)
            G = HEADS * NCH
            for c in range(0, NCH, 2):
                c0, cw = CH[c]
                step(f"o{c}", V.tensor_copy(gT[:, c0:c0 + cw], ps[:, c, 0:cw]))
            step("den", V.tensor_scalar(den, ps[0:G, 7, :], 1e-16, None, ALU.add))
            after("den")
            step("rden", V.reciprocal(rden, den))
            dve.wait_ge(s_ac, AC[f"o{NCH - 2}"])
            for c, (c0, cw) in enumerate(CH):
                b = c % 2
                o = gT[:, c0:c0 + cw]
                dve.wait_ge(f_mm, 2 * c + 1)
                V.tensor_tensor(o, o, ps[:, 2 + b, 0:cw], ALU.mult).then_inc(f_dve, 1)
                dve.wait_ge(f_dve, 3 * c + 1)
                dve.wait_ge(f_act, 2 * c + 1)
                V.tensor_tensor(wk[:, 1, b, 0:cw], o, wk[:, 0, b, 0:cw], ALU.subtract).then_inc(f_dve, 1)
                dve.wait_ge(f_act, 2 * c + 2)
                step(f"at{c}", V.tensor_tensor(wk[:, 2, b, 0:cw], wk[:, 1, b, 0:cw], wk[:, 3, b, 0:cw], ALU.mult))
                after(f"at{c}")
                step(f"xa{c}", V.tensor_tensor(wk[:, 2, b, 0:cw], o, wk[:, 2, b, 0:cw], ALU.subtract))
                after(f"xa{c}")
                V.tensor_tensor(hT[:, c0:c0 + cw], xT[:, c0:c0 + cw], wk[:, 2, b, 0:cw], ALU.add).then_inc(f_dve, 1)
            dve.wait_ge(f_dve, 3 * NCH)
            stats(hT, lambda c: None, "gn")
            step("gn_m", V.tensor_tensor(small[:, 6:7], small[:, 0:1], b_("L3_gn_ms"), ALU.mult))
            after("gn_m")
            step("gn_d", V.tensor_tensor(small[:, 7:8], small[:, 0:1], small[:, 6:7], ALU.subtract))
            after("gn_d")
            step("gn_d2", V.tensor_tensor(small[:, 7:8], small[:, 7:8], small[:, 7:8], ALU.mult))
            after("gn_d2")
            step("gn_var", V.tensor_tensor(small[:, 1:2], small[:, 1:2], small[:, 7:8], ALU.add))
            dve.wait_ge(s_ac, AC["gn_sqrt"])
            step("gn_rs", V.reciprocal(small[:, 3:4], small[:, 2:3]))
            after("gn_rs")
            step("gn_scale", V.tensor_tensor(small[:, 4:5], small[:, 3:4], b_("L3_gn_w"), ALU.mult))
            after("gn_scale")
            step("gn_ms", V.tensor_tensor(small[:, 7:8], small[:, 4:5], small[:, 6:7], ALU.mult))
            after("gn_ms")
            step("gn_shift", V.tensor_tensor(small[:, 5:6], b_("L3_gn_b"), small[:, 7:8], ALU.subtract))
            for c, (c0, cw) in enumerate(CH):
                dve.wait_ge(s_pe, PE[f"ffo{c}"])
                step(f"y{c}", V.scalar_tensor_tensor(yT[:, c0:c0 + cw], ps[:, 4 + c % 2, 0:cw], b_("L3_b2"),
                                                     hT[:, c0:c0 + cw], ALU.add, ALU.add))
                after(f"y{c}")
                V.tensor_tensor(yT[:, c0:c0 + cw], yT[:, c0:c0 + cw], xT[:, c0:c0 + cw], ALU.add).then_inc(ln_y, 1)
            dve.wait_ge(ln_y, 4 * NCH)
            norm(3, lambda c: None)

        @block.tensor
        def _(pe):
            T = nc.tensor
            n_pe = [0]

            def step(name, ins):
                n_pe[0] += 1
                seen["PE"].append(name)
                ins.then_inc(s_pe, 1)

            def mm(o, lhsT, rhs, start=True, stop=True):
                return T.matmul(o, lhsT, rhs, start=start, stop=stop, skip_group_check=True)

            def zero(banks):
                for b in banks:
                    mm(ps[:, b, :], zrow[0:1, 0:P], zrow[0:1, :], stop=False)

            pe.wait_ge(s_w, NLOADS)
            pe.wait_ge(s_dv, DV["f_sum"])
            step("flag", mm(ps[:, 7, 0:1], ones, small[:, 639:640]))
            pe.wait_ge(s_dv, DV["flag"])
            unsorted = pe.value_load(flag[0:1, 0:1], min_val=0, max_val=1)
            with pe.If(unsorted > 0):
                with pe.Fori(0, SORT_TILES // 2) as c:
                    pe.wait_ge(srt_in, c + 1)
                    for v_ in range(2):
                        ins = T.transpose(ps[:, 6, v_ * P:(v_ + 1) * P], turn_in[:, v_, :], ident)
                    ins.then_inc(srt_row, 1)
            pe.wait_ge(s_dv, DV["w_cnt1"])
            step("off", mm(ps[:, 7, 0:EXTRA], ones, small[:, 0:EXTRA]))
            pe.wait_ge(s_dv, DV["w_gx"])
            mm(ps[:, 5, 0:SLOTS], ones[0:1, :], basef[0:1, 0, :])
            step("base", mm(ps[:, 6, 0:SLOTS], ones[0:1, :], basef[0:1, 1, :]))
            pe.wait_ge(s_dv, DV["x_last"])
            for q in range(WAVES // 4):
                if q >= 4:
                    pe.wait_ge(s_ac, q - 3)
                for j in range(4):
                    g = 4 * q + j
                    ins = T.transpose(ps[:, q % 4, j * P:(j + 1) * P],
                                      rec[:, g * WV:(g + 1) * WV, :].rearrange("p s f -> p (s f)"), ident)
                step(f"recT{q}", ins)
            blocks = [(b * P, min(P, TILES - b * P)) for b in range(4)]
            for b, (t0, tn) in enumerate(blocks):
                ins = T.transpose(ps[0:tn, 4, b * P:(b + 1) * P], rec[:, t0:t0 + tn, F_DST], ident)
            step("dT", ins)

            def table(t, h, wts, width, first):
                for n in range(WIN):
                    if n == 0:
                        first()
                    if n >= RING:
                        pe.wait_ge(mt_ev, t * WIN + (n - RING + 1))
                    mm(ps[:, n % RING, 0:width], h[:, n * P:(n + 1) * P], wts).then_inc(mt_mm, 1)

            def sums(k):
                with pe.Fori(0, TURNS) as i:
                    for u in range(RING):
                        cs = load_cols(pe, cols, i, u)
                        pe.wait_ge(gat[u], (k * TURNS + i + 1) * (16 * WV))
                        pe.wait_ge(oh_ready, oh_no(k, i, u))
                        for j in range(WV):
                            ins = mm(psf[:, ds(cs[j], P)], ring[:, u, j, 0:D], oh[:, u % 2, j, :], start=False,
                                     stop=False)
                        ins.then_inc(credit, 1)

            def gru(r, L, gin, hin):
                wi, wh = w(L + "_wihT", 0, 3), w(L + "_whhT", 0, 3)
                for c, (c0, cw) in enumerate(CH):
                    b = c % 2
                    if c == 0:
                        gin()
                    if c >= 2:
                        pe.wait_ge(gru_p, r * NCH + (c - 1))
                        pe.wait_ge(gru_z, r * NCH + (c - 1))
                    g, h = rT[:, c0:c0 + cw], hin[:, c0:c0 + cw]
                    for j in range(2):
                        mm(ps[:, 4 * b + j, 0:cw], wi[:, j * P:(j + 1) * P], g, stop=False)
                        mm(ps[:, 4 * b + j, 0:cw], wh[:, j * P:(j + 1) * P], h, start=False)
                    mm(ps[:, 4 * b + 2, 0:cw], wi[:, 2 * P:3 * P], g)
                    mm(ps[:, 4 * b + 3, 0:cw], wh[:, 2 * P:3 * P], h).then_inc(gru_mm, 1)

            def norm(ln, banks_free):
                n0 = NCH * ln
                for c in range(NCH + 3):
                    if 2 <= c <= NCH + 1:
                        w0, nw = CH[c - 2][0] // P, CH[c - 2][1] // P
                        pe.wait_ge(ln_r, n0 + c - 1)
                        if c >= 4:
                            pe.wait_ge(ln_x, n0 + c - 3)
                        for j in range(nw):
                            ins = T.transpose(ps[:, 6 + c % 2, j * P:(j + 1) * P],
                                              rs[:, w0 + j:w0 + j + 1].to_broadcast([P, P]), ident)
                        ins.then_inc(ln_b, 1)
                    if c < NCH:
                        c0, cw = CH[c]
                        if c == 0:
                            banks_free()
                        pe.wait_ge(ln_y, n0 + c + 1)
                        if c >= 2:
                            pe.wait_ge(ln_c, n0 + c - 1)
                        mm(ps[:, c % 2, 0:cw], onesD, yT[:, c0:c0 + cw]).then_inc(ln_m, 1)
                    if 1 <= c <= NCH:
                        cw, b = CH[c - 1][1], (c - 1) % 2
                        pe.wait_ge(ln_q, n0 + c)
                        if c >= 3:
                            pe.wait_ge(ln_s, n0 + c - 2)
                        for j in range(cw // P):
                            ins = mm(ps[:, 2 + b, j:j + 1], wk[:, 1, b, j * P:(j + 1) * P], onesD[:, 0:1])
                        ins.then_inc(ln_v, 1)
                    if c >= 3 and ln != 2:
                        c0, cw = CH[c - 3]
                        pe.wait_ge(ln_x, n0 + c - 2)
                        if c >= 5:
                            pe.wait_ge(ln_o, NCH * OUTS[ln] + c - 4)
                        for j in range(cw // P):
                            ins = T.transpose(ps[:, 4 + (c - 3) % 2, j * P:(j + 1) * P],
                                              xT[:, c0 + j * P:c0 + (j + 1) * P], ident)
                        ins.then_inc(ln_t, 1)

            def after_recT():
                pe.wait_ge(s_ac, AC[f"recT{WAVES // 4 - 1}"])
                pe.wait_ge(s_dv, DV["i_gm"])
            table(0, hT, w("L0_WmsgT", 0, 4), 512, after_recT)
            pe.wait_ge(mt_ev, WIN)
            pe.wait_ge(s_dv, DV["z_t9"])
            zero(range(NCH))
            with pe.Fori(0, WAVES // RING) as i:
                for u in range(RING):
                    cs = load_cols(pe, cols, i, u)
                    pe.wait_ge(cnt_oh, i * RING + (u + 1))
                    for j in range(WV):
                        ins = mm(psf[:, ds(cs[j], P)], t9oh[:, u % 2, j, :], ohb[:, u % 2, j, :], start=False, stop=False)
                    ins.then_inc(cnt_mm, 1)
            pe.wait_ge(s_dv, DV[f"c9_{NCH - 1}"])
            pe.wait_ge(s_ac, AC[f"c9_{NCH - 2}"])
            rT = gT

            def evacuated(k):
                def f():
                    pe.wait_ge(ev_d, (k + 1) * EV_D)
                    pe.wait_ge(ev_a, (k + 1) * EV_A)
                return f

            with pe.Fori(0, STEPS - 1) as s:
                zero(range(NCH))
                sums(s)
                gru(s, "L0", evacuated(s), hT)
                table(s + 1, hT, w("L0_WmsgT", 0, 4), 512, lambda: pe.wait_ge(gru_h, (s + 1) * NCH))
                pe.wait_ge(mt_ev, (s + 2) * WIN)
            zero(range(NCH))
            sums(STEPS - 1)
            gru(STEPS - 1, "L0", evacuated(STEPS - 1), hT)
            norm(0, lambda: pe.wait_ge(gru_h, STEPS * NCH))

            pe.wait_ge(ln_o, NCH)
            zero(range(NCH))
            with pe.Fori(0, TURNS) as i:
                for u in range(RING):
                    last, cs = (cs if u else None), load_cols(pe, cols, i, u)
                    for hf in range(2):
                        q = (i * RING + u) * 2 + hf
                        if hf == 0:
                            pe.wait_ge(oh_ready, oh_no(PASS_L1, i, u))
                        pe.wait_ge(l1_msg, q + 1)
                        for j in range(4):
                            ins = mm(ps[:, 7, j * P:(j + 1) * P], wpad[:, 0, 4 * hf + j, :], rts[:, u % 2, :])
                        ins.then_inc(l1_hid, 1)
                        if u or hf:
                            u0, h0, c0 = (u, 0, cs) if hf else (u - 1, 1, last)
                            for j in range(4):
                                ins = mm(psf[:, ds(c0[4 * h0 + j], P)], ring[:, u0, 4 * h0 + j, 0:D],
                                         oh[:, u0 % 2, 4 * h0 + j, :], start=False, stop=False)
                            if not hf:
                                ins.then_inc(credit, 1)
                        pe.wait_ge(l1_relu, q + 1)
                        for j in range(4):
                            ins = mm(ps[:, 7, j * P:(j + 1) * P], pw[:, hf, j * P:(j + 1) * P], w("L1_pos_w2"))
                        ins.then_inc(l1_pe, 1)
                pe.wait_ge(l1_msg, (i + 1) * (2 * RING) + 1)
                for j in range(4):
                    ins = mm(psf[:, ds(cs[4 + j], P)], ring[:, RING - 1, 4 + j, 0:D],
                             oh[:, (RING - 1) % 2, 4 + j, :], start=False, stop=False)
                ins.then_inc(credit, 1)
            evacuated(PASS_L1)()
            for c, (c0, cw) in enumerate(CH):
                if c >= 2:
                    pe.wait_ge(s_dv, DV[f"mx{c - 2}"])
                step(f"cnt{c}", mm(ps[:, c % 2, 0:cw], ones, C9[:, c0:c0 + cw]))
            for c, (c0, cw) in enumerate(CH):
                pe.wait_ge(s_dv, DV[f"ag{c}"])
                if c >= 2:
                    pe.wait_ge(s_ac, AC[f"sage{c - 2}"])
                mm(ps[:, 4 + c % 2, 0:cw], w("L1_sage", 0), xT[:, c0:c0 + cw], stop=False)
                step(f"sage{c}", mm(ps[:, 4 + c % 2, 0:cw], w("L1_sage", 1), gT[:, c0:c0 + cw], start=False))
            norm(1, lambda: pe.wait_ge(s_ac, AC[f"sage{NCH - 1}"]))

            pe.wait_ge(ln_o, 2 * NCH)
            zero(range(NCH))
            sums(PASS_L2)
            evacuated(PASS_L2)()
            NT9 = 9
            for c, (c0, cw) in enumerate(CH):
                if c >= 2:
                    pe.wait_ge(s_ac, AC[f"msg{c - 2}"])
                o = ps[:, c % 2, 0:cw]
                mm(o, w("L2_WmsgT"), gT[:, c0:c0 + cw], stop=False)
                mm(o, w("L2_emb", rows=NT9), C9[0:NT9, c0:c0 + cw], start=False, stop=False)
                step(f"msg{c}", mm(o, w("L2_bmsg9", rows=NT9), C9[0:NT9, c0:c0 + cw], start=False))
            rT = yT
            gru(STEPS, "L2", lambda: pe.wait_ge(s_ac, AC[f"msg{NCH - 1}"]), xT)
            norm(2, lambda: pe.wait_ge(gru_h, (STEPS + 1) * NCH))

            def after_l2():
                pe.wait_ge(ln_x, 3 * NCH)
                pe.wait_ge(ln_s, 3 * NCH)
            table(STEPS, xT, w("L3_qkv", 0, 3), 3 * D, after_l2)
            pe.wait_ge(mt_ev, (STEPS + 1) * WIN)
            q_rows = hT
            with pe.Fori(0, TURNS) as i:
                for u in range(RING):
                    g2 = (i * RING + u) * 2
                    cs = load_cols(pe, cols, i, u)
                    pe.wait_ge(oh_ready, oh_no(PASS_L3, i, u))
                    for hf in range(2):
                        for j in range(4):
                            ins = T.transpose(ps[:, 4 + hf, j * P:(j + 1) * P], oh[:, u % 2, 4 * hf + j, :], ident)
                        ins.then_inc(a_tp, 1)
                    pe.wait_ge(a_v, g2 + 1)
                    for hf in range(2):
                        for j in range(4):
                            ins = mm(ps[:, hf, j * P:(j + 1) * P], rts[:, u % 2, :], wpad[:, 1, 4 * hf + j, :])
                        ins.then_inc(a_e, 1)
                    pe.wait_ge(a_prod, g2 + 1)
                    for hf in range(2):
                        pe.wait_ge(a_oht, g2 + (hf + 1))
                        for j in range(4):
                            ins = mm(ps[:, 2 + hf, j * P:(j + 1) * P], oht[:, u % 2, (4 * hf + j) * P:(4 * hf + j + 1) * P],
                                     q_rows[:, ds(cs[4 * hf + j], P)])
                        ins.then_inc(a_q, 1)
            pe.wait_ge(a_out, EXTRA + 1)
            for h in range(HEADS):
                for b, (t0, tn) in enumerate(blocks):
                    ins = T.transpose(ps[0:tn, h, b * P:(b + 1) * P], alE[:, t0:t0 + tn, h], ident)
                step(f"alT{h}", ins)
            pe.wait_ge(s_dv, DV["t_h1"])
            for j in range(4):
                src = small[:, 384 + 32 * j:384 + 32 * j + 32].rearrange("p (b h) -> p b h", b=4)
                for b in range(4):
                    ins = T.transpose(ps[0:HEADS, 1 + j, b * P:(b + 1) * P], src[:, b, :], ident)
            step("line", ins)
            pe.wait_ge(s_dv, DV["c_9"])
            for j in range(2):
                for b in range(4):
                    o = (j * 4 + b) * HEADS
                    ins = T.transpose(ps[:, 5, o:o + HEADS],
                                      (cf, cb)[j][:, b * P:(b + 1) * P],
                                      ident[0:HEADS, 0:HEADS])
            step("carry", ins)
            alT = ring_flat[:, 0:4096].rearrange("p (h b e) -> p h b e", h=HEADS, b=4)
            for h in range(HEADS):
                pe.wait_ge(s_ac, AC[f"exp{h}"])
                for b, (t0, tn) in enumerate(blocks):
                    ins = T.transpose(ps[:, h, t0:t0 + tn], alT[0:tn, h, b, :], ident[0:tn, 0:tn])
                step(f"exE{h}", ins)
            pe.wait_ge(s_dv, DV["ex_done"])
            zero(range(8))
            with pe.Fori(0, TURNS) as i:
                for u in range(RING):
                    cs = load_cols(pe, cols, i, u)
                    c7 = load_cols(pe, cols7, i, u, 512 - P)
                    pe.wait_ge(b_ready, i * RING + (u + 1))
                    for j in range(WV):
                        mm(psf[:, ds(cs[j], P)], ring[:, u, j // 2, (j % 2) * D:(j % 2 + 1) * D], oh[:, u % 2, j, :],
                           start=False, stop=False)
                        ins = mm(psf[0:HEADS * NCH, ds(c7[j] + 7 * 512, P)], exg[:, u, j, :], oh[:, u % 2, j, :],
                                 start=False, stop=False)
                    ins.then_inc(b_used, 1)
            pe.wait_ge(s_dv, DV["rden"])
            pe.wait_ge(s_ac, AC[f"o{NCH - 2}"])
            for c, (c0, cw) in enumerate(CH):
                b = c % 2
                x, o = xT[:, c0:c0 + cw], gT[:, c0:c0 + cw]
                if c >= 2:
                    pe.wait_ge(f_dve, 3 * (c - 2) + 1)
                    pe.wait_ge(f_act, 2 * (c - 2) + 2)
                mm(ps[:, b, 0:cw], w("L3_Wskip"), x)
                mm(ps[:, 2 + b, 0:cw], sel[:, c, :], rden[:, 0:cw]).then_inc(f_mm, 1)
                pe.wait_ge(f_dve, 3 * c + 2)
                pe.wait_ge(f_act, 2 * c + 1)
                mm(ps[:, 4 + b, 0:cw], wbeta[:, 0, :], o, stop=False)
                mm(ps[:, 4 + b, 0:cw], wbeta[:, 1, :], wk[:, 0, b, 0:cw], start=False, stop=False)
                mm(ps[:, 4 + b, 0:cw], wbeta[:, 2, :], wk[:, 1, b, 0:cw], start=False).then_inc(f_mm, 1)
            for c, (c0, cw) in enumerate(CH):
                pe.wait_ge(s_ac, AC[f"gn{c}"])
                for j in range(4):
                    if c >= 1:
                        pe.wait_ge(s_ac, AC[f"gelu{c - 1}_{j}"])
                    step(f"ff{c}_{j}", mm(ps[:, j, 0:cw], w("L3_W1", j), hT[:, c0:c0 + cw]))
                if c >= 2:
                    pe.wait_ge(s_dv, DV[f"y{c - 2}"])
                for j in range(4):
                    pe.wait_ge(s_ac, AC[f"gelu{c}_{j}"])
                    ins = mm(ps[:, 4 + c % 2, 0:cw], w("L3_W2", j), wk[:, j // 2, j % 2, 0:cw], start=(j == 0),
                             stop=(j == 3))
                step(f"ffo{c}", ins)
            norm(3, lambda: pe.wait_ge(ln_y, 4 * NCH))


GRU_COLS = [f"{L}_{n}" for L in ("L0", "L2") for n in ("bih_r", "bih_z", "bin", "bhh_r", "bhh_z", "bhn")]
HOST_COLS = GRU_COLS + ["L1_sage_b", "L1_gamma", "L1_beta", "L3_bskip", "L3_gn_w", "L3_gn_b", "L3_gn_ms", "L3_b2",
                        "L3_b1_0", "L3_b1_1", "L3_b1_2", "L3_b1_3", "L3_wbeta0", "L3_wbeta1", "L3_wbeta2", "eps"]
BCOLS = HOST_COLS + ["L0_br", "L0_bz", "L2_br", "L2_bz"]


def kernel(**inputs):
    import numpy as np
    import concourse.bacc as bacc
    from concourse import mybir as _mybir
    from concourse.bass_utils import run_bass_kernel_spmd

    v = {k: np.asarray(x) for k, x in inputs.items()}
    f32 = np.float32
    EP = TILES * P

    def pad(x, fill=0):
        out = np.full((EP,) + x.shape[1:], fill, x.dtype)
        out[:E] = x
        return out

    def tiles(x):
        x = x.reshape((TILES, P) + x.shape[1:])
        return np.ascontiguousarray(np.swapaxes(x, 0, 1)).reshape(P, -1)

    a = {}
    xT = np.zeros((P, NP), v["x"].dtype)
    xT[:, :N] = v["x"].T
    a["xT"] = xT
    a["dst_t"] = tiles(pad(v["dst"], NP - 1))
    a["dstn_t"] = tiles(np.append(pad(v["dst"], NP - 1)[1:], v["dst"].dtype.type(NP - 1)))
    for n, k in (("src_t", "src"), ("t4_t", "edge_type_4"), ("t9_t", "edge_type_9"), ("attr10_t", "edge_attr_10"),
                 ("attr2_t", "edge_attr_2")):
        a[n] = tiles(pad(v[k]))
    a["L0_WmsgT"] = v["L0_gnn_W_msg"].T
    a["L0_wihT"], a["L0_whhT"] = v["L0_gnn_w_ih"].T, v["L0_gnn_w_hh"].T
    a["L1_pos_w2"] = v["L1_gnn_pos_w2"]
    a["L1_sage"] = np.concatenate([v["L1_gnn_sage_w"][:D], v["L1_gnn_sage_w"][D:]], 1)
    a["L2_WmsgT"] = v["L2_gnn_W_msg"].T
    a["L2_wihT"], a["L2_whhT"] = v["L2_gnn_W_ih"].T, v["L2_gnn_W_hh"].T
    a["L2_emb"] = v["L2_gnn_edge_embed"]
    a["L2_bmsg9"] = np.broadcast_to(v["L2_gnn_b_msg"], (9, D))
    a["L3_qkv"] = np.concatenate([v["L3_gnn_Wq"], v["L3_gnn_Wk"], v["L3_gnn_Wv"]], 1)
    a["L3_Wskip"] = v["L3_gnn_Wskip"]
    a["L3_W1"] = v["L3_gnn_W1"]
    a["L3_W2"] = np.concatenate([v["L3_gnn_W2"][j * D:(j + 1) * D] for j in range(4)], 1)
    a["brows"] = np.concatenate([v["L0_gnn_b_msg"], v["L3_gnn_bq"], v["L3_gnn_bk"], v["L3_gnn_bv"]])
    col = {}
    for L, bi, bh in (("L0", v["L0_gnn_b_ih"], v["L0_gnn_b_hh"]), ("L2", v["L2_gnn_b_ih"], v["L2_gnn_b_hh"])):
        for j, (n, m) in enumerate((("bih_r", "bhh_r"), ("bih_z", "bhh_z"), ("bin", "bhn"))):
            col[f"{L}_{n}"], col[f"{L}_{m}"] = bi[j * D:(j + 1) * D], bh[j * D:(j + 1) * D]
    for n, k in (("L1_sage_b", "L1_gnn_sage_b"), ("L1_gamma", "L1_gnn_bn_gamma"), ("L1_beta", "L1_gnn_bn_beta"),
                 ("L3_bskip", "L3_gnn_bskip"), ("L3_gn_w", "L3_gnn_gn_w"), ("L3_gn_b", "L3_gnn_gn_b"),
                 ("L3_gn_ms", "L3_gnn_gn_ms"), ("L3_b2", "L3_gnn_b2")):
        col[n] = v[k]
    for j in range(4):
        col[f"L3_b1_{j}"] = v["L3_gnn_b1"][j * D:(j + 1) * D]
    for j in range(3):
        col[f"L3_wbeta{j}"] = v["L3_gnn_Wbeta"][j * D:(j + 1) * D, 0]
    col["eps"] = np.full(D, EPS, f32)
    a["bcols"] = np.stack([col[n] for n in HOST_COLS], 1)
    a["consts"] = np.concatenate([np.eye(P), np.tile(np.arange(P), (P, 1)), np.ones((P, P)),
                                  np.full((P, P), 1.0 / D)], 1).astype(f32)
    wpad = np.zeros((P, 2, WV, P), f32)
    for s in range(WV):
        wpad[s * FIELDS + F_ATTR2:s * FIELDS + F_ATTR2 + 2, 0, s] = v["L1_gnn_pos_w1"]
        wpad[s * FIELDS:s * FIELDS + 10, 1, s] = v["L3_gnn_We"]
    a["wpad"] = wpad.reshape(P, -1)
    sel = np.zeros((NCH, HEADS, NCH, HEADS, HC), f32)
    for g in range(NCH):
        for h in range(HEADS):
            sel[g, h, g, h] = 1
    a["sel"] = sel.reshape(NCH * HEADS, -1)

    def program(seen, known):
        nc = bacc.Bacc("TRN2", target_bir_lowering=False, num_devices=1)
        arrays, args = {}, {}
        for n, x in a.items():
            arrays["in_" + n] = np.ascontiguousarray(x)
            args[n] = nc.dram_tensor("in_" + n, x.shape, _mybir.dt.from_np(x.dtype), kind="ExternalInput").ap()
        out = nc.dram_tensor("out_x", (N, D), _mybir.dt.float32, kind="ExternalOutput").ap()
        build(nc, args, out, seen, known)
        return nc, arrays
    seen = {"DV": [], "PE": [], "AC": []}
    program(seen, None)
    nc, arrays = program({"DV": [], "PE": [], "AC": []}, seen)
    r = run_bass_kernel_spmd(nc, [arrays], core_ids=[0])
    return r.results[0]["out_x"]
```

```python
from contextlib import ExitStack

import numpy as np
import concourse.bass as bass
from concourse import mybir

F32 = mybir.dt.float32
BF16 = mybir.dt.bfloat16
I32 = mybir.dt.int32
ALU = mybir.AluOpType
ACT = mybir.ActivationFunctionType
AX = mybir.AxisListType
ds = bass.ds

P = 128
N = 3125
E = 50000
D = 128
ET = 4
HEADS, HC = 8, 16
WIN = (N + P - 1) // P
NP = WIN * P
TILES = (E + P - 1) // P
EXTRA = WIN - 1
WV = 8
WAVES = -(-(TILES + EXTRA) // WV)
SLOTS = WAVES * WV
RING = 4
TURNS = WAVES // RING
AHEAD = RING - 1
GATES = WAVES // 2 + 1
STAGED = WAVES + AHEAD
FIELDS = 16
F_ATTR2, F_DST, F_SRC, F_T4, F_T9 = 10, 12, 13, 14, 15
CH = [(c * 512, min(512, NP - c * 512)) for c in range(-(-NP // 512))]
NCH = len(CH)
EV_D = (NCH + 1) // 2
EV_A = NCH // 2
FAR = 1.0e6
BIG = 1.0e38
STEPS = 4
FIRST_ACT = 9
EX_DV = 6
NT = 16
SORT_G = 23
SORT_N = TILES // SORT_G
SORT_TILES = TILES + TILES % 2
assert SORT_N * SORT_G == TILES
EPS = 1e-5
OUTS = [0, 1, 2, 2, 3]
MT_SLOTS = [len(range(b, WIN, RING)) for b in range(RING)]
assert WAVES % RING == 0



def LN_DMA(ln, b):
    return 16 * OUTS[ln] * len(range(b, NCH, 2))


def load_cols(pe, row, i, u, hi=NP - P):
    return pe.bass.values_load_multi_w_load_instructions(
        row[0:1, ds((i * RING + u) * WV, WV)], engines=[mybir.EngineType.PE], min_val=0, max_val=hi,
        skip_runtime_bounds_check_because="window starts are multiples of 128 under 3200 by construction")[1]


def load_tiles(dve, tix, i):
    return dve.bass.values_load_multi_w_load_instructions(
        tix[0:1, ds(i * WV, WV)], engines=[mybir.EngineType.DVE], min_val=0, max_val=TILES - 1,
        skip_runtime_bounds_check_because="a number of edges before the last, over 128")[1]


PASS_L1, PASS_L2, PASS_L3 = STEPS, STEPS + 1, STEPS + 2


class Any1(dict):

    def __missing__(self, k):
        return 1


def build(nc, a, out, seen, known):
    ctx = ExitStack()
    with ctx:
        def sb(name, shape, dt=F32):
            return ctx.enter_context(nc.sbuf_tensor(name, shape, dt))

        def sem(name):
            return ctx.enter_context(nc.semaphore(name))

        def dram(name, shape):
            return nc.dram_tensor(name, shape, F32, kind="Internal").ap()

        m_tab = dram("m_tab", (NP * ET, D))
        x_tab = [dram(f"x_tab{i}", (NP, D)) for i in (1, 2)]
        kv_tab = dram("kv_tab", (NP, 2 * D))
        sorted_dr = dram("sorted_dr", (TILES * P, FIELDS))
        ve_dr = dram("ve_dr", (WAVES * P, WV * D))

        rec = sb("rec", [P, SLOTS, FIELDS])
        rec_flat = rec[:, :, :].rearrange("p s f -> p (s f)")
        recT = sb("recT", [P, (WAVES + 1) * P])
        idx4 = sb("idx4", [P, STAGED * WV], I32)
        idx1 = sb("idx1", [P, STAGED * WV], I32)
        dl = sb("dl", [P, SLOTS + WV])
        dlb = sb("dlb", [P, SLOTS], BF16)
        t9b = sb("t9b", [P, SLOTS], BF16)
        cols = sb("cols", [1, SLOTS], I32)
        cols16 = sb("cols16", [1, SLOTS], I32)
        cols24 = sb("cols24", [1, SLOTS], I32)
        tix = sb("tix", [1, 2 * EXTRA], I32)
        basef = sb("basef", [1, SLOTS])
        ring = sb("ring", [P, RING, WV, 2 * D])
        ring_flat = ring[:, :, :, :].rearrange("p r w d -> p (r w d)")
        raw_i = ring_flat[:, 12 * TILES:16 * TILES].bitcast(I32).rearrange("p (k t) -> p k t", k=4)
        next_i = ring_flat[:, 16 * TILES:17 * TILES].bitcast(I32)
        wk = ring_flat[:, 0:6 * 1024].rearrange("p (k b c) -> p k b c", k=6, b=2)
        key = ring_flat[:, 0:SORT_TILES]
        rank, part, tile_no, one_s = (ring_flat[:, 512 + 512 * j:512 + 512 * j + SORT_TILES] for j in range(4))
        rank_i = ring_flat[:, 2560:2560 + TILES].bitcast(I32)
        turn_in = ring_flat[:, 3072:3072 + 2 * P].rearrange("p (v e) -> p v e", e=P)
        tri, tie = ring_flat[:, 3328:3328 + P], ring_flat[:, 3328 + P:3328 + P + 2]
        sc_rec = ring_flat[:, 3584:3584 + SORT_G * FIELDS].rearrange("p (g f) -> p g f", f=FIELDS)
        sc_idx = ring_flat[:, 4096:4096 + SORT_G].bitcast(I32)
        flag = sb("flag", [1, 1], I32)
        yc = ring_flat[:, 7168:8192].rearrange("p (b c) -> p b c", b=2)
        tb = ring_flat[:, 6144:6144 + RING * 512].rearrange("p (b c) -> p b c", b=RING)
        ixr = sb("ixr", [P, RING, WV], I32)
        oh = sb("oh", [P, 2, WV, P])
        rts = sb("rts", [P, 2, P])
        tb0 = oh[:, :, :, :].rearrange("p b s c -> p (b s c)").rearrange("p (b c) -> p b c", b=RING)
        nodes = sb("nodes", [P, 4, NP])
        xT, hT, gT, yT = (nodes[:, i, :] for i in range(4))
        hid = {"L0": (rec_flat[:, 0:NP], yT), "L2": (hT, yT)}
        pw = sb("pw", [P, 4, 512])
        C9 = rec_flat[0:NT, 0:NP]
        counts = rec_flat[:, NP:NP + WIN * NT].rearrange("p (w t) -> p w t", t=NT)
        alE = rec_flat[:, 0:SLOTS * HEADS].rearrange("p (s h) -> p s h", h=HEADS)
        oht = rec_flat[:, 3328:3328 + 2048].rearrange("p (b c) -> p b c", b=2)
        fF, fB = (rec_flat[:, 5376 + 512 * j:5888 + 512 * j] for j in range(2))
        ex3 = recT[:, 0:SLOTS * 12].bitcast(BF16).rearrange("p (s k h) -> p s k h", k=3, h=HEADS)
        ex3f = ex3.rearrange("p s k h -> p s (k h)")
        ex3w = recT[:, 5504:5504 + WV * 24].bitcast(BF16).rearrange("p (b s c) -> p b s c", b=2, s=WV)
        den, rden = (recT[:, SLOTS * 12 + WIN * HEADS * j:SLOTS * 12 + WIN * HEADS * (j + 1)] for j in range(2))
        rdenx = recT[:, 0:NP]
        rest = nodes[:, 1:3, :].rearrange("p a b -> p (a b)")
        wt = sb("wt", [P, 36, P])
        wpad = sb("wpad", [P, 2, WV, P])
        brow = sb("brow", [P, 512 + 3 * P])
        bc = sb("bc", [P, 48])
        cst = sb("cst", [P, 4 * P])
        ident, iota, ones, onesD = (cst[:, i * P:(i + 1) * P] for i in range(4))
        iotab = sb("iotab", [P, P], BF16)
        small = sb("small", [P, 640])
        sd, rs = small[:, 576:576 + WIN], small[:, 608:608 + WIN]
        gate = sb("gate", [1, 2])
        zrow = sb("zrow", [1, 512], BF16)
        ps = ctx.enter_context(nc.psum_tensor("ps", [P, 8, 512], F32))
        psf = ps[:, :, :].rearrange("p b c -> p (b c)")

        s_edge = sem("s_edge")
        srt_d = sem("srt_d")
        srt_in = sem("srt_in")
        srt_row = sem("srt_row")
        srt_cmp = sem("srt_cmp")
        srt_red = sem("srt_red")
        srt_acc = sem("srt_acc")
        srt_st = sem("srt_st")
        srt_gate = sem("srt_gate")
        srt_sc = sem("srt_sc")
        srt_ld = sem("srt_ld")
        s_attr = sem("s_attr")
        s_c = sem("s_c")
        s_w = sem("s_w")
        in_mm = sem("in_mm")
        s_dv = sem("s_dv")
        s_pe = sem("s_pe")
        s_ac = sem("s_ac")
        s_gate = sem("s_gate")
        ix_ready = sem("ix_ready")
        oh_ready = sem("oh_ready")
        credit = sem("credit")
        gat = [sem(f"gat{i}") for i in range(RING)]
        mt_mm = sem("mt_mm")
        mt_ev = sem("mt_ev")
        mt_ac = sem("mt_ac")
        mt_dma = [sem(f"mt_dma{i}") for i in range(RING)]
        ev_d = sem("ev_d")
        ev_a = sem("ev_a")
        hid_mm = sem("hid_mm")
        hid_ac = sem("hid_ac")
        gru_mm = sem("gru_mm")
        gru_ar = sem("gru_ar")
        gru_az = sem("gru_az")
        gru_r = sem("gru_r")
        gru_z = sem("gru_z")
        gru_t = sem("gru_t")
        gru_p = sem("gru_p")
        gru_n = sem("gru_n")
        gru_d = sem("gru_d")
        gru_e = sem("gru_e")
        gru_h = sem("gru_h")
        l1_hid = sem("l1_hid")
        l1_relu = sem("l1_relu")
        l1_pe = sem("l1_pe")
        l1_msg = sem("l1_msg")
        a_tp = sem("a_tp")
        a_e = sem("a_e")
        a_q = sem("a_q")
        a_oht = sem("a_oht")
        a_kv = sem("a_kv")
        a_v = sem("a_v")
        a_prod = sem("a_prod")
        a_red = sem("a_red")
        a_out = sem("a_out")
        a_st = [sem(f"a_st{i}") for i in range(2)]
        b_ld = [sem(f"b_ld{i}") for i in range(RING)]
        b_oh = sem("b_oh")
        b_ohb = sem("b_ohb")
        b_ready = sem("b_ready")
        b_used = sem("b_used")
        ln_y = sem("ln_y")
        ln_m = sem("ln_m")
        ln_c = sem("ln_c")
        ln_q = sem("ln_q")
        ln_v = sem("ln_v")
        ln_s = sem("ln_s")
        ln_r = sem("ln_r")
        ln_x = sem("ln_x")
        ln_b = sem("ln_b")
        ln_t = sem("ln_t")
        ln_o = sem("ln_o")
        ln_dma = [sem(f"ln_dma{i}") for i in range(2)]
        x_step = sem("x_step")
        SPREADS = (7, NCH - 2, NCH - 1)
        f_x, f_xs, f_b, f_sg, f_df, f_at, f_xa, f_h = (
            sem("f_" + n) for n in ("x", "xs", "b", "sg", "df", "at", "xa", "h"))

        W = {}
        loads = []

        def weight(name, src, k=1):
            i = sum(v[1] for v in W.values())
            W[name] = (i, k)
            loads.append((wt[:src.shape[0], i:i + k, :].rearrange("p k d -> p (k d)"), src))

        for n, k in (("L0_WmsgT", 4), ("L0_wihT", 3), ("L0_whhT", 3), ("L1_pos_w2", 1), ("L1_sage", 2),
                     ("L2_WmsgT", 1), ("L2_wihT", 3), ("L2_whhT", 3), ("L2_emb", 1), ("L2_bmsg9", 1),
                     ("L3_qkv", 3), ("L3_Wskip", 1), ("L3_W1", 4), ("L3_W2", 4)):
            weight(n, a[n], k)

        def w(name, j=0, k=1, rows=P):
            i = W[name][0] + j
            return wt[:rows, i:i + k, :].rearrange("p k d -> p (k d)")

        NBC = a["bcols"].shape[1]
        bcol = {n: i for i, n in enumerate(BCOLS)}

        def b_(name):
            return bc[:, bcol[name]:bcol[name] + 1]

        first = [(cst[:, :], a["consts"]), (bc[:, 0:NBC], a["bcols"]), loads.pop(0),
                 (brow[:, :], a["brows"].rearrange("(a n) -> a n", a=1).to_broadcast([P, brow.shape[1]])),
                 (hT, a["xT"])]
        loads += [(wpad[:, :, :, :].rearrange("p a s d -> p (a s d)"), a["wpad"]),
                  (xT, a["xT"])]
        NFIRST, NLOADS = 16 * len(first), 16 * len(loads)
        wbeta = recT[:, 6016:6016 + 2 * P].rearrange("p (j c) -> p j c", j=2)

        t9oh = pw[:, 0, 0:WV * NT].bitcast(BF16).rearrange("p (b s c) -> p b s c", b=2, c=NT)
        ohb = (pw[:, 2:4, :].rearrange("p a b -> p (a b)").bitcast(BF16)
               .rearrange("p (b s c) -> p b s c", b=2, c=P))
        cntc, inv = small[:, 208:208 + WIN], small[:, 176:176 + WIN]
        HALVES = slice(0, SLOTS // 2), slice(SLOTS // 2, SLOTS)
        RESTS = [rest[:, HEADS * h.start:HEADS * h.stop].rearrange("p (s h) -> p s h", h=HEADS) for h in HALVES]
        tail = nodes[:, 1:4, :].rearrange("p a b -> p (a b)")
        L8 = ([tail[0:HEADS, j * 512:(j + 1) * 512] for j in range(6)]
              + [tail[0:HEADS, NP + 4096 + j * 512:NP + 4608 + j * 512] for j in range(4)]
              + [pw[0:HEADS, j, :] for j in range(2)])
        fd, ld, hd, tl, conn, full, A, B, Dd, De, cf, cb = L8

        block = ctx.enter_context(nc.Block())

        def wave_no(k, i, u):
            return k * WAVES + i * RING + u

        FUSED = (0, 2, 3)
        MEAN, VAR, TURN, SPREAD = range(4)

        def bank(ln, use, c):
            return 4 + use if ln in FUSED else 2 * use + c % 2

        def deep(ln):
            return 1 if ln in FUSED else 2

        def oh_no(k, i, u):
            return wave_no(k, i, u) + (2 if k > PASS_L1 else 1)

        DV, PE, AC = ({n: i + 1 for i, n in enumerate(known[e])} if known else Any1() for e in ("DV", "PE", "AC"))

        @block.sync
        def _(sp):
            sp.dma_start(raw_i[:, 0, :], a["dst_t"]).then_inc(s_edge, 16)
            sp.dma_start(next_i, a["dstn_t"]).then_inc(s_edge, 16)
            for dst, src in first[0:1]:
                sp.dma_start(dst, src).then_inc(s_c, 16)
            for i, n in enumerate(("src_t", "t4_t", "t9_t")):
                sp.dma_start(raw_i[:, 1 + i, :], a[n]).then_inc(s_edge, 16)
            for dst, src in first[1:]:
                sp.dma_start(dst, src).then_inc(s_c, 16)
            sp.dma_start(ring_flat[:, 0:TILES * 10], a["attr10_t"]).then_inc(s_attr, 16)
            sp.dma_start(ring_flat[:, TILES * 10:TILES * 12], a["attr2_t"]).then_inc(s_attr, 16)
            for dst, src in loads:
                sp.dma_start(dst, src).then_inc(s_w, 16)

            def table(t, rows, width, buf=tb):
                for n in range(WIN):
                    b = n % RING
                    if buf is tb0 and n < FIRST_ACT:
                        sp.wait_ge(mt_ac, n + 1)
                    else:
                        sp.wait_ge(mt_ev, t * WIN + (n + 1) - FIRST_ACT)
                    sp.dma_start(rows[n], buf[:, b, 0:width]).then_inc(mt_dma[b], 16)

            m_rows = m_tab.rearrange("(n p t) d -> n p (t d)", p=P, t=ET)
            kv_rows = kv_tab.rearrange("(n p) d -> n p d", p=P)
            table(0, m_rows, 512, tb0)
            with sp.Fori(0, STEPS - 1) as s:
                table(s + 1, m_rows, 512)

            def rows_out(ln):
                for c, (c0, cw) in enumerate(CH):
                    sp.wait_ge(ln_o, NCH * OUTS[ln] + c + 1)
                    buf = tb[:, c % 2, 0:cw].rearrange("p (w d) -> p w d", d=D)
                    if ln < 3:
                        dst = x_tab[ln].rearrange("(w p) d -> p w d", p=P)[:, c0 // P:(c0 + cw) // P, :]
                    elif c0 + cw <= N:
                        dst = out.rearrange("(a w) d -> a w d", a=1)[0, c0:c0 + cw, :].rearrange("(w p) d -> p w d", p=P)
                    else:
                        dst = out[c0:N, :].rearrange("(w p) d -> p w d", w=1)
                        buf = buf[0:N - c0, :, :]
                    sp.dma_start(dst, buf).then_inc(ln_dma[c % 2], 16)

            for ln in (0, 1):
                rows_out(ln)
            table(STEPS, kv_rows, 2 * D)
            with sp.Fori(0, TURNS) as i:
                for u in range(RING):
                    sp.wait_ge(a_v, (i * RING + (u + 1)) * 2 + 1)
                    sp.dma_start(ve_dr[ds((i * RING + u) * P, P), :],
                                 pw[:, 2 * (u % 2):2 * (u % 2) + 2, :].rearrange("p a b -> p (a b)")
                                 ).then_inc(a_st[u % 2], 16)
            for b in range(2):
                sp.wait_ge(a_st[b], 16 * (WAVES // 2 + 1))
            sp.wait_ge(s_dv, DV["ex_done"])
            with sp.Fori(0, TURNS) as i:
                for u in range(RING):
                    sp.wait_ge(b_used, i * RING + (u + 1))
                    sp.dma_start(ring[:, u, 0:WV // 2, :].rearrange("p a b -> p (a b)"),
                                 ve_dr[ds((i * RING + u) * P, P), :]).then_inc(b_ld[u], 16)
            rows_out(3)
            for c in range(2):
                sp.wait_ge(ln_dma[c], LN_DMA(4, c))

        @block.gpsimd
        def _(pool):
            pool.wait_ge(s_c, NFIRST)
            pool.wait_ge(s_dv, DV["flag"])
            unsorted = pool.value_load(flag[0:1, 0:1], min_val=0, max_val=1)
            with pool.If(unsorted > 0):
                with pool.Fori(0, SORT_N) as c:
                    pool.wait_ge(srt_st, c * 2 + 2)
                    nc.gpsimd.tensor_tensor(gate[:, 0:1], cst[0:1, 0:1], cst[0:1, 0:1], ALU.add).then_inc(srt_gate, 1)
                    for g in range(SORT_G):
                        pool.indirect_dma_start(
                            sorted_dr, bass.IndirectOffsetOnAxis(ap=sc_idx[:, g:g + 1], axis=0),
                            sc_rec[:, g, :], None).then_inc(srt_sc, 16)
                    pool.wait_ge(srt_sc, (c + 1) * (16 * SORT_G))
                    pool.wait_ge(srt_gate, c * 2 + 1)
                    nc.gpsimd.tensor_tensor(gate[:, 1:2], cst[0:1, 0:1], cst[0:1, 0:1], ALU.add).then_inc(srt_gate, 1)
                pool.wait_ge(srt_gate, 2 * SORT_N)
                back = sorted_dr.rearrange("(t p) f -> p t f", p=P)
                for c in range(SORT_N):
                    cs = slice(c * SORT_G, (c + 1) * SORT_G)
                    pool.dma_start(rec[:, cs, :], back[:, cs, :]).then_inc(srt_ld, 16)

            def passage(gates, *waits):
                for s_, v_ in waits:
                    pool.wait_ge(s_, v_)
                pool.wait_ge(s_gate, gates + 1)
                nc.gpsimd.tensor_tensor(gate[:, 0:1], cst[0:1, 0:1], cst[0:1, 0:1], ALU.add).then_inc(s_gate, 1)

            def gathers(k, table, width):
                with pool.Fori(0, TURNS) as i:
                    for u in range(RING):
                        if u % 2 == 0:
                            passage(k * GATES + i * (RING // 2) + (u // 2 + 1),
                                    (ix_ready, k * STAGED + i * RING + (u + 2)))
                        for j in range(WV):
                            pool.indirect_dma_start(
                                ring[:, u, j, 0:width], None, table,
                                bass.IndirectOffsetOnAxis(ap=ixr[:, u, j:j + 1], axis=0)).then_inc(gat[u], 16)

            def norm(ln):
                for c in range(NCH):
                    ws = slice(CH[c][0] // P, (CH[c][0] + CH[c][1]) // P)
                    pool.wait_ge(ln_s, NCH * ln + c + 1)
                    nc.gpsimd.tensor_tensor(rs[:, ws], sd[:, ws], b_("minus_half").to_broadcast([P, CH[c][1] // P]),
                                            ALU.pow).then_inc(ln_r, 1)

            with pool.Fori(0, STEPS) as s:
                passage(s * GATES, *[(mt_dma[b], (s + 1) * (16 * MT_SLOTS[b])) for b in range(RING)])
                gathers(s, m_tab, D)
            for k, ln in ((PASS_L1, 0), (PASS_L2, 1)):
                norm(ln)
                passage(k * GATES, *[(ln_dma[c], LN_DMA(ln + 1, c)) for c in range(2)])
                gathers(k, x_tab[ln], D)
            norm(2)
            passage(PASS_L3 * GATES,
                    *[(mt_dma[b], (STEPS + 1) * 16 * MT_SLOTS[b]) for b in range(RING)])
            gathers(PASS_L3, kv_tab, 2 * D)
            norm(3)

        @block.scalar
        def _(act):
            n_ac = [0]

            def step(name, ins):
                n_ac[0] += 1
                seen["AC"].append(name)
                ins.then_inc(s_ac, 1)

            act.wait_ge(s_attr, 32)
            R = rec[:, 0:TILES, :]
            step("r_a2", nc.scalar.activation(R[:, :, F_ATTR2:F_DST],
                                              ring_flat[:, TILES * 10:TILES * 12].rearrange("p (t f) -> p t f", f=2),
                                              ACT.Copy))
            step("r_a10", nc.scalar.activation(R[:, :, 0:10],
                                               ring_flat[:, 0:TILES * 10].rearrange("p (t f) -> p t f", f=10), ACT.Copy))
            for n in range(FIRST_ACT):
                b = n % RING
                act.wait_ge(in_mm, n + 1)
                if n >= RING:
                    act.wait_ge(mt_dma[b], 16 * (n // RING))
                nc.scalar.activation(tb0[:, b, :], ps[:, 4 + b, :], ACT.Copy).then_inc(mt_ac, 1)
            act.wait_ge(s_w, NLOADS)
            for q in range(WAVES // 4):
                act.wait_ge(s_pe, PE[f"recT{q}"])
                step(f"recT{q}", nc.scalar.activation(recT[:, q * 512:(q + 1) * 512], ps[:, q % 4, :], ACT.Copy))
            def evac(k):
                act.wait_ge(credit, (k + 1) * WAVES + RING)
                for c in range(1, NCH, 2):
                    c0, cw = CH[c]
                    nc.scalar.activation(gT[:, c0:c0 + cw], ps[:, c, 0:cw], ACT.Copy).then_inc(ev_a, 1)

            def hidden(r, L):
                for n in range(2 * NCH):
                    c0, cw = CH[n // 2]
                    act.wait_ge(hid_mm, r * (2 * NCH) + (n + 1))
                    nc.scalar.activation(hid[L][n % 2][:, c0:c0 + cw], ps[:, n % 8, 0:cw], ACT.Copy).then_inc(hid_ac, 1)

            def gru(r, L, c):
                if 1 <= c <= NCH:
                    cw, b = CH[c - 1][1], (c - 1) % 2
                    act.wait_ge(gru_p, r * NCH + c)
                    nc.scalar.activation(wk[:, 3, b, 0:cw], wk[:, 2, b, 0:cw], ACT.Tanh,
                                         bias=b_(L + "_bin")).then_inc(gru_n, 1)
                if c < NCH:
                    cw, b, t = CH[c][1], c % 2, r * NCH + (c + 1)
                    act.wait_ge(gru_ar, t)
                    nc.scalar.activation(wk[:, 0, b, 0:cw], wk[:, 0, b, 0:cw], ACT.Sigmoid,
                                         bias=b_(L + "_br")).then_inc(gru_r, 1)
                    act.wait_ge(gru_az, t)
                    nc.scalar.activation(wk[:, 1, b, 0:cw], wk[:, 1, b, 0:cw], ACT.Sigmoid,
                                         bias=b_(L + "_bz")).then_inc(gru_z, 1)

            def norm(ln, c):
                n0 = NCH * ln
                if 0 <= c < NCH:
                    cw, b = CH[c][1], c % 2
                    act.wait_ge(ln_c, n0 + c + 1)
                    if c >= 2:
                        act.wait_ge(ln_v, n0 + c - 1)
                    nc.scalar.activation(wk[:, 5, b, 0:cw], yc[:, b, 0:cw], ACT.Square).then_inc(ln_q, 1)
                if 3 <= c and ln != 2:
                    cw, b = CH[c - 3][1], (c - 3) % 2
                    act.wait_ge(ln_t, NCH * OUTS[ln] + c - 2)
                    if c >= 5:
                        act.wait_ge(ln_dma[b], LN_DMA(ln, b) + 16 * ((c - 3) // 2))
                    nc.scalar.activation(tb[:, b, 0:cw], ps[:, bank(ln, TURN, c - 3), 0:cw],
                                         ACT.Copy).then_inc(ln_o, 1)

            with act.Fori(0, STEPS - 1) as s:
                hidden(s, "L0")
                evac(s)
                for c in range(NCH + 1):
                    gru(s, "L0", c)
            hidden(STEPS - 1, "L0")
            evac(STEPS - 1)
            step("counts", nc.scalar.activation(counts, ps[:, 7, 0:WIN * NT].rearrange("p (w t) -> p w t", t=NT),
                                                ACT.Copy))
            for c in range(NCH + 5):
                gru(STEPS - 1, "L0", c)
                norm(0, c - 2)

            with act.Fori(0, TURNS) as i:
                for u in range(RING):
                    for hf in range(2):
                        q = (i * RING + u) * 2 + hf
                        act.wait_ge(l1_hid, q + 1)
                        nc.scalar.activation(pw[:, hf, :], ps[:, 7, :], ACT.Relu).then_inc(l1_relu, 1)
            evac(PASS_L1)
            for c, (c0, cw) in enumerate(CH):
                act.wait_ge(s_pe, PE[f"sage{c}"])
                step(f"sage{c}", nc.scalar.activation(yT[:, c0:c0 + cw], ps[:, 4 + c % 2, 0:cw], ACT.Identity,
                                                      bias=b_("L1_sage_b")))
            act.wait_ge(s_dv, DV["bn_agg"])
            step("bn_sqrt", nc.scalar.activation(small[:, 2:3], small[:, 1:2], ACT.Sqrt, bias=b_("eps")))

            def bn_relu(c):
                c0, cw = CH[c]
                if c == 0:
                    act.wait_ge(s_dv, DV["bn_shift"])
                nc.scalar.activation(yT[:, c0:c0 + cw], yT[:, c0:c0 + cw], ACT.Relu, bias=small[:, 5:6],
                                     scale=small[:, 4:5]).then_inc(x_step, 1)

            for c in range(NCH):
                bn_relu(c)
            for c in range(NCH + 3):
                norm(1, c)

            for c, (c0, cw) in enumerate(CH):
                act.wait_ge(s_pe, PE[f"c9_{c}"])
                step(f"c9_{c}", nc.scalar.activation(C9[:, c0:c0 + cw], ps[0:NT, 7, 0:cw], ACT.Copy))
            hidden(STEPS, "L2")
            evac(PASS_L2)

            def message(c):
                c0, cw = CH[c]
                act.wait_ge(s_pe, PE[f"msg{c}"])
                step(f"msg{c}", nc.scalar.activation(gT[:, c0:c0 + cw], ps[:, 4 + TURN, 0:cw], ACT.Copy))

            message(0)
            for c in range(NCH + 4):
                if c + 1 < NCH:
                    message(c + 1)
                gru(STEPS, "L2", c)
                norm(2, c - 2)

            with act.Fori(0, TURNS) as i:
                for u in range(RING):
                    for hf in range(2):
                        g2 = (i * RING + u) * 2 + hf
                        act.wait_ge(a_tp, g2 + 1)
                        nc.scalar.activation(oht[:, u % 2, hf * 512:(hf + 1) * 512], ps[:, 4 + hf, :],
                                             ACT.Copy).then_inc(a_oht, 1)
            alT = ring_flat[:, 0:4096]
            for h in range(HEADS):
                act.wait_ge(s_dv, DV[f"sub{h}"])
                step(f"exp{h}", nc.scalar.activation(alT[:, h * 512:(h + 1) * 512], alT[:, h * 512:(h + 1) * 512],
                                                     ACT.Exp))
            for h in range(EX_DV, HEADS):
                act.wait_ge(s_pe, PE[f"exE{h}"])
                step(f"ex{h}", nc.scalar.activation(alE[:, 0:TILES, h], ps[:, h, 0:TILES], ACT.Copy))
            act.wait_ge(s_dv, DV["ex_done"])
            for j, sl in enumerate(HALVES):
                step(f"ex_a{j}", nc.scalar.activation(ex3[:, sl, 0, :], alE[:, sl, :], ACT.Copy))
            for j, (sl, rs3) in enumerate(zip(HALVES, RESTS)):
                act.wait_ge(s_dv, DV[f"ex_r{j}"])
                step(f"ex_b{j}", nc.scalar.activation(ex3[:, sl, 1, :], rs3, ACT.Copy))
            act.wait_ge(s_dv, DV["ex_c1"])
            with act.Fori(0, TURNS) as i:
                for u in range(RING):
                    act.wait_ge(b_oh, i * RING + (u + 1))
                    nc.scalar.activation(ex3w[:, u % 2, :, :], ex3f[:, ds((i * RING + u) * WV, WV), :], ACT.Copy)
                    nc.scalar.activation(ohb[:, u % 2, :, :], oh[:, u % 2, :, :], ACT.Copy).then_inc(b_ohb, 1)
            act.wait_ge(s_dv, DV["den3"])
            for c in (NCH - 2, NCH - 1, *range(NCH - 2)):
                c0, cw = CH[c]
                step(f"o{c}", nc.scalar.activation(gT[:, c0:c0 + cw], ps[:, c, 0:cw], ACT.Copy))

            def skip(c):
                cw, b = CH[c][1], c % 2
                act.wait_ge(f_x, c + 1)
                if c >= 2:
                    act.wait_ge(f_b, c - 1)
                    act.wait_ge(f_df, c - 1)
                nc.scalar.activation(wk[:, 0, b, 0:cw], ps[:, b, 0:cw], ACT.Identity,
                                     bias=b_("L3_bskip")).then_inc(f_xs, 1)

            skip(0)
            for c in range(NCH):
                if c + 1 < NCH:
                    skip(c + 1)
                cw, b = CH[c][1], c % 2
                act.wait_ge(f_b, c + 1)
                if c >= 2:
                    act.wait_ge(f_at, c - 1)
                nc.scalar.activation(wk[:, 3, b, 0:cw], ps[:, 2 + b, 0:cw], ACT.Sigmoid).then_inc(f_sg, 1)
            act.wait_ge(s_dv, DV["gn_var"])
            step("gn_sqrt", nc.scalar.activation(small[:, 2:3], small[:, 1:2], ACT.Sqrt, bias=b_("eps")))
            act.wait_ge(s_dv, DV["gn_shift"])
            for c, (c0, cw) in enumerate(CH):
                step(f"gn{c}", nc.scalar.activation(hT[:, c0:c0 + cw], hT[:, c0:c0 + cw], ACT.Identity,
                                                    bias=small[:, 5:6], scale=small[:, 4:5]))
            for c in range(NCH + 4):
                for j in range(4 if c < NCH else 0):
                    cw = CH[c][1]
                    act.wait_ge(s_pe, PE[f"ff{c}_{j}"])
                    if c >= 1:
                        act.wait_ge(s_pe, PE[f"ffo{c - 1}_{j}"])
                    step(f"gelu{c}_{j}", nc.scalar.activation(wk[:, j // 2, j % 2, 0:cw], ps[:, (4 * c + j) % 3, 0:cw],
                                                              ACT.Gelu, bias=b_(f"L3_b1_{j}")))
                norm(3, c - 1)

        @block.vector
        def _(dve):
            V = nc.vector
            n_dv = [0]

            def step(name, ins):
                n_dv[0] += 1
                seen["DV"].append(name)
                ins.then_inc(s_dv, 1)

            def after(name):
                dve.wait_ge(s_dv, DV[name])

            start = ((credit, RING), (b_used, RING), (s_gate, 1), (l1_msg, 1), (a_v, 1), (a_q, 1),
                     (a_prod, 1), (a_out, 1), (a_st[0], 16), (a_st[1], 16))
            for j, (s_, v_) in enumerate(start):
                V.memset(idx4[:, j * 44:(j + 1) * 44], 0).then_inc(s_, v_)
            step("z_idx1", V.memset(idx1[:, :], 0))
            step("z_dl", V.memset(dl[:, :], -1.0))
            step("z_row", V.memset(zrow[:, :], 0.0))
            step("z_cols", V.memset(cols[:, :], 0))
            step("z_recT", V.memset(recT[:, WAVES * P:(WAVES + 1) * P], 0.0))
            step("z_base", V.memset(basef[:, :], FAR))
            dve.wait_ge(s_edge, 80)
            R = rec[:, 0:TILES, :]
            far = nodes[:, 2, 0:TILES]
            step("f_gt", V.tensor_tensor(far, raw_i[:, 0, :], next_i, ALU.is_gt))
            after("f_gt")
            step("f_sum", V.tensor_reduce(small[:, 639:640], far, AX.X, ALU.add))
            for n, (i, f) in enumerate(((0, F_DST), (1, F_SRC), (2, F_T4))):
                step(f"r_i{n}", V.tensor_copy(R[:, :, f], raw_i[:, i, :]))
            step("r_t9", V.tensor_scalar(R[:, :, F_T9], raw_i[:, 3, :], 0, 8, ALU.max, ALU.min))
            dve.wait_ge(s_c, NFIRST)
            dve.wait_ge(s_pe, PE["flag"])
            step("flag", V.tensor_scalar(flag[:, :], ps[0:1, 3, 0:1], 1.0, None, ALU.min))
            after("flag")
            unsorted = dve.value_load(flag[0:1, 0:1], min_val=0, max_val=1)
            with dve.If(unsorted > 0):
                dve.wait_ge(s_ac, AC["r_a10"])
                n_srt = [0]

                def then(ins):
                    n_srt[0] += 1
                    ins.then_inc(srt_d, 1)
                    dve.wait_ge(srt_d, n_srt[0])

                then(V.memset(one_s, 1.0))
                then(V.memset(rank, 0.0))
                then(V.tensor_tensor_scan(tile_no, one_s, rank, 0.0, ALU.add, ALU.add))
                then(V.memset(key, 4.0e6))
                then(V.scalar_tensor_tensor(key[:, 0:TILES], R[:, :, F_DST], 512.0, tile_no[:, 0:TILES],
                                            ALU.mult, ALU.add))
                then(V.tensor_tensor(tri, ident, iota, ALU.mult))
                then(V.tensor_reduce(tie[:, 0:1], tri, AX.X, ALU.add))
                then(V.tensor_tensor(tri, iota, tie[:, 0:1].to_broadcast([P, P]), ALU.is_lt))
                cmp_ = nodes[:, 2:4, :].rearrange("p a b -> p (a b)")[:, 0:SORT_G * 2 * P].rearrange(
                    "p (t e) -> p t e", t=SORT_G)
                c2 = nodes[:, 2, 0:2 * P].rearrange("p (v e) -> p v e", e=P)
                rows = ps[:, 0, 0:2 * P]
                NG = SORT_N + 1
                with dve.Fori(0, SORT_TILES // 2) as c:
                    V.tensor_scalar(turn_in, key[:, ds(c * 2, 2)].unsqueeze(2).to_broadcast([P, 2, P]), 0.0, None,
                                    ALU.add).then_inc(srt_in, 1)
                    dve.wait_ge(srt_row, c + 1)
                    for g in range(SORT_N):
                        gs = slice(g * SORT_G, (g + 1) * SORT_G)
                        V.tensor_tensor(cmp_, rows.unsqueeze(1).to_broadcast([P, SORT_G, 2 * P]),
                                        key[:, gs].unsqueeze(2).to_broadcast([P, SORT_G, 2 * P]),
                                        ALU.is_lt).then_inc(srt_cmp, 1)
                        dve.wait_ge(srt_cmp, c * (NG + 1) + (g + 1))
                        V.tensor_reduce(part[:, gs], cmp_, AX.X, ALU.add).then_inc(srt_red, 1)
                        dve.wait_ge(srt_red, c * NG + (g + 1))
                    V.tensor_tensor(rank[:, 0:TILES], rank[:, 0:TILES], part[:, 0:TILES], ALU.add).then_inc(srt_acc, 1)
                    V.tensor_tensor(c2, rows.rearrange("p (v e) -> p v e", e=P),
                                    key[:, ds(c * 2, 2)].unsqueeze(2).to_broadcast([P, 2, P]),
                                    ALU.is_equal).then_inc(srt_cmp, 1)
                    dve.wait_ge(srt_cmp, c * (NG + 1) + NG)
                    V.tensor_tensor(c2, c2, tri.unsqueeze(1).to_broadcast([P, 2, P]), ALU.mult).then_inc(srt_cmp, 1)
                    dve.wait_ge(srt_cmp, c * (NG + 1) + (NG + 1))
                    V.tensor_reduce(tie, c2, AX.X, ALU.add).then_inc(srt_red, 1)
                    dve.wait_ge(srt_red, c * NG + NG)
                    dve.wait_ge(srt_acc, c * 2 + 1)
                    V.tensor_tensor(rank[:, ds(c * 2, 2)], rank[:, ds(c * 2, 2)], tie, ALU.add).then_inc(srt_acc, 1)
                    dve.wait_ge(srt_acc, c * 2 + 2)
                then(V.tensor_copy(rank_i, rank[:, 0:TILES]))
                with dve.Fori(0, SORT_N) as c:
                    V.tensor_scalar(sc_rec, rec[:, ds(c * SORT_G, SORT_G), :], 0.0, None, ALU.add).then_inc(srt_st, 1)
                    V.tensor_scalar(sc_idx, rank_i[:, ds(c * SORT_G, SORT_G)], 0.0, None, ALU.add).then_inc(srt_st, 1)
                    dve.wait_ge(srt_sc, (c + 1) * (16 * SORT_G))
                dve.wait_ge(srt_ld, 16 * SORT_N)
            step("w_dst", V.tensor_copy(raw_i[0:1, 0, :], rec[0:1, 0:TILES, F_DST]))
            after("w_dst")
            step("w_col", V.tensor_scalar(cols[0:1, 0:TILES], raw_i[0:1, 0, :], 7, 7, ALU.arith_shift_right,
                                          ALU.logical_shift_left))
            th = small[:, 32:32 + EXTRA]
            step("w_th", V.tensor_scalar(th, iota[:, 1:1 + EXTRA], float(P), None, ALU.mult))
            dve.wait_ge(s_pe, PE["fd"])
            cmp = nodes[:, 2, 0:TILES]
            step("w_cmp", V.tensor_tensor(cmp, ps[:, 1, 0:TILES], b_("window_end").to_broadcast([P, TILES]), ALU.is_lt))
            after("w_cmp")
            step("w_cnt", V.tensor_reduce(small[:, 0:1], cmp, AX.X, ALU.add))
            dve.wait_ge(s_pe, PE["off"])
            offs = small[0:1, 64:64 + EXTRA]
            step("w_off", V.tensor_scalar(small[0:1, 96:96 + EXTRA], ps[0:1, 2, 0:EXTRA], -1.0, 0.0, ALU.add, ALU.max))
            step("w_inv", V.tensor_scalar(offs, ps[0:1, 2, 0:EXTRA], 0.0, FAR, ALU.is_equal, ALU.mult))
            after("w_inv")
            step("w_tix", V.tensor_copy(tix[0:1, 0:EXTRA], small[0:1, 96:96 + EXTRA]))
            step("w_colx", V.tensor_copy(cols[0:1, TILES:TILES + EXTRA], small[0:1, 32:32 + EXTRA]))
            after("w_colx")
            step("w_b0", V.tensor_copy(basef[0:1, 0:TILES], cols[0:1, 0:TILES]))
            step("w_bx", V.tensor_tensor(basef[0:1, TILES:TILES + EXTRA], offs, small[0:1, 32:32 + EXTRA], ALU.add))
            step("w_c16", V.tensor_scalar(cols16[:, :], cols[:, :], 3, None, ALU.arith_shift_right))
            step("w_c8", V.tensor_scalar(cols24[:, :], cols[:, :], 4, None, ALU.arith_shift_right))
            after("w_c8")
            step("w_c24", V.tensor_scalar(cols24[:, :], cols24[:, :], 3, NP, ALU.mult, ALU.add))
            dve.wait_ge(s_ac, AC["r_a10"])
            with dve.Fori(0, EXTRA // WV) as i:
                t = load_tiles(dve, tix, i)
                for j in range(WV):
                    V.tensor_scalar(rec[:, ds(i * WV + (TILES + j), 1), :], rec[:, ds(t[j], 1), :], 0.0, None, ALU.add)
            step("x_last", V.tensor_copy(rec[:, TILES + EXTRA:SLOTS, :], rec[:, 0:SLOTS - TILES - EXTRA, :]))
            after("x_last")
            step("i_4", V.scalar_tensor_tensor(idx4[:, 0:SLOTS], rec[:, :, F_SRC], float(ET), rec[:, :, F_T4],
                                               ALU.mult, ALU.add))
            step("i_1", V.tensor_copy(idx1[:, 0:SLOTS], rec[:, :, F_SRC]))
            step("i_t9", V.tensor_copy(t9b[:, :], rec[:, :, F_T9]))
            dve.wait_ge(s_pe, PE["base"])
            step("i_dl", V.tensor_tensor(dl[:, 0:SLOTS], rec[:, :, F_DST], ps[:, 1, 0:SLOTS], ALU.subtract))
            after("i_dl")
            step("i_dlb", V.tensor_copy(dlb[:, :], dl[:, 0:SLOTS]))
            step("i_iob", V.tensor_copy(iotab[:, :], iota))
            for L, j in (("L0", 0), ("L2", 2)):
                for g, n in enumerate(("r", "z")):
                    step(f"{L}_b{n}", V.tensor_tensor(b_(f"{L}_b{n}"), b_(f"{L}_bih_{n}"), b_(f"{L}_bhh_{n}"), ALU.add))

            def stage(k, i, u, idx):
                g3 = wave_no(k, i, u) + AHEAD
                dve.wait_ge(credit, g3 + 1)
                V.tensor_scalar(ixr[:, (u + AHEAD) % RING, :], idx[:, ds((i * RING + (u + AHEAD)) * WV, WV)], 0.0, None,
                                ALU.add).then_inc(ix_ready, 1)

            def stage_first(k, idx):
                for u in range(AHEAD):
                    dve.wait_ge(credit, k * WAVES + u + 1)
                    V.tensor_scalar(ixr[:, u, :], idx[:, u * WV:(u + 1) * WV], 0.0, None, ALU.add).then_inc(ix_ready, 1)

            def one_hot(k, i, u, ahead=0):
                v = (u + ahead) % 2
                return V.tensor_tensor(oh[:, v, :, :], iota.unsqueeze(1).to_broadcast([P, WV, P]),
                                       dl[:, ds((i * RING + (u + ahead)) * WV, WV)].unsqueeze(2)
                                       .to_broadcast([P, WV, P]), ALU.is_equal)

            def sums(k, idx, counting=False):
                with dve.Fori(0, TURNS) as i:
                    for u in range(RING):
                        dve.wait_ge(credit, wave_no(k, i, u) + 3)
                        ins = one_hot(k, i, u)
                        if counting:
                            sl = ds((i * RING + u) * WV, WV)
                            V.tensor_tensor(t9oh[:, u % 2, :, :], iotab[:, 0:NT].unsqueeze(1).to_broadcast([P, WV, NT]),
                                            t9b[:, sl].unsqueeze(2).to_broadcast([P, WV, NT]), ALU.is_equal)
                            ins = V.tensor_tensor(ohb[:, u % 2, :, :],
                                                  iotab[:, :].unsqueeze(1).to_broadcast([P, WV, P]),
                                                  dlb[:, sl].unsqueeze(2).to_broadcast([P, WV, P]), ALU.is_equal)
                        ins.then_inc(oh_ready, 1)
                        stage(k, i, u, idx)

            def evac(k):
                dve.wait_ge(credit, (k + 1) * WAVES + RING)
                for c in range(0, NCH, 2):
                    c0, cw = CH[c]
                    V.tensor_copy(gT[:, c0:c0 + cw], ps[:, c, 0:cw]).then_inc(ev_d, 1)

            def table(t, n, width, bias, q_rows=None, buf=tb):
                b = n % RING
                dve.wait_ge(mt_mm, t * WIN + (n + 1) - FIRST_ACT)
                if n >= RING:
                    dve.wait_ge(mt_dma[b], t * (16 * MT_SLOTS[b]) + 16 * (n // RING))
                if q_rows is not None:
                    V.tensor_tensor(q_rows[:, n, :], ps[:, 4 + b, 0:D], bias[:, 0:D], ALU.add)
                    bs = bias[:, D:D + width]
                    src = ps[:, 4 + b, D:D + width]
                else:
                    bs, src = bias, ps[:, 4 + b, 0:width]
                V.tensor_tensor(buf[:, b, 0:width], src, bs, ALU.add).then_inc(mt_ev, 1)

            def windows(c):
                return range(CH[c][0] // P, (CH[c][0] + CH[c][1]) // P)

            def gru(r, L, c, h_in, h_out):
                if c < NCH:
                    (c0, cw), b, t = CH[c], c % 2, r * NCH + (c + 1)
                    for j, s_ in enumerate((gru_ar, gru_az)):
                        dve.wait_ge(gru_mm, r * (3 * NCH) + (3 * c + j + 1))
                        V.tensor_tensor(wk[:, j, b, 0:cw], ps[:, j, 0:cw], hid[L][j][:, c0:c0 + cw],
                                        ALU.add).then_inc(s_, 1)
                if 1 <= c <= NCH:
                    c0, cw = CH[c - 1]
                    b, t = (c - 1) % 2, r * NCH + c
                    hi, ho, n = h_in[:, c0:c0 + cw], h_out[:, c0:c0 + cw], wk[:, 3, b, 0:cw]
                    dve.wait_ge(gru_n, t)
                    V.tensor_tensor(wk[:, 4, b, 0:cw], hi, n, ALU.subtract).then_inc(gru_d, 1)
                    dve.wait_ge(gru_d, t)
                    V.tensor_tensor(wk[:, 4, b, 0:cw], wk[:, 4, b, 0:cw], wk[:, 1, b, 0:cw],
                                    ALU.mult).then_inc(gru_e, 1)
                    dve.wait_ge(gru_e, t)
                    V.tensor_tensor(ho, n, wk[:, 4, b, 0:cw], ALU.add).then_inc(gru_h, 1)
                if c < NCH:
                    cw, b, t = CH[c][1], c % 2, r * NCH + (c + 1)
                    dve.wait_ge(gru_r, t)
                    dve.wait_ge(gru_mm, t * 3)
                    V.scalar_tensor_tensor(wk[:, 2, b, 0:cw], ps[:, 3, 0:cw], b_(L + "_bhn"),
                                           wk[:, 0, b, 0:cw], ALU.add, ALU.mult).then_inc(gru_t, 1)
                    dve.wait_ge(gru_t, t)
                    V.tensor_tensor(wk[:, 2, b, 0:cw], wk[:, 2, b, 0:cw], ps[:, 2, 0:cw],
                                    ALU.add).then_inc(gru_p, 1)

            def norm(ln, c, make_y):
                n0 = NCH * ln
                if 0 <= c < NCH:
                    make_y(c)
                if 2 <= c < NCH + 2:
                    (c0, cw), b = CH[c - 2], c % 2
                    dve.wait_ge(ln_b, n0 + c - 1)
                    V.tensor_tensor(xT[:, c0:c0 + cw], yc[:, b, 0:cw], ps[:, bank(ln, SPREAD, c), 0:cw],
                                    ALU.mult).then_inc(ln_x, 1)
                if 0 <= c < NCH:
                    (c0, cw), b = CH[c], c % 2
                    dve.wait_ge(ln_m, n0 + c + 1)
                    if c >= 2:
                        dve.wait_ge(ln_q, n0 + c - 1)
                        dve.wait_ge(ln_x, n0 + c - 1)
                    V.tensor_tensor(yc[:, b, 0:cw], yT[:, c0:c0 + cw], ps[:, bank(ln, MEAN, c), 0:cw],
                                    ALU.subtract).then_inc(ln_c, 1)
                if 1 <= c <= NCH:
                    w0, nw = CH[c - 1][0] // P, CH[c - 1][1] // P
                    dve.wait_ge(ln_v, n0 + c)
                    V.tensor_scalar(sd[:, w0:w0 + nw], ps[:, bank(ln, VAR, c - 1), 0:nw], EPS, None,
                                    ALU.add).then_inc(ln_s, 1)

            for n in range(FIRST_ACT, WIN):
                table(0, n, 512, brow[:, 0:512], buf=tb0)
            stage_first(0, idx4)
            dT = pw[:, 0, :]
            LAST = TILES % P
            step("t_zd", V.memset(dT, -1.0))
            after("t_zd")
            dve.wait_ge(s_pe, PE["dT"])
            step("t_d0", V.tensor_copy(dT[:, 0:384], ps[:, 4, 0:384]))
            step("t_d1", V.tensor_copy(dT[0:LAST, 384:512], ps[0:LAST, 4, 384:512]))
            after("t_d1")
            dv, ff, fb = (x.rearrange("p (b e) -> p b e", e=P) for x in (dT, fF, fB))
            dve.wait_ge(s_pe, PE[f"recT{WAVES // 4 - 1}"])
            step("t_f0", V.memset(rec_flat[:, 5376:6400], -BIG))
            after("t_f0")
            step("t_f1", V.tensor_tensor(ff[:, :, 1:P], dv[:, :, 1:P], dv[:, :, 0:P - 1], ALU.not_equal))
            step("t_f2", V.tensor_tensor(fb[:, :, 0:P - 1], dv[:, :, 1:P], dv[:, :, 0:P - 1], ALU.not_equal))
            after("t_f2")
            step("t_f3", V.tensor_scalar(ff[:, :, 1:P], ff[:, :, 1:P], -BIG, None, ALU.mult))
            step("t_f4", V.tensor_scalar(fb[:, :, 0:P - 1], fb[:, :, 0:P - 1], -BIG, None, ALU.mult))
            edge = small[:, 384:384 + 64].rearrange("p (w b h) -> p w b h", w=2, b=4)
            step("t_e0", V.tensor_copy(edge[:, 0, :, :], dv[:, :, 0:1].to_broadcast([P, 4, HEADS])))
            step("t_e1", V.tensor_copy(edge[:, 1, :, :], dv[:, :, P - 1:P].to_broadcast([P, 4, HEADS])))
            for b in range(RING):
                dve.wait_ge(mt_dma[b], 16 * MT_SLOTS[b])
            with dve.Fori(0, STEPS - 1) as s:
                sums(s, idx4)
                evac(s)
                for c in range(NCH + 2):
                    gru(s, "L0", c, hT, hT)
                    if c >= 2:
                        for n in windows(c - 2):
                            table(s + 1, n, 512, brow[:, 0:512])
                stage_first(s + 1, idx4)
            after("t_e1")
            sums(STEPS - 1, idx4, counting=True)
            evac(STEPS - 1)

            def y_sum(c):
                c0, cw = CH[c]
                V.tensor_tensor(yT[:, c0:c0 + cw], xT[:, c0:c0 + cw], hT[:, c0:c0 + cw], ALU.add).then_inc(ln_y, 1)

            def update_norm(r, L, ln, h_in):
                for c in range(NCH + 4):
                    if 2 <= c < NCH + 2:
                        dve.wait_ge(gru_h, r * NCH + c - 1)
                        y_sum(c - 2)
                    gru(r, L, c, h_in, hT)
                    norm(ln, c - 2, lambda c: None)

            update_norm(STEPS - 1, "L0", 0, hT)

            stage_first(PASS_L1, idx1)
            dve.wait_ge(s_ac, AC["counts"])
            step("n_cnt", V.tensor_reduce(cntc, counts, AX.X, ALU.add))
            after("n_cnt")
            step("n_max", V.tensor_scalar(cntc, cntc, 1.0, None, ALU.max))
            after("n_max")
            step("n_inv", V.reciprocal(inv, cntc))
            V.tensor_scalar(rts[:, 0, :], recT[:, 0:P], 0.0, None, ALU.add)
            V.tensor_tensor(oh[:, 0, :, :], iota.unsqueeze(1).to_broadcast([P, WV, P]),
                            dl[:, 0:WV].unsqueeze(2).to_broadcast([P, WV, P]), ALU.is_equal).then_inc(oh_ready, 1)
            with dve.Fori(0, TURNS) as i:
                for u in range(RING):
                    for hf in range(2):
                        if hf:
                            dve.wait_ge(credit, wave_no(PASS_L1, i, u) + RING)
                            V.tensor_scalar(rts[:, (u + 1) % 2, :], recT[:, ds((i * RING + (u + 1)) * P, P)], 0.0,
                                            None, ALU.add)
                            one_hot(PASS_L1, i, u, ahead=1).then_inc(oh_ready, 1)
                            stage(PASS_L1, i, u, idx1)
                        dve.wait_ge(gat[u], (PASS_L1 * TURNS + i + 1) * (16 * WV))
                        dve.wait_ge(l1_pe, (i * RING + u) * 2 + (hf + 1))
                        xj = ring[:, u, 4 * hf:4 * hf + 4, 0:D]
                        V.scalar_tensor_tensor(xj, ps[:, 7, :].rearrange("p (s d) -> p s d", d=D), 1.0, xj,
                                               ALU.add, ALU.mult).then_inc(l1_msg, 1)
            evac(PASS_L1)
            for c, (c0, cw) in enumerate(CH):
                dve.wait_ge(s_pe, PE[f"cnt{c}"])
                if c == 1:
                    dve.wait_ge(ev_a, (PASS_L1 + 1) * EV_A)
                step(f"ag{c}", V.tensor_tensor(gT[:, c0:c0 + cw], gT[:, c0:c0 + cw], ps[:, c % 2, 0:cw], ALU.mult))

            def stats(T, ready, name):
                for c, (c0, cw) in enumerate(CH):
                    ready(c)
                    step(f"{name}s{c}", V.bn_stats(small[:, 128 + 6 * c:134 + 6 * c], T[:, c0:min(c0 + cw, N)]))
                after(f"{name}s{NCH - 1}")
                step(f"{name}_agg", V.bn_aggr(small[:, 0:2], small[:, 128:128 + 6 * NCH]))
                after(f"{name}_agg")

            stats(yT, lambda c: dve.wait_ge(s_ac, AC[f"sage{c}"]), "bn")
            dve.wait_ge(s_ac, AC["bn_sqrt"])
            step("bn_rs", V.reciprocal(small[:, 3:4], small[:, 2:3]))
            after("bn_rs")
            step("bn_scale", V.tensor_tensor(small[:, 4:5], small[:, 3:4], b_("L1_gamma"), ALU.mult))
            after("bn_scale")
            step("bn_ms", V.tensor_tensor(small[:, 7:8], small[:, 4:5], small[:, 0:1], ALU.mult))
            after("bn_ms")
            step("bn_shift", V.tensor_tensor(small[:, 5:6], b_("L1_beta"), small[:, 7:8], ALU.subtract))

            def y_l1(c):
                c0, cw = CH[c]
                dve.wait_ge(x_step, c + 1)
                V.scalar_tensor_tensor(yT[:, c0:c0 + cw], xT[:, c0:c0 + cw], 2.0, yT[:, c0:c0 + cw],
                                       ALU.mult, ALU.add).then_inc(ln_y, 1)

            for c in range(NCH + 2):
                norm(1, c, y_l1)

            stage_first(PASS_L2, idx1)
            dve.wait_ge(s_w, NLOADS)
            step("emb", V.tensor_tensor(w("L2_emb", rows=9), w("L2_emb", rows=9), w("L2_bmsg9", rows=9), ALU.add))
            dve.wait_ge(oh_ready, (PASS_L1 + 1) * WAVES + 1)
            sums(PASS_L2, idx1)
            evac(PASS_L2)
            update_norm(STEPS, "L2", 2, xT)

            q_rows = hT.rearrange("p (n d) -> p n d", d=D)
            dve.wait_ge(ln_x, 3 * NCH)
            for n in range(WIN):
                table(STEPS, n, 2 * D, brow[:, 512:512 + 3 * D], q_rows)
            stage_first(PASS_L3, idx1)
            V.tensor_scalar(rts[:, 0, :], recT[:, 0:P], 0.0, None, ALU.add)
            V.tensor_tensor(oh[:, 0, :, :], iota.unsqueeze(1).to_broadcast([P, WV, P]),
                            dl[:, 0:WV].unsqueeze(2).to_broadcast([P, WV, P]), ALU.is_equal).then_inc(oh_ready, 1)
            ve = pw[:, :, :].rearrange("p (b c) d -> p b (c d)", b=2)
            red = small[:, 256:256 + 128].rearrange("p (b s) -> p b s", b=2)
            with dve.Fori(0, TURNS) as i:
                for u in range(RING):
                    g2 = (i * RING + u) * 2
                    v = u % 2
                    dve.wait_ge(a_q, g2 + 1)
                    w1 = (u + 1) % 2
                    V.tensor_scalar(rts[:, w1, :], recT[:, ds((i * RING + (u + 1)) * P, P)], 0.0, None, ALU.add)
                    one_hot(PASS_L3, i, u, ahead=1).then_inc(oh_ready, 1)
                    stage(PASS_L3, i, u, idx1)
                    dve.wait_ge(gat[u], (PASS_L3 * TURNS + i + 1) * (16 * WV))
                    dve.wait_ge(a_st[v], (i * 2 + (u // 2 + 1)) * 16)
                    for hf in range(2):
                        hs = slice(512 * hf, 512 * hf + 512)
                        dve.wait_ge(a_e, g2 + (hf + 1))
                        pe_ = ps[:, hf, :].rearrange("p (s d) -> p s d", d=D)
                        kj = ring[:, u, 4 * hf:4 * hf + 4, 0:D]
                        V.tensor_tensor(kj, kj, pe_, ALU.add).then_inc(a_kv, 1)
                        V.tensor_tensor(ve[:, v, hs].rearrange("p (s d) -> p s d", d=D),
                                        ring[:, u, 4 * hf:4 * hf + 4, D:2 * D], pe_, ALU.add).then_inc(a_v, 1)
                    for hf in range(2):
                        dve.wait_ge(a_kv, g2 + (hf + 1))
                        dve.wait_ge(a_q, g2 + (hf + 2))
                        kj = ring[:, u, 4 * hf:4 * hf + 4, 0:D]
                        V.tensor_tensor(kj, kj, ps[:, 2 + hf, :].rearrange("p (s d) -> p s d", d=D),
                                        ALU.mult).then_inc(a_prod, 1)
                    dve.wait_ge(a_prod, g2 + 3)
                    V.tensor_reduce(red[:, v, :].rearrange("p (s h) -> p s h", h=HEADS),
                                    ring[:, u, :, 0:D].rearrange("p s (h c) -> p s h c", c=HC), AX.X,
                                    ALU.add).then_inc(a_red, 1)
                    dve.wait_ge(a_red, i * RING + (u + 1))
                    dve.wait_ge(a_v, g2 + 3)
                    V.tensor_scalar(alE[:, ds((i * RING + u) * WV, WV), :],
                                    red[:, v, :].rearrange("p (s h) -> p s h", h=HEADS), 1.0 / HC ** 0.5, None,
                                    ALU.mult).then_inc(credit, 1)
            dve.wait_ge(credit, (PASS_L3 + 1) * WAVES + RING)
            for j, op in enumerate((ALU.add, ALU.subtract)):
                step(f"wb{j}", V.tensor_tensor(wbeta[:, j, :], b_(f"L3_wbeta{j}").to_broadcast([P, P]),
                                               b_("L3_wbeta2").to_broadcast([P, P]), op))
            with dve.Fori(0, EXTRA // WV) as i:
                t = load_tiles(dve, tix, i)
                for j in range(WV):
                    dve.wait_ge(a_out, i * WV + (j + 1))
                    V.tensor_tensor(alE[:, ds(t[j], 1), :], alE[:, ds(t[j], 1), :],
                                    alE[:, ds(i * WV + (TILES + j), 1), :], ALU.add).then_inc(a_out, 1)
            dve.wait_ge(a_out, EXTRA + 1)
            alT = ring_flat[:, 0:4096].rearrange("p (h c) -> p h c", h=HEADS)
            fwd = ring_flat[:, 4096:8192].rearrange("p (h c) -> p h c", h=HEADS)
            bwd = nodes[:, 2:4, :].rearrange("p a b -> p (a b)")[:, 0:4096].rearrange("p (h c) -> p h c", h=HEADS)
            step("t_z", V.memset(alT[:, :, 384:512], 0.0))
            after("t_z")
            for h in range(HEADS):
                dve.wait_ge(s_pe, PE[f"alT{h}"])
                step(f"t_a{h}", V.tensor_copy(alT[:, h, 0:384], ps[:, h, 0:384]))
                step(f"t_b{h}", V.tensor_copy(alT[0:LAST, h, 384:512], ps[0:LAST, h, 384:512]))
                after(f"t_b{h}")
                step(f"t_s{h}", V.tensor_tensor_scan(fwd[:, h, :], fF, alT[:, h, :], -BIG, ALU.add, ALU.max))
                step(f"t_r{h}", V.tensor_tensor_scan(bwd[:, h, ::-1], fB[:, ::-1], alT[:, h, ::-1], -BIG, ALU.add,
                                                     ALU.max))
            after(f"t_r{HEADS - 1}")
            ht = small[:, 448:448 + 64].rearrange("p (w b h) -> p w b h", w=2, b=4)
            step("t_h0", V.tensor_copy(ht[:, 0, :, :], bwd.rearrange("p h (b e) -> p b h e", e=P)[:, :, :, 0]))
            step("t_h1", V.tensor_copy(ht[:, 1, :, :], fwd.rearrange("p h (b e) -> p b h e", e=P)[:, :, :, P - 1]))
            n1 = slice(1, 512)
            n0 = slice(0, 511)
            for b in range(2):
                dve.wait_ge(a_st[b], 16 * (WAVES // 2 + 1))
            for j in range(4, 12):
                step(f"c_i{j}", V.memset(L8[j], -BIG))
            dve.wait_ge(s_pe, PE["line"])
            for j in range(4):
                step(f"t_l{j}", V.tensor_copy(L8[j], ps[0:HEADS, 1 + j, :]))
            after("t_l3")
            step("c_1", V.tensor_tensor(conn[:, n1], fd[:, n1], ld[:, n0], ALU.is_equal))
            step("c_2", V.tensor_tensor(full, fd, ld, ALU.is_equal))
            after("c_2")
            step("c_3", V.tensor_tensor(A[:, n1], conn[:, n1], full[:, n0], ALU.mult))
            step("c_4", V.tensor_tensor(B[:, n1], conn[:, n1], full[:, n1], ALU.mult))
            after("c_4")
            for j, x in enumerate((A, B, conn)):
                step(f"c_5{j}", V.tensor_scalar(x[:, n1], x[:, n1], -1.0, BIG, ALU.add, ALU.mult))
            after("c_52")
            step("c_6", V.tensor_tensor(Dd[:, n1], tl[:, n0], conn[:, n1], ALU.add))
            step("c_7", V.tensor_tensor(De[:, n1], hd[:, n1], conn[:, n1], ALU.add))
            after("c_7")
            step("c_8", V.tensor_tensor_scan(cf[:, n1], A[:, n1], Dd[:, n1], -BIG, ALU.add, ALU.max))
            step("c_9", V.tensor_tensor_scan(cb[:, 510::-1], B[:, 511:0:-1], De[:, 511:0:-1], -BIG, ALU.add, ALU.max))
            dve.wait_ge(s_pe, PE["carry"])
            keep = small[:, 512:512 + 64].rearrange("p (w h b) -> p w h b", w=2, b=4)
            al4 = alT.rearrange("p h (b e) -> p h b e", e=P)
            crr = ps[:, 5, 0:64].rearrange("p (w b h) -> p w h b", w=2, b=4)
            for j, e in enumerate((0, P - 1)):
                step(f"k_{j}", V.tensor_copy(keep[:, j, :, :], al4[:, :, :, e]))
            after("k_1")
            for j, e in enumerate((0, P - 1)):
                step(f"k_m{j}", V.tensor_tensor(al4[:, :, :, e], keep[:, j, :, :], crr[:, j, :, :], ALU.max))
            after("k_m1")
            for h in range(HEADS):
                step(f"u_s{h}", V.tensor_tensor_scan(fwd[:, h, :], fF, alT[:, h, :], -BIG, ALU.add, ALU.max))
                step(f"u_r{h}", V.tensor_tensor_scan(bwd[:, h, ::-1], fB[:, ::-1], alT[:, h, ::-1], -BIG, ALU.add,
                                                     ALU.max))
            after(f"u_r{HEADS - 1}")
            for j, e in enumerate((0, P - 1)):
                step(f"k_b{j}", V.tensor_copy(al4[:, :, :, e], keep[:, j, :, :]))
            for h in range(HEADS):
                step(f"mx_{h}", V.tensor_tensor(fwd[:, h, :], fwd[:, h, :], bwd[:, h, :], ALU.max))
            after(f"mx_{HEADS - 1}")
            for h in range(HEADS):
                step(f"sub{h}", V.tensor_tensor(alT[:, h, :], alT[:, h, :], fwd[:, h, :], ALU.subtract))
            for h in range(EX_DV):
                dve.wait_ge(s_pe, PE[f"exE{h}"])
                step(f"ex{h}", V.tensor_copy(alE[:, 0:TILES, h], ps[:, h, 0:TILES]))
            after(f"ex{EX_DV - 1}")
            dve.wait_ge(s_ac, AC[f"ex{HEADS - 1}"])
            with dve.Fori(0, EXTRA // WV) as i:
                t = load_tiles(dve, tix, i)
                for j in range(WV):
                    V.tensor_scalar(alE[:, ds(i * WV + (TILES + j), 1), :], alE[:, ds(t[j], 1), :], 0.0, None, ALU.add)
            step("ex_done", V.tensor_copy(alE[:, TILES + EXTRA:SLOTS, :], alE[:, 0:SLOTS - TILES - EXTRA, :]))
            after("ex_done")
            for j, (sl, rs3) in enumerate(zip(HALVES, RESTS)):
                dve.wait_ge(s_ac, AC[f"ex_a{j}"])
                step(f"ex_r{j}", V.tensor_tensor(rs3, alE[:, sl, :], ex3[:, sl, 0, :], ALU.subtract))
            for j, (sl, rs3) in enumerate(zip(HALVES, RESTS)):
                dve.wait_ge(s_ac, AC[f"ex_b{j}"])
                step(f"ex_c{j}", V.tensor_tensor(ex3[:, sl, 2, :], rs3, ex3[:, sl, 1, :], ALU.subtract))
            with dve.Fori(0, TURNS) as i:
                for u in range(RING):
                    g = i * RING + u
                    sl = ds(g * WV, WV)
                    dve.wait_ge(b_used, g + (RING - 1))
                    one_hot(PASS_L3, i, u).then_inc(b_oh, 1)
                    dve.wait_ge(b_ld[u], (i + 1) * 16)
                    vv = ring[:, u, 0:WV // 2, :].rearrange("p a (s c) -> p (a s) c", c=HC)
                    V.tensor_tensor(vv, vv, alE[:, sl, :].rearrange("p s h -> p (s h)").unsqueeze(2)
                                    .to_broadcast([P, WV * HEADS, HC]), ALU.mult).then_inc(b_ready, 1)

            dve.wait_ge(b_used, WAVES + RING)
            parts = psf[:, NP:NP + WIN * 24].rearrange("p (w k h) -> p w h k", k=3, h=HEADS)
            step("den3", V.tensor_reduce(den.rearrange("p (w h) -> p w h", h=HEADS), parts, AX.X, ALU.add))
            after("den3")
            step("den", V.tensor_scalar(den, den, 1e-16, None, ALU.add))
            after("den")
            step("rden", V.reciprocal(rden, den))
            after("rden")
            for c, (c0, cw) in enumerate(CH):
                step(f"rx{c}", V.tensor_scalar(rdenx[:, c0:c0 + cw].rearrange("p (h c) -> p h c", c=HC),
                                               rden[:, c0 // HC:(c0 + cw) // HC].unsqueeze(2)
                                               .to_broadcast([P, cw // HC, HC]), 0.0, None, ALU.add))
            for c, (c0, cw) in enumerate(CH):
                dve.wait_ge(s_pe, PE[f"sp{c}"])
                o = gT[:, c0:c0 + cw]
                dve.wait_ge(s_ac, AC[f"o{c}"])
                step(f"n{c}", V.tensor_tensor(o, o, ps[:, SPREADS[c % 3], 0:cw], ALU.mult))
            after(f"n{NCH - 1}")
            for c in range(NCH + 1):
                if c < NCH:
                    (c0, cw), b = CH[c], c % 2
                    dve.wait_ge(f_xs, c + 1)
                    if c >= 2:
                        dve.wait_ge(f_at, c - 1)
                    V.tensor_tensor(wk[:, 1, b, 0:cw], gT[:, c0:c0 + cw], wk[:, 0, b, 0:cw],
                                    ALU.subtract).then_inc(f_df, 1)
                if c >= 1:
                    (c0, cw), b = CH[c - 1], (c - 1) % 2
                    dve.wait_ge(f_sg, c)
                    dve.wait_ge(f_df, c)
                    if c >= 3:
                        dve.wait_ge(f_h, c - 2)
                    V.tensor_tensor(wk[:, 2, b, 0:cw], wk[:, 1, b, 0:cw], wk[:, 3, b, 0:cw], ALU.mult).then_inc(f_at, 1)
                    dve.wait_ge(f_at, c)
                    V.tensor_tensor(wk[:, 2, b, 0:cw], gT[:, c0:c0 + cw], wk[:, 2, b, 0:cw],
                                    ALU.subtract).then_inc(f_xa, 1)
                    dve.wait_ge(f_xa, c)
                    V.tensor_tensor(hT[:, c0:c0 + cw], xT[:, c0:c0 + cw], wk[:, 2, b, 0:cw], ALU.add).then_inc(f_h, 1)
            dve.wait_ge(f_h, NCH)
            stats(hT, lambda c: None, "gn")
            step("gn_m", V.tensor_tensor(small[:, 6:7], small[:, 0:1], b_("L3_gn_ms"), ALU.mult))
            after("gn_m")
            step("gn_d", V.tensor_tensor(small[:, 7:8], small[:, 0:1], small[:, 6:7], ALU.subtract))
            after("gn_d")
            step("gn_d2", V.tensor_tensor(small[:, 7:8], small[:, 7:8], small[:, 7:8], ALU.mult))
            after("gn_d2")
            step("gn_var", V.tensor_tensor(small[:, 1:2], small[:, 1:2], small[:, 7:8], ALU.add))
            dve.wait_ge(s_ac, AC["gn_sqrt"])
            step("gn_rs", V.reciprocal(small[:, 3:4], small[:, 2:3]))
            after("gn_rs")
            step("gn_scale", V.tensor_tensor(small[:, 4:5], small[:, 3:4], b_("L3_gn_w"), ALU.mult))
            after("gn_scale")
            step("gn_ms", V.tensor_tensor(small[:, 7:8], small[:, 4:5], small[:, 6:7], ALU.mult))
            after("gn_ms")
            step("gn_shift", V.tensor_tensor(small[:, 5:6], b_("L3_gn_b"), small[:, 7:8], ALU.subtract))
            for c in range(NCH + 3):
                norm(3, c - 1, lambda c: None)
                if c < NCH:
                    c0, cw = CH[c]
                    dve.wait_ge(s_pe, PE[f"ffo{c}_3"])
                    step(f"y{c}", V.scalar_tensor_tensor(yT[:, c0:c0 + cw], ps[:, 3, 0:cw], b_("L3_b2"),
                                                         hT[:, c0:c0 + cw], ALU.add, ALU.add))
                    after(f"y{c}")
                    V.tensor_tensor(yT[:, c0:c0 + cw], yT[:, c0:c0 + cw], xT[:, c0:c0 + cw], ALU.add).then_inc(ln_y, 1)


        @block.tensor
        def _(pe):
            T = nc.tensor
            n_pe = [0]

            def step(name, ins):
                n_pe[0] += 1
                seen["PE"].append(name)
                ins.then_inc(s_pe, 1)

            def mm(o, lhsT, rhs, start=True, stop=True):
                return T.matmul(o, lhsT, rhs, start=start, stop=stop, skip_group_check=True)

            def zero(banks):
                for b in banks:
                    mm(ps[:, b, :], zrow[0:1, 0:P], zrow[0:1, :], stop=False)

            pe.wait_ge(s_c, 16)
            pe.wait_ge(s_dv, DV["f_sum"])
            step("flag", mm(ps[:, 3, 0:1], ones, small[:, 639:640]))
            pe.wait_ge(s_dv, DV["flag"])
            unsorted = pe.value_load(flag[0:1, 0:1], min_val=0, max_val=1)
            with pe.If(unsorted > 0):
                with pe.Fori(0, SORT_TILES // 2) as c:
                    pe.wait_ge(srt_in, c + 1)
                    for v_ in range(2):
                        ins = T.transpose(ps[:, 0, v_ * P:(v_ + 1) * P], turn_in[:, v_, :], ident)
                    ins.then_inc(srt_row, 1)

            def table(t, n, h, wts, width):
                if n >= RING:
                    pe.wait_ge(mt_ev, t * WIN + (n - RING + 1) - FIRST_ACT)
                mm(ps[:, 4 + n % RING, 0:width], h[:, n * P:(n + 1) * P], wts).then_inc(mt_mm, 1)

            def first_table(*ns):
                for n in ns:
                    if n < FIRST_ACT:
                        if n >= RING:
                            pe.wait_ge(mt_ac, n - RING + 1)
                        mm(ps[:, 4 + n % RING, :], ident[:, 0:1].to_broadcast([P, P]), brow[:, 0:512], stop=False)
                        mm(ps[:, 4 + n % RING, :], hT[:, n * P:(n + 1) * P], w("L0_WmsgT", 0, 4),
                           start=False).then_inc(in_mm, 1)
                    elif n < FIRST_ACT + RING:
                        pe.wait_ge(mt_ac, n - RING + 1)
                        mm(ps[:, 4 + n % RING, :], hT[:, n * P:(n + 1) * P], w("L0_WmsgT", 0, 4)).then_inc(mt_mm, 1)
                    else:
                        table(0, n, hT, w("L0_WmsgT", 0, 4), 512)

            pe.wait_ge(s_dv, DV["w_th"])
            step("fd", mm(ps[:, 1, 0:TILES], ones[0:1, :], rec[0:1, 0:TILES, F_DST]))
            first_table(0)
            pe.wait_ge(s_dv, DV["w_cnt"])
            step("off", T.transpose(ps[0:1, 2, 0:P], small[:, 0:1], ident))
            first_table(1, 2)
            pe.wait_ge(s_dv, DV["w_bx"])
            step("base", mm(ps[:, 1, 0:SLOTS], ones[0:1, :], basef[0:1, :]))
            first_table(*range(3, WIN))
            pe.wait_ge(s_dv, DV["i_dl"])
            for q in range(WAVES // 4):
                if q >= 4:
                    pe.wait_ge(s_ac, AC[f"recT{q - 4}"])
                for j in range(4):
                    g = 4 * q + j
                    ins = T.transpose(ps[:, q % 4, j * P:(j + 1) * P],
                                      rec[:, g * WV:(g + 1) * WV, :].rearrange("p s f -> p (s f)"), ident)
                step(f"recT{q}", ins)
            pe.wait_ge(mt_ev, WIN - FIRST_ACT)
            blocks = [(b * P, min(P, TILES - b * P)) for b in range(4)]
            for b, (t0, tn) in enumerate(blocks):
                ins = T.transpose(ps[0:tn, 4, b * P:(b + 1) * P], rec[:, t0:t0 + tn, F_DST], ident)
            step("dT", ins)

            def sums(k, counting=False):
                with pe.Fori(0, TURNS) as i:
                    for u in range(RING):
                        cs = load_cols(pe, cols, i, u)
                        c16 = load_cols(pe, cols16, i, u, (WIN - 1) * NT) if counting else None
                        pe.wait_ge(gat[u], (k * TURNS + i + 1) * (16 * WV))
                        pe.wait_ge(oh_ready, oh_no(k, i, u))
                        for j in range(WV):
                            ins = mm(psf[:, ds(cs[j], P)], ring[:, u, j, 0:D], oh[:, u % 2, j, :], start=False,
                                     stop=False)
                            if counting:
                                ins = mm(ps[:, 7, ds(c16[j], NT)], ohb[:, u % 2, j, :], t9oh[:, u % 2, j, :],
                                         start=False, stop=False)
                        ins.then_inc(credit, 1)

            def hidden(r, L, h):
                wh = w(L + "_whhT", 0, 3)
                for n in range(2 * NCH):
                    (c0, cw), j = CH[n // 2], n % 2
                    if n >= 8:
                        pe.wait_ge(hid_ac, r * (2 * NCH) + (n - 7))
                    mm(ps[:, n % 8, 0:cw], wh[:, j * P:(j + 1) * P], h[:, c0:c0 + cw]).then_inc(hid_mm, 1)
                pe.wait_ge(hid_ac, r * (2 * NCH) + 2 * NCH)

            def gru(r, L, c, gin, hin):
                if c >= NCH:
                    return
                wi, wh = w(L + "_wihT", 0, 3), w(L + "_whhT", 0, 3)
                (c0, cw), t = CH[c], r * NCH + c
                gin(c)
                g, h = rT[:, c0:c0 + cw], hin[:, c0:c0 + cw]
                for j, s_ in enumerate((gru_ar, gru_az)):
                    if c >= 1:
                        pe.wait_ge(s_, t)
                    mm(ps[:, j, 0:cw], wi[:, j * P:(j + 1) * P], g).then_inc(gru_mm, 1)
                if c >= 1:
                    pe.wait_ge(gru_p, t)
                mm(ps[:, 2, 0:cw], wi[:, 2 * P:3 * P], g)
                mm(ps[:, 3, 0:cw], wh[:, 2 * P:3 * P], h).then_inc(gru_mm, 1)

            def norm(ln, c, banks_free=None):
                n0, far = NCH * ln, deep(ln)
                if 2 <= c <= NCH + 1:
                    w0, nw = CH[c - 2][0] // P, CH[c - 2][1] // P
                    pe.wait_ge(ln_r, n0 + c - 1)
                    if c - 2 >= far:
                        pe.wait_ge(ln_x, n0 + c - 1 - far)
                    for j in range(nw):
                        ins = T.transpose(ps[:, bank(ln, SPREAD, c), j * P:(j + 1) * P],
                                          rs[:, w0 + j:w0 + j + 1].to_broadcast([P, P]), ident)
                    ins.then_inc(ln_b, 1)
                if 0 <= c < NCH:
                    c0, cw = CH[c]
                    if c == 0 and banks_free:
                        banks_free()
                    pe.wait_ge(ln_y, n0 + c + 1)
                    if c >= far:
                        pe.wait_ge(ln_c, n0 + c + 1 - far)
                    mm(ps[:, bank(ln, MEAN, c), 0:cw], onesD, yT[:, c0:c0 + cw]).then_inc(ln_m, 1)
                if 1 <= c <= NCH:
                    cw, b = CH[c - 1][1], (c - 1) % 2
                    pe.wait_ge(ln_q, n0 + c)
                    if c - 1 >= far:
                        pe.wait_ge(ln_s, n0 + c - far)
                    for j in range(cw // P):
                        ins = mm(ps[:, bank(ln, VAR, c - 1), j:j + 1], wk[:, 5, b, j * P:(j + 1) * P], onesD[:, 0:1])
                    ins.then_inc(ln_v, 1)
                if c >= 3 and ln != 2:
                    c0, cw = CH[c - 3]
                    pe.wait_ge(ln_x, n0 + c - 2)
                    if c - 3 >= far:
                        pe.wait_ge(ln_o, NCH * OUTS[ln] + c - 2 - far)
                    for j in range(cw // P):
                        ins = T.transpose(ps[:, bank(ln, TURN, c - 3), j * P:(j + 1) * P],
                                          xT[:, c0 + j * P:c0 + (j + 1) * P], ident)
                    ins.then_inc(ln_t, 1)

            def after_recT():
                pe.wait_ge(s_ac, AC[f"recT{WAVES // 4 - 1}"])
                pe.wait_ge(s_dv, DV["t_d1"])

            after_recT()
            pe.wait_ge(s_w, NLOADS)
            rT = gT

            def evacuated(k):
                def f(c=0):
                    if c == 0:
                        pe.wait_ge(ev_d, (k + 1) * EV_D)
                        pe.wait_ge(ev_a, (k + 1) * EV_A)
                return f

            with pe.Fori(0, STEPS - 1) as s:
                hidden(s, "L0", hT)
                zero(range(NCH))
                sums(s)
                for c in range(NCH + 2):
                    gru(s, "L0", c, evacuated(s), hT)
                    if c >= 2:
                        pe.wait_ge(gru_h, s * NCH + (c - 1))
                        for n in range(CH[c - 2][0] // P, (CH[c - 2][0] + CH[c - 2][1]) // P):
                            table(s + 1, n, hT, w("L0_WmsgT", 0, 4), 512)
                pe.wait_ge(mt_ev, (s + 2) * WIN - FIRST_ACT)
            hidden(STEPS - 1, "L0", hT)
            zero(range(NCH + 1))
            sums(STEPS - 1, counting=True)
            pe.wait_ge(s_ac, AC["counts"])
            for c in range(NCH + 5):
                gru(STEPS - 1, "L0", c, evacuated(STEPS - 1), hT)
                norm(0, c - 2)

            pe.wait_ge(ln_o, NCH)
            zero(range(NCH))
            with pe.Fori(0, TURNS) as i:
                for u in range(RING):
                    last, cs = (cs if u else None), load_cols(pe, cols, i, u)
                    for hf in range(2):
                        q = (i * RING + u) * 2 + hf
                        if hf == 0:
                            pe.wait_ge(oh_ready, oh_no(PASS_L1, i, u))
                        pe.wait_ge(l1_msg, q + 1)
                        for j in range(4):
                            ins = mm(ps[:, 7, j * P:(j + 1) * P], wpad[:, 0, 4 * hf + j, :], rts[:, u % 2, :])
                        ins.then_inc(l1_hid, 1)
                        if u or hf:
                            u0, h0, c0 = (u, 0, cs) if hf else (u - 1, 1, last)
                            for j in range(4):
                                ins = mm(psf[:, ds(c0[4 * h0 + j], P)], ring[:, u0, 4 * h0 + j, 0:D],
                                         oh[:, u0 % 2, 4 * h0 + j, :], start=False, stop=False)
                            if not hf:
                                ins.then_inc(credit, 1)
                        pe.wait_ge(l1_relu, q + 1)
                        for j in range(4):
                            ins = mm(ps[:, 7, j * P:(j + 1) * P], pw[:, hf, j * P:(j + 1) * P], w("L1_pos_w2"))
                        ins.then_inc(l1_pe, 1)
                pe.wait_ge(l1_msg, (i + 1) * (2 * RING) + 1)
                for j in range(4):
                    ins = mm(psf[:, ds(cs[4 + j], P)], ring[:, RING - 1, 4 + j, 0:D],
                             oh[:, (RING - 1) % 2, 4 + j, :], start=False, stop=False)
                ins.then_inc(credit, 1)
            evacuated(PASS_L1)()
            for c, (c0, cw) in enumerate(CH):
                if c == 0:
                    pe.wait_ge(s_dv, DV["n_inv"])
                if c >= 2:
                    pe.wait_ge(s_dv, DV[f"ag{c - 2}"])
                for j in range(cw // P):
                    wd = c0 // P + j
                    ins = T.transpose(ps[:, c % 2, j * P:(j + 1) * P], inv[:, wd:wd + 1].to_broadcast([P, P]), ident)
                step(f"cnt{c}", ins)
            for c, (c0, cw) in enumerate(CH):
                pe.wait_ge(s_dv, DV[f"ag{c}"])
                if c >= 2:
                    pe.wait_ge(s_ac, AC[f"sage{c - 2}"])
                mm(ps[:, 4 + c % 2, 0:cw], w("L1_sage", 0), xT[:, c0:c0 + cw], stop=False)
                step(f"sage{c}", mm(ps[:, 4 + c % 2, 0:cw], w("L1_sage", 1), gT[:, c0:c0 + cw], start=False))
            for c in range(NCH + 3):
                norm(1, c, lambda: pe.wait_ge(s_ac, AC[f"sage{NCH - 1}"]))

            pe.wait_ge(ln_o, 2 * NCH)
            for c, (c0, cw) in enumerate(CH):
                if c >= 1:
                    pe.wait_ge(s_ac, AC[f"c9_{c - 1}"])
                for j in range(cw // P):
                    ins = T.transpose(ps[0:NT, 7, j * P:(j + 1) * P], counts[:, c0 // P + j, :], ident)
                step(f"c9_{c}", ins)
            pe.wait_ge(s_ac, AC[f"c9_{NCH - 1}"])
            hidden(STEPS, "L2", xT)
            zero(range(NCH))
            sums(PASS_L2)
            evacuated(PASS_L2)()
            NT9 = 9

            def message(c):
                c0, cw = CH[c]
                if c >= 1:
                    pe.wait_ge(s_ac, AC[f"msg{c - 1}"])
                o = ps[:, 4 + TURN, 0:cw]
                mm(o, w("L2_WmsgT"), gT[:, c0:c0 + cw], stop=False)
                step(f"msg{c}", mm(o, w("L2_emb", rows=NT9), C9[0:NT9, c0:c0 + cw], start=False))

            pe.wait_ge(s_dv, DV["emb"])
            message(0)
            for c in range(NCH + 4):
                if c + 1 < NCH:
                    message(c + 1)
                gru(STEPS, "L2", c, lambda c: pe.wait_ge(s_ac, AC[f"msg{c}"]), xT)
                norm(2, c - 2)

            def after_l2():
                pe.wait_ge(ln_x, 3 * NCH)
                pe.wait_ge(ln_s, 3 * NCH)
            after_l2()
            for n in range(WIN):
                table(STEPS, n, xT, w("L3_qkv", 0, 3), 3 * D)
            pe.wait_ge(mt_ev, (STEPS + 1) * WIN - FIRST_ACT)
            q_rows = hT
            with pe.Fori(0, TURNS) as i:
                for u in range(RING):
                    g2 = (i * RING + u) * 2
                    cs = load_cols(pe, cols, i, u)
                    pe.wait_ge(oh_ready, oh_no(PASS_L3, i, u))
                    for hf in range(2):
                        for j in range(4):
                            ins = T.transpose(ps[:, 4 + hf, j * P:(j + 1) * P], oh[:, u % 2, 4 * hf + j, :], ident)
                        ins.then_inc(a_tp, 1)
                    pe.wait_ge(a_v, g2 + 1)
                    for hf in range(2):
                        for j in range(4):
                            ins = mm(ps[:, hf, j * P:(j + 1) * P], rts[:, u % 2, :], wpad[:, 1, 4 * hf + j, :])
                        ins.then_inc(a_e, 1)
                    pe.wait_ge(a_prod, g2 + 1)
                    for hf in range(2):
                        pe.wait_ge(a_oht, g2 + (hf + 1))
                        for j in range(4):
                            ins = mm(ps[:, 2 + hf, j * P:(j + 1) * P],
                                     oht[:, u % 2, (4 * hf + j) * P:(4 * hf + j + 1) * P],
                                     q_rows[:, ds(cs[4 * hf + j], P)])
                        ins.then_inc(a_q, 1)
            pe.wait_ge(a_out, EXTRA + 1)
            for h in range(HEADS):
                for b, (t0, tn) in enumerate(blocks):
                    ins = T.transpose(ps[0:tn, h, b * P:(b + 1) * P], alE[:, t0:t0 + tn, h], ident)
                step(f"alT{h}", ins)
            pe.wait_ge(s_dv, DV["t_h1"])
            for j in range(4):
                src = small[:, 384 + 32 * j:384 + 32 * j + 32].rearrange("p (b h) -> p b h", b=4)
                for b in range(4):
                    ins = T.transpose(ps[0:HEADS, 1 + j, b * P:(b + 1) * P], src[:, b, :], ident)
            step("line", ins)
            pe.wait_ge(s_dv, DV["c_9"])
            for j in range(2):
                for b in range(4):
                    o = (j * 4 + b) * HEADS
                    ins = T.transpose(ps[:, 5, o:o + HEADS],
                                      (cf, cb)[j][:, b * P:(b + 1) * P],
                                      ident[0:HEADS, 0:HEADS])
            step("carry", ins)
            alT = ring_flat[:, 0:4096].rearrange("p (h b e) -> p h b e", h=HEADS, b=4)
            for h in range(HEADS):
                pe.wait_ge(s_ac, AC[f"exp{h}"])
                for b, (t0, tn) in enumerate(blocks):
                    ins = T.transpose(ps[:, h, t0:t0 + tn], alT[0:tn, h, b, :], ident[0:tn, 0:tn])
                step(f"exE{h}", ins)
            pe.wait_ge(s_dv, DV["ex_done"])
            zero(range(8))
            with pe.Fori(0, TURNS) as i:
                for u in range(RING):
                    cs = load_cols(pe, cols, i, u)
                    c24 = load_cols(pe, cols24, i, u, NP + (WIN - 1) * 24)
                    pe.wait_ge(b_ohb, i * RING + (u + 1))
                    for j in range(WV):
                        mm(psf[:, ds(c24[j], 24)], ohb[:, u % 2, j, :], ex3w[:, u % 2, j, :], start=False, stop=False)
                    pe.wait_ge(b_ready, i * RING + (u + 1))
                    for j in range(WV):
                        ins = mm(psf[:, ds(cs[j], P)], ring[:, u, j // 2, (j % 2) * D:(j % 2 + 1) * D],
                                 oh[:, u % 2, j, :], start=False, stop=False)
                    ins.then_inc(b_used, 1)
            for c, (c0, cw) in enumerate(CH):
                pe.wait_ge(s_dv, DV[f"rx{c}"])
                if c == 1:
                    pe.wait_ge(s_ac, AC[f"o{NCH - 1}"])
                if c >= 3:
                    pe.wait_ge(s_dv, DV[f"n{c - 3}"])
                for j in range(cw // P):
                    ins = T.transpose(ps[:, SPREADS[c % 3], j * P:(j + 1) * P],
                                      rdenx[:, c0 + j * P:c0 + (j + 1) * P], ident)
                step(f"sp{c}", ins)
            pe.wait_ge(s_dv, DV[f"n{NCH - 1}"])

            def skip(c):
                c0, cw = CH[c]
                if c >= 2:
                    pe.wait_ge(f_xs, c - 1)
                mm(ps[:, c % 2, 0:cw], w("L3_Wskip"), xT[:, c0:c0 + cw]).then_inc(f_x, 1)

            skip(0)
            for c, (c0, cw) in enumerate(CH):
                if c + 1 < NCH:
                    skip(c + 1)
                b = c % 2
                pe.wait_ge(f_xs, c + 1)
                if c >= 2:
                    pe.wait_ge(f_sg, c - 1)
                mm(ps[:, 2 + b, 0:cw], wbeta[:, 0, :], gT[:, c0:c0 + cw], stop=False)
                mm(ps[:, 2 + b, 0:cw], wbeta[:, 1, :], wk[:, 0, b, 0:cw], start=False).then_inc(f_b, 1)
            for k in range(4 * NCH + 2):
                if k < 4 * NCH:
                    c, j = divmod(k, 4)
                    c0, cw = CH[c]
                    if j == 0:
                        pe.wait_ge(s_ac, AC[f"gn{c}"])
                    if k >= 3:
                        pe.wait_ge(s_ac, AC["gelu%d_%d" % divmod(k - 3, 4)])
                    step(f"ff{c}_{j}", mm(ps[:, k % 3, 0:cw], w("L3_W1", j), hT[:, c0:c0 + cw]))
                if k >= 2:
                    c, j = divmod(k - 2, 4)
                    cw = CH[c][1]
                    if c >= 1 and j == 0:
                        pe.wait_ge(s_dv, DV[f"y{c - 1}"])
                    pe.wait_ge(s_ac, AC[f"gelu{c}_{j}"])
                    step(f"ffo{c}_{j}", mm(ps[:, 3, 0:cw], w("L3_W2", j), wk[:, j // 2, j % 2, 0:cw], start=(j == 0),
                                           stop=(j == 3)))
                    if j == 1:
                        norm(3, c - 1)
            for c in range(NCH - 1, NCH + 3):
                norm(3, c)


GRU_COLS = [f"{L}_{n}" for L in ("L0", "L2") for n in ("bih_r", "bih_z", "bin", "bhh_r", "bhh_z", "bhn")]
HOST_COLS = GRU_COLS + ["L1_sage_b", "L1_gamma", "L1_beta", "L3_bskip", "L3_gn_w", "L3_gn_b", "L3_gn_ms", "L3_b2",
                        "L3_b1_0", "L3_b1_1", "L3_b1_2", "L3_b1_3", "L3_wbeta0", "L3_wbeta1", "L3_wbeta2", "eps",
                        "minus_half", "window_end"]
BCOLS = HOST_COLS + ["L0_br", "L0_bz", "L2_br", "L2_bz"]


def kernel(**inputs):
    import numpy as np
    import concourse.bacc as bacc
    from concourse import mybir as _mybir
    from concourse.bass_utils import run_bass_kernel_spmd

    v = {k: np.asarray(x) for k, x in inputs.items()}
    f32 = np.float32
    EP = TILES * P

    def pad(x, fill=0):
        out = np.full((EP,) + x.shape[1:], fill, x.dtype)
        out[:E] = x
        return out

    def tiles(x):
        x = x.reshape((TILES, P) + x.shape[1:])
        return np.ascontiguousarray(np.swapaxes(x, 0, 1)).reshape(P, -1)

    a = {}
    xT = np.zeros((P, NP), v["x"].dtype)
    xT[:, :N] = v["x"].T
    a["xT"] = xT
    a["dst_t"] = tiles(pad(v["dst"], NP - 1))
    a["dstn_t"] = tiles(np.append(pad(v["dst"], NP - 1)[1:], v["dst"].dtype.type(NP - 1)))
    for n, k in (("src_t", "src"), ("t4_t", "edge_type_4"), ("t9_t", "edge_type_9"), ("attr10_t", "edge_attr_10"),
                 ("attr2_t", "edge_attr_2")):
        a[n] = tiles(pad(v[k]))
    a["L0_WmsgT"] = v["L0_gnn_W_msg"].T
    a["L0_wihT"], a["L0_whhT"] = v["L0_gnn_w_ih"].T, v["L0_gnn_w_hh"].T
    a["L1_pos_w2"] = v["L1_gnn_pos_w2"]
    a["L1_sage"] = np.concatenate([v["L1_gnn_sage_w"][:D], v["L1_gnn_sage_w"][D:]], 1)
    a["L2_WmsgT"] = v["L2_gnn_W_msg"].T
    a["L2_wihT"], a["L2_whhT"] = v["L2_gnn_W_ih"].T, v["L2_gnn_W_hh"].T
    a["L2_emb"] = v["L2_gnn_edge_embed"]
    a["L2_bmsg9"] = np.broadcast_to(v["L2_gnn_b_msg"], (9, D))
    a["L3_qkv"] = np.concatenate([v["L3_gnn_Wq"], v["L3_gnn_Wk"], v["L3_gnn_Wv"]], 1)
    a["L3_Wskip"] = v["L3_gnn_Wskip"]
    a["L3_W1"] = v["L3_gnn_W1"]
    a["L3_W2"] = np.concatenate([v["L3_gnn_W2"][j * D:(j + 1) * D] for j in range(4)], 1)
    a["brows"] = np.concatenate([v["L0_gnn_b_msg"], v["L3_gnn_bq"], v["L3_gnn_bk"], v["L3_gnn_bv"]])
    col = {}
    for L, bi, bh in (("L0", v["L0_gnn_b_ih"], v["L0_gnn_b_hh"]), ("L2", v["L2_gnn_b_ih"], v["L2_gnn_b_hh"])):
        for j, (n, m) in enumerate((("bih_r", "bhh_r"), ("bih_z", "bhh_z"), ("bin", "bhn"))):
            col[f"{L}_{n}"], col[f"{L}_{m}"] = bi[j * D:(j + 1) * D], bh[j * D:(j + 1) * D]
    for n, k in (("L1_sage_b", "L1_gnn_sage_b"), ("L1_gamma", "L1_gnn_bn_gamma"), ("L1_beta", "L1_gnn_bn_beta"),
                 ("L3_bskip", "L3_gnn_bskip"), ("L3_gn_w", "L3_gnn_gn_w"), ("L3_gn_b", "L3_gnn_gn_b"),
                 ("L3_gn_ms", "L3_gnn_gn_ms"), ("L3_b2", "L3_gnn_b2")):
        col[n] = v[k]
    for j in range(4):
        col[f"L3_b1_{j}"] = v["L3_gnn_b1"][j * D:(j + 1) * D]
    for j in range(3):
        col[f"L3_wbeta{j}"] = v["L3_gnn_Wbeta"][j * D:(j + 1) * D, 0]
    col["eps"] = np.full(D, EPS, f32)
    col["minus_half"] = np.full(D, -0.5, f32)
    col["window_end"] = np.arange(1, P + 1).astype(f32) * P
    a["bcols"] = np.stack([col[n] for n in HOST_COLS], 1)
    a["consts"] = np.concatenate([np.eye(P), np.tile(np.arange(P), (P, 1)), np.ones((P, P)),
                                  np.full((P, P), 1.0 / D)], 1).astype(f32)
    wpad = np.zeros((P, 2, WV, P), f32)
    for s in range(WV):
        wpad[s * FIELDS + F_ATTR2:s * FIELDS + F_ATTR2 + 2, 0, s] = v["L1_gnn_pos_w1"]
        wpad[s * FIELDS:s * FIELDS + 10, 1, s] = v["L3_gnn_We"]
    a["wpad"] = wpad.reshape(P, -1)

    def program(seen, known):
        nc = bacc.Bacc("TRN2", target_bir_lowering=False, num_devices=1)
        arrays, args = {}, {}
        for n, x in a.items():
            arrays["in_" + n] = np.ascontiguousarray(x)
            args[n] = nc.dram_tensor("in_" + n, x.shape, _mybir.dt.from_np(x.dtype), kind="ExternalInput").ap()
        out = nc.dram_tensor("out_x", (N, D), _mybir.dt.float32, kind="ExternalOutput").ap()
        build(nc, args, out, seen, known)
        return nc, arrays
    seen = {"DV": [], "PE": [], "AC": []}
    program(seen, None)
    nc, arrays = program({"DV": [], "PE": [], "AC": []}, seen)
    r = run_bass_kernel_spmd(nc, [arrays], core_ids=[0])
    return r.results[0]["out_x"]
```
